# Optimizing a Trainium2 kernel written in Bass

```python
import numpy as np
import jax
import jax.numpy as jnp

def _softmax(x, axis=-1):
    return jax.nn.softmax(x, axis=axis)

def _gelu(x):
    return jax.nn.gelu(x, approximate=True)

def _silu(x):
    return jax.nn.silu(x)

def _sigmoid(x):
    return jax.nn.sigmoid(x)

def _layernorm(x, axis=-1, eps=1e-05):
    m = jnp.mean(x, axis=axis, keepdims=True)
    v = jnp.var(x, axis=axis, keepdims=True)
    return (x - m) / jnp.sqrt(v + eps)

def _scatter_add(tgt, idx, src, axis=0):
    return tgt.at[idx].add(src)

def _segment_sum(src, seg, n):
    return jax.ops.segment_sum(src, seg, n)
kernel_name = 'mk_macaron_d2_jaxref_r8_7617b0'

def setup_inputs(seed: int=0):
    np.random.seed(seed)
    _w = jnp.asarray

    def _L0_attn_setup():
        import jax, jax.numpy as jnp
        import numpy as np
        import math
        B, T, DIM, NH = (2, 256, 256, 16)
        HD = DIM // NH

        def rotate_half(x):
            h = x.shape[-1] // 2
            return jnp.concatenate([-x[..., h:], x[..., :h]], axis=-1)

        def rope_tables(t_len, rot_dim, base=10000.0, dtype=jnp.float32):
            inv_freq = 1.0 / base ** (jnp.arange(0, rot_dim, 2, dtype=dtype) / rot_dim)
            t = jnp.arange(t_len, dtype=dtype)
            ang = jnp.einsum('i,j->ij', t, inv_freq)
            return (jnp.sin(ang), jnp.cos(ang))

        def apply_rope(q, k, sin, cos):
            h = q.shape[-1] // 2
            q1, q2 = (q[..., :h], q[..., h:])
            k1, k2 = (k[..., :h], k[..., h:])
            sin = sin[None, None]
            cos = cos[None, None]
            q1r = q1 * cos + rotate_half(q1) * sin
            k1r = k1 * cos + rotate_half(k1) * sin
            return (jnp.concatenate([q1r, q2], axis=-1), jnp.concatenate([k1r, k2], axis=-1))
        key = jax.random.key(seed)
        ks = jax.random.split(key, 5)
        s = 1.0 / math.sqrt(DIM)
        return {'x': jax.random.normal(ks[0], (B, T, DIM), jnp.float32), 'wq': jax.random.normal(ks[1], (DIM, DIM), jnp.float32) * s, 'wk': jax.random.normal(ks[2], (DIM, DIM), jnp.float32) * s, 'wv': jax.random.normal(ks[3], (DIM, DIM), jnp.float32) * s, 'wo': jax.random.normal(ks[4], (DIM, DIM), jnp.float32) * s}
    _L0_attn_in = _L0_attn_setup()

    def _L0_ffn_setup():
        import jax, jax.numpy as jnp
        import numpy as np
        DIM = 256
        HID = 704
        ZERO_POINT = 128.0

        def _qlinear(x, wq, scale):
            W = (wq.astype(jnp.float32) - ZERO_POINT) * scale[:, None]
            return jnp.einsum('bsd,hd->bsh', x, W)
        key = jax.random.key(seed)
        ks = jax.random.split(key, 7)
        B, S = (4, 256)
        sg = jax.random.uniform(ks[1], (HID,)) * (0.02 / np.sqrt(DIM)) + 0.0001
        su = jax.random.uniform(ks[3], (HID,)) * (0.02 / np.sqrt(DIM)) + 0.0001
        sd = jax.random.uniform(ks[5], (DIM,)) * (0.02 / np.sqrt(HID)) + 0.0001
        return {'x': jax.random.normal(ks[0], (B, S, DIM), dtype=jnp.float32), 'wq_gate': jax.random.randint(ks[2], (HID, DIM), 0, 32, dtype=jnp.int32), 's_gate': sg, 'wq_up': jax.random.randint(ks[4], (HID, DIM), 0, 32, dtype=jnp.int32), 's_up': su, 'wq_down': jax.random.randint(ks[6], (DIM, HID), 0, 32, dtype=jnp.int32), 's_down': sd}
    _L0_ffn_in = _L0_ffn_setup()

    def _L1_attn_setup():
        import jax, jax.numpy as jnp
        import numpy as np
        import math
        N_EMBD = 256
        N_HEADS = 16
        HEAD_DIM = N_EMBD // N_HEADS
        CTX = 256

        def alibi_bias(seq_len: int, n_heads: int) -> jnp.ndarray:
            i = jnp.arange(seq_len)[:, None]
            j = jnp.arange(seq_len)[None, :]
            pos = jnp.where(j <= i, (j - i).astype(jnp.float32), 0.0)
            slopes = 2.0 ** (-8.0 / jnp.arange(1, n_heads + 1, dtype=jnp.float32))
            return slopes[:, None, None] * pos[None, :, :]

        def causal_mask(seq_len: int) -> jnp.ndarray:
            i = jnp.arange(seq_len)[:, None]
            j = jnp.arange(seq_len)[None, :]
            return jnp.where(j > i, -jnp.inf, 0.0).astype(jnp.float32)
        key = jax.random.key(seed)
        k_x, k_qkv, k_o = jax.random.split(key, 3)
        scale = 1.0 / math.sqrt(N_EMBD)
        x = jax.random.normal(k_x, (2, CTX, N_EMBD), dtype=jnp.float32)
        W_qkv = jax.random.normal(k_qkv, (N_EMBD, 3 * N_EMBD), dtype=jnp.float32) * scale
        W_o = jax.random.normal(k_o, (N_EMBD, N_EMBD), dtype=jnp.float32) * scale
        return {'x': x, 'W_qkv': W_qkv, 'W_o': W_o}
    _L1_attn_in = _L1_attn_setup()

    def _L1_ffn_setup():
        import jax, jax.numpy as jnp
        import numpy as np
        B, S, H = (2, 256, 256)
        E, K, F = (32, 4, 176)
        FS = 704
        EPS = 1e-06
        CAP = 128
        key = jax.random.key(seed)
        ks = jax.random.split(key, 10)
        s = 0.02
        return {'hidden_states': jax.random.normal(ks[0], (B, S, H), jnp.float32), 'w_norm': 1.0 + 0.02 * jax.random.normal(ks[1], (H,), jnp.float32), 'w_router': s * jax.random.normal(ks[2], (H, E), jnp.float32), 'w_gate': s * jax.random.normal(ks[3], (E, H, F), jnp.float32), 'w_up': s * jax.random.normal(ks[4], (E, H, F), jnp.float32), 'w_down': s * jax.random.normal(ks[5], (E, F, H), jnp.float32), 'sw_gate': s * jax.random.normal(ks[6], (H, FS), jnp.float32), 'sw_up': s * jax.random.normal(ks[7], (H, FS), jnp.float32), 'sw_down': s * jax.random.normal(ks[8], (FS, H), jnp.float32), 'w_shared_gate': s * jax.random.normal(ks[9], (H, 1), jnp.float32)}
    _L1_ffn_in = _L1_ffn_setup()
    _d = {'L0_attn_x': _L0_attn_in['x'], 'L0_attn_wq': _L0_attn_in['wq'], 'L0_attn_wk': _L0_attn_in['wk'], 'L0_attn_wv': _L0_attn_in['wv'], 'L0_attn_wo': _L0_attn_in['wo'], 'L0_ffn_wq_gate': _L0_ffn_in['wq_gate'], 'L0_ffn_s_gate': _L0_ffn_in['s_gate'], 'L0_ffn_wq_up': _L0_ffn_in['wq_up'], 'L0_ffn_s_up': _L0_ffn_in['s_up'], 'L0_ffn_wq_down': _L0_ffn_in['wq_down'], 'L0_ffn_s_down': _L0_ffn_in['s_down'], 'L1_attn_W_qkv': _L1_attn_in['W_qkv'], 'L1_attn_W_o': _L1_attn_in['W_o'], 'L1_ffn_w_norm': _L1_ffn_in['w_norm'], 'L1_ffn_w_router': _L1_ffn_in['w_router'], 'L1_ffn_w_gate': _L1_ffn_in['w_gate'], 'L1_ffn_w_up': _L1_ffn_in['w_up'], 'L1_ffn_w_down': _L1_ffn_in['w_down'], 'L1_ffn_sw_gate': _L1_ffn_in['sw_gate'], 'L1_ffn_sw_up': _L1_ffn_in['sw_up'], 'L1_ffn_sw_down': _L1_ffn_in['sw_down'], 'L1_ffn_w_shared_gate': _L1_ffn_in['w_shared_gate']}
    _x0 = _d['L0_attn_x']
    _d['L0_attn_x'] = jax.random.normal(jax.random.fold_in(jax.random.key(seed), 1), (4, 1024, 256), dtype=_x0.dtype)
    del _x0
    return _d

def reference(L0_attn_x, L0_attn_wq, L0_attn_wk, L0_attn_wv, L0_attn_wo, L0_ffn_wq_gate, L0_ffn_s_gate, L0_ffn_wq_up, L0_ffn_s_up, L0_ffn_wq_down, L0_ffn_s_down, L1_attn_W_qkv, L1_attn_W_o, L1_ffn_w_norm, L1_ffn_w_router, L1_ffn_w_gate, L1_ffn_w_up, L1_ffn_w_down, L1_ffn_sw_gate, L1_ffn_sw_up, L1_ffn_sw_down, L1_ffn_w_shared_gate):

    def _L0_attn_ref(x, wq, wk, wv, wo):
        import jax, jax.numpy as jnp
        import numpy as np
        import math
        B, T, DIM, NH = (2, 256, 256, 16)
        HD = DIM // NH

        def rotate_half(x):
            h = x.shape[-1] // 2
            return jnp.concatenate([-x[..., h:], x[..., :h]], axis=-1)

        def rope_tables(t_len, rot_dim, base=10000.0, dtype=jnp.float32):
            inv_freq = 1.0 / base ** (jnp.arange(0, rot_dim, 2, dtype=dtype) / rot_dim)
            t = jnp.arange(t_len, dtype=dtype)
            ang = jnp.einsum('i,j->ij', t, inv_freq)
            return (jnp.sin(ang), jnp.cos(ang))

        def apply_rope(q, k, sin, cos):
            h = q.shape[-1] // 2
            q1, q2 = (q[..., :h], q[..., h:])
            k1, k2 = (k[..., :h], k[..., h:])
            sin = sin[None, None]
            cos = cos[None, None]
            q1r = q1 * cos + rotate_half(q1) * sin
            k1r = k1 * cos + rotate_half(k1) * sin
            return (jnp.concatenate([q1r, q2], axis=-1), jnp.concatenate([k1r, k2], axis=-1))
        b, t, c = x.shape

        def proj(w):
            return (x @ w.T).reshape(b, t, NH, HD).transpose(0, 2, 1, 3)
        q, k, v = (proj(wq), proj(wk), proj(wv))
        sin, cos = rope_tables(t, HD, dtype=x.dtype)
        q, k = apply_rope(q, k, sin, cos)
        att = jnp.einsum('bhqd,bhkd->bhqk', q, k) * (1.0 / math.sqrt(HD))
        att = jax.nn.softmax(att, axis=-1)
        y = jnp.einsum('bhqk,bhkd->bhqd', att, v)
        y = y.transpose(0, 2, 1, 3).reshape(b, t, c)
        return y @ wo.T

    def _L0_ffn_ref(x, wq_gate, s_gate, wq_up, s_up, wq_down, s_down):
        import jax, jax.numpy as jnp
        import numpy as np
        DIM = 256
        HID = 704
        ZERO_POINT = 128.0

        def _qlinear(x, wq, scale):
            W = (wq.astype(jnp.float32) - ZERO_POINT) * scale[:, None]
            return jnp.einsum('bsd,hd->bsh', x, W)
        gate = _qlinear(x, wq_gate, s_gate)
        gate = jax.nn.silu(gate)
        up = _qlinear(x, wq_up, s_up)
        return _qlinear(gate * up, wq_down, s_down)

    def _L1_attn_ref(x, W_qkv, W_o):
        import jax, jax.numpy as jnp
        import numpy as np
        import math
        N_EMBD = 256
        N_HEADS = 16
        HEAD_DIM = N_EMBD // N_HEADS
        CTX = 256

        def alibi_bias(seq_len: int, n_heads: int) -> jnp.ndarray:
            i = jnp.arange(seq_len)[:, None]
            j = jnp.arange(seq_len)[None, :]
            pos = jnp.where(j <= i, (j - i).astype(jnp.float32), 0.0)
            slopes = 2.0 ** (-8.0 / jnp.arange(1, n_heads + 1, dtype=jnp.float32))
            return slopes[:, None, None] * pos[None, :, :]

        def causal_mask(seq_len: int) -> jnp.ndarray:
            i = jnp.arange(seq_len)[:, None]
            j = jnp.arange(seq_len)[None, :]
            return jnp.where(j > i, -jnp.inf, 0.0).astype(jnp.float32)
        bsz, seq_len, n_embd = x.shape
        qkv = jnp.einsum('bsd,de->bse', x, W_qkv)
        q, k, v = jnp.split(qkv, 3, axis=-1)

        def to_heads(t):
            return t.reshape(bsz, seq_len, N_HEADS, HEAD_DIM).transpose(0, 2, 1, 3)
        q, k, v = (to_heads(q), to_heads(k), to_heads(v))
        attn = jnp.einsum('bhqd,bhkd->bhqk', q, k) / math.sqrt(HEAD_DIM)
        attn = attn + alibi_bias(seq_len, N_HEADS)[None] + causal_mask(seq_len)[None, None]
        attn = jax.nn.softmax(attn, axis=-1)
        y = jnp.einsum('bhqk,bhkd->bhqd', attn, v)
        y = y.transpose(0, 2, 1, 3).reshape(bsz, seq_len, n_embd)
        return jnp.einsum('bsd,de->bse', y, W_o)

    def _L1_ffn_ref(hidden_states, w_norm, w_router, w_gate, w_up, w_down, sw_gate, sw_up, sw_down, w_shared_gate):
        import jax, jax.numpy as jnp
        import numpy as np
        B, S, H = (2, 256, 256)
        E, K, F = (32, 4, 176)
        FS = 704
        EPS = 1e-06
        CAP = 128
        inp = hidden_states
        xf = inp.astype(jnp.float32)
        var = jnp.mean(xf * xf, axis=-1, keepdims=True)
        x = (w_norm * (xf * jax.lax.rsqrt(var + EPS))).astype(inp.dtype)
        Bq, Sq, Hq = x.shape
        x = x.reshape(-1, Hq)
        T = Bq * Sq
        logits = x @ w_router
        probs = jax.nn.softmax(logits.astype(jnp.float32), axis=-1)
        w_topk, sel = jax.lax.top_k(probs, K)
        w_topk = w_topk.astype(x.dtype)
        flat_e = sel.reshape(-1)
        order = jnp.argsort(flat_e)
        sorted_e = flat_e[order]
        counts = jnp.zeros((E,), jnp.int32).at[flat_e].add(1)
        starts = jnp.cumsum(counts) - counts
        pos = jnp.arange(T * K) - starts[sorted_e]
        tok = order // K
        valid = pos < CAP
        dest = jnp.where(valid, pos, CAP)
        buf = jnp.zeros((E, CAP + 1, Hq), x.dtype).at[sorted_e, dest].set(x[tok])
        buf = buf[:, :CAP]
        g = jnp.einsum('ech,ehf->ecf', buf, w_gate)
        u = jnp.einsum('ech,ehf->ecf', buf, w_up)
        y = jnp.einsum('ecf,efh->ech', jax.nn.silu(g) * u, w_down)
        wv = w_topk.reshape(-1)[order] * valid.astype(x.dtype)
        gath = y[sorted_e, jnp.minimum(pos, CAP - 1)]
        out = jnp.zeros((T, Hq), x.dtype).at[tok].add(gath * wv[:, None])
        sh = jax.nn.silu(x @ sw_gate) * (x @ sw_up) @ sw_down
        sh = jax.nn.sigmoid(x @ w_shared_gate) * sh
        out = out + sh
        return inp + out.reshape(Bq, Sq, Hq)
    x = L0_attn_x
    x = x + 0.5 * _L0_ffn_ref(_layernorm(x, axis=-1), L0_ffn_wq_gate, L0_ffn_s_gate, L0_ffn_wq_up, L0_ffn_s_up, L0_ffn_wq_down, L0_ffn_s_down)
    x = x + _L0_attn_ref(_layernorm(x, axis=-1), L0_attn_wq, L0_attn_wk, L0_attn_wv, L0_attn_wo)
    x = x + 0.5 * _L0_ffn_ref(_layernorm(x, axis=-1), L0_ffn_wq_gate, L0_ffn_s_gate, L0_ffn_wq_up, L0_ffn_s_up, L0_ffn_wq_down, L0_ffn_s_down)
    x = x + 0.5 * _L1_ffn_ref(_layernorm(x, axis=-1), L1_ffn_w_norm, L1_ffn_w_router, L1_ffn_w_gate, L1_ffn_w_up, L1_ffn_w_down, L1_ffn_sw_gate, L1_ffn_sw_up, L1_ffn_sw_down, L1_ffn_w_shared_gate)
    x = x + _L1_attn_ref(_layernorm(x, axis=-1), L1_attn_W_qkv, L1_attn_W_o)
    x = x + 0.5 * _L1_ffn_ref(_layernorm(x, axis=-1), L1_ffn_w_norm, L1_ffn_w_router, L1_ffn_w_gate, L1_ffn_w_up, L1_ffn_w_down, L1_ffn_sw_gate, L1_ffn_sw_up, L1_ffn_sw_down, L1_ffn_w_shared_gate)
    return x

_drawn_inputs = setup_inputs


def setup_inputs(seed=0):
    import zlib

    import numpy as np

    out = dict(_drawn_inputs(seed))
    spreads = {}
    factors = {'L0_ffn_s_gate': 8.0,
     'L0_ffn_s_up': 8.0,
     'L0_ffn_s_down': 8.0,
     'L1_ffn_w_norm': 8.0,
     'L1_ffn_w_router': 8.0,
     'L1_ffn_w_gate': 8.0,
     'L1_ffn_w_up': 8.0,
     'L1_ffn_w_down': 8.0,
     'L1_ffn_sw_gate': 7.286,
     'L1_ffn_sw_up': 7.197,
     'L1_ffn_sw_down': 7.182,
     'L1_ffn_w_shared_gate': 8.0}
    for name, (base, spread) in spreads.items():
        noise = np.random.default_rng([zlib.crc32(name.encode()), seed]).standard_normal(out[name].shape)
        drawn = base * np.exp(spread * noise) if base else spread * noise
        out[name] = jnp.asarray(drawn.astype(out[name].dtype))
    for name, factor in factors.items():
        out[name] = (out[name] * factor).astype(out[name].dtype)
    return out
```

```python
from contextlib import ExitStack

import concourse.bass as bass
from concourse import mybir
import numpy as np

F32 = mybir.dt.float32
BF16 = mybir.dt.bfloat16
I32 = mybir.dt.int32
U32 = mybir.dt.uint32
ALU = mybir.AluOpType
ACT = mybir.ActivationFunctionType
AX = mybir.AxisListType

P = 128
B, T, D = 4, 1024, 256
NTOK = B * T
NT = NTOK // P
TPB = T // P
KC = D // P
NH, HD = 16, 16
FF = 704
FB = -(-FF // P)
NE, TOPK, CAP, EF = 32, 4, 128, 176
EH = EF // 2
CT = 4
NCH = NT // CT
CW = CT * P
TRASH = P
ZERO_POINT = 128.0
LN_EPS, RMS_EPS = 1e-5, 1e-6
NEG = -1e30
VW = 32
ROPE = HD // 2

CONST = {}
_at = 0
for _name, _w in (("ident", P), ("tri", P), ("mask_qk", P), ("mask_kq", P), ("expert", NE), ("token", NT),
                  ("slopes", NH * 6), ("kbase", TPB * 3), ("kpos", 3), ("rope", TPB * 2 * ROPE), ("slot", NE)):
    CONST[_name] = (_at, _at + _w)
    _at += _w
NCONST = _at


def hid(j):
    return min(P, FF - j * P)


def constants():
    c = np.zeros((P, NCONST), np.float32)
    p = np.arange(P)

    def put(name, a):
        lo, hi = CONST[name]
        c[:, lo:hi] = a.reshape(P, hi - lo)

    put("ident", np.eye(P))
    put("tri", (p[:, None] < p[None, :]) * 1.0)
    put("mask_qk", np.where(p[None, :] > p[:, None], NEG, 0.0))
    put("mask_kq", np.where(p[:, None] > p[None, :], NEG, 0.0))
    put("expert", np.tile(np.arange(NE), (P, 1)))
    put("token", p[:, None] + P * np.arange(NT)[None, :])
    put("slot", NTOK + np.tile(p[:, None], (1, NE)))
    slopes = (2.0 ** (-8.0 / np.arange(1, NH + 1, dtype=np.float32))).astype(np.float32)
    parts, rest = [], slopes.copy()
    for _ in range(3):
        part = (rest.view(np.uint32) & np.uint32(0xFFFF0000)).view(np.float32)
        parts.append(part)
        rest = rest - part
    put("slopes", np.tile(np.stack(parts + parts, 1).reshape(-1), (P, 1)))
    put("kbase", np.tile(np.repeat(P * (np.arange(TPB) - TPB // 2), 3), (P, 1)))
    put("kpos", np.tile(p[:, None], (1, 3)))
    inv = (1.0 / 10000.0 ** (np.arange(0, HD, 2, dtype=np.float32) / np.float32(HD))).astype(np.float32)
    ang = (np.arange(T, dtype=np.float32)[:, None] * inv[None, :]).astype(np.float32)
    sin = np.sin(ang)
    sin[:, :ROPE // 2] *= -1
    tab = np.concatenate([np.cos(ang), sin], 1).astype(np.float32)
    put("rope", tab.reshape(TPB, P, 2 * ROPE).transpose(1, 0, 2))
    return c


class Core:

    def __init__(self, nc, ctx, dram):
        self.nc, self.dram, self.sems = nc, dram, []

        def sb(name, shape, dt=F32):
            return ctx.enter_context(nc.sbuf_tensor(name, shape, dt))

        self.x = sb("x", [P, NT, D])
        self.mv = sb("mv", [P, NT, 2])
        self.rstd = sb("rstd", [P, NT])
        self.consts = sb("consts", [P, NCONST])
        self.ident_b = sb("ident_b", [P, P], BF16)
        self.eps = sb("eps", [P, 2])
        self.wgT = sb("wgT", [P, KC, FF])
        self.wuT = sb("wuT", [P, KC, FF])
        self.wdT = sb("wdT", [P, FB, D])
        self.wqkvT = sb("wqkvT", [P, KC, 3 * D])
        self.woT = sb("woT", [P, KC, D])

    def clear_semaphores(self):
        self.nc.clear_and_free_semaphores(self.sems)
        self.nc.all_engine_barrier()
        self.sems = []

    def const(self, name):
        lo, hi = CONST[name]
        return self.consts[:, lo:hi]


def scope(core, ctx):
    nc = core.nc

    def sb(name, shape, dt=F32):
        return ctx.enter_context(nc.sbuf_tensor(name, shape, dt))

    def ps(name, shape, dt=F32):
        return ctx.enter_context(nc.psum_tensor(name, shape, dt))

    def sem(name):
        core.sems.append(nc.alloc_semaphore(name=name))
        return core.sems[-1]

    return sb, ps, sem


def prepare_phase(core):
    nc, dram = core.nc, core.dram
    with ExitStack() as ctx:
        sb, ps, sem = scope(core, ctx)
        qg = sb("p_qg", [P, FB, D], I32)
        qu = sb("p_qu", [P, FB, D], I32)
        qd = sb("p_qd", [P, KC, FF], I32)
        sg = sb("p_sg", [P, FB])
        su = sb("p_su", [P, FB])
        sd = sb("p_sd", [P, KC])
        wn = sb("p_wn", [P, 4, KC, D])
        fg = sb("p_fg", [P, FB, D])
        fu = sb("p_fu", [P, FB, D])
        fd = sb("p_fd", [P, KC, FF])
        bn = sb("p_bn", [P, NT, 6])
        tp = [ps(f"p_tp{i}", [P, 4, P]) for i in range(4)]
        c_in, q_in, s_in, w_in, x_in = sem("p_c_in"), sem("p_q_in"), sem("p_s_in"), sem("p_w_in"), sem("p_x_in")
        deq, turned, kept, stat = sem("p_deq"), sem("p_turned"), sem("p_kept"), sem("p_stat")

        jobs = []
        for q, (src, dst) in enumerate(((fg, core.wgT), (fu, core.wuT))):
            for kc in range(KC):
                for j in range(FB):
                    jobs.append((src[0:hid(j), j, kc * P:(kc + 1) * P], hid(j), P,
                                 dst[:, kc, j * P:j * P + hid(j)]))
        for j in range(FB):
            for kc in range(KC):
                jobs.append((fd[:, kc, j * P:j * P + hid(j)], P, hid(j), core.wdT[0:hid(j), j, kc * P:(kc + 1) * P]))
        nq = len(jobs)
        for w in range(4):
            dst = core.wqkvT if w < 3 else core.woT
            off = w * D if w < 3 else 0
            for kc in range(KC):
                for m in range(KC):
                    jobs.append((wn[:, w, m, kc * P:(kc + 1) * P], P, P,
                                 dst[:, kc, off + m * P:off + (m + 1) * P]))
        assert len(jobs) % 4 == 0

        with nc.Block() as block:
            @block.sync
            def _(sp):
                sp.dma_start(core.consts[:], dram["consts"]).then_inc(c_in, 16)
                for q, s, a, b in (("L0_ffn_wq_gate", "L0_ffn_s_gate", qg, sg), ("L0_ffn_wq_up", "L0_ffn_s_up", qu, su)):
                    full = (FB - 1) * P
                    sp.dma_start(a[:, 0:FB - 1, :], dram[q][0:full, :].rearrange("(j p) d -> p j d", p=P)).then_inc(q_in, 16)
                    sp.dma_start(a[0:hid(FB - 1), FB - 1, :], dram[q][full:FF, :]).then_inc(q_in, 16)
                sp.dma_start(qd[:], dram["L0_ffn_wq_down"].rearrange("(k p) f -> p k f", p=P)).then_inc(q_in, 16)
                for w, name in enumerate(("L0_attn_wq", "L0_attn_wk", "L0_attn_wv", "L0_attn_wo")):
                    sp.dma_start(wn[:, w], dram[name].rearrange("(m p) d -> p m d", p=P)).then_inc(w_in, 16)

            @block.gpsimd
            def _(pool):
                full = (FB - 1) * P
                for s, b in (("L0_ffn_s_gate", sg), ("L0_ffn_s_up", su)):
                    v = dram[s].rearrange("(f a) -> f a", a=1)
                    pool.dma_start(b[:, 0:FB - 1].rearrange("p (j a) -> p j a", a=1),
                                   v[0:full].rearrange("(j p) a -> p j a", p=P)).then_inc(s_in, 16)
                    pool.dma_start(b[0:hid(FB - 1), FB - 1:FB], v[full:FF]).then_inc(s_in, 16)
                pool.dma_start(sd[:].rearrange("p (k a) -> p k a", a=1),
                               dram["L0_ffn_s_down"].rearrange("(k p a) -> p k a", p=P, a=1)).then_inc(s_in, 16)

            @block.scalar
            def _(act):
                for b in range(B):
                    act.dma_start(core.x[:, b * TPB:(b + 1) * TPB, :],
                                  dram["L0_attn_x"][b].rearrange("(i p) d -> p i d", p=P)).then_inc(x_in, 16)
                for n in range(1, len(jobs) // 4, 2):
                    act.wait_ge(turned, n + 1)
                    for i in range(4):
                        _, rows, cols, dst = jobs[4 * n + i]
                        last = nc.scalar.activation(dst, tp[n % 4][0:cols, i, 0:rows], ACT.Copy)
                    last.then_inc(kept, 1)

            @block.vector
            def _(dve):
                nc.vector.memset(core.eps[:, 0:1], LN_EPS)
                nc.vector.memset(core.eps[:, 1:2], RMS_EPS)
                dve.wait_ge(c_in, 16)
                nc.vector.tensor_copy(core.ident_b[:], core.const("ident"))
                dve.wait_ge(q_in, 16 * 5)
                dve.wait_ge(s_in, 16 * 5)
                for q, s, f in ((qg, sg, fg), (qu, su, fu)):
                    for j in range(FB):
                        r = hid(j)
                        nc.vector.tensor_scalar(f[0:r, j, :], q[0:r, j, :], ZERO_POINT, s[0:r, j:j + 1],
                                                ALU.subtract, ALU.mult).then_inc(deq, 1)
                for k in range(KC):
                    nc.vector.tensor_scalar(fd[:, k, :], qd[:, k, :], ZERO_POINT, sd[:, k:k + 1],
                                            ALU.subtract, ALU.mult).then_inc(deq, 1)
                for n in range(0, len(jobs) // 4, 2):
                    dve.wait_ge(turned, n + 1)
                    for i in range(4):
                        _, rows, cols, dst = jobs[4 * n + i]
                        last = nc.vector.tensor_copy(dst, tp[n % 4][0:cols, i, 0:rows])
                    last.then_inc(stat, 1)
                for t in range(NT):
                    if t % TPB == 0:
                        dve.wait_ge(x_in, 16 * B)
                    nc.vector.bn_stats(bn[:, t, :], core.x[:, t, :]).then_inc(deq, 1)
                for t in range(NT):
                    dve.wait_ge(deq, 2 * FB + KC + t + 1)
                    nc.vector.bn_aggr(core.mv[:, t, :], bn[:, t, :])

            @block.tensor
            def _(pe):
                pe.wait_ge(c_in, 16)
                for n in range(len(jobs) // 4):
                    if 4 * n < nq:
                        pe.wait_ge(deq, 2 * FB + KC)
                    else:
                        pe.wait_ge(w_in, 16 * 4)
                    if n >= 4:
                        k = n - 4
                        pe.wait_ge(stat if k % 2 == 0 else kept, k // 2 + 1)
                    for i in range(4):
                        src, rows, cols, _ = jobs[4 * n + i]
                        last = nc.tensor.transpose(tp[n % 4][0:cols, i, 0:rows], src, core.const("ident")[0:rows, 0:rows])
                    last.then_inc(turned, 1)


def ffn0_phase(core, tag):
    nc = core.nc
    with ExitStack() as ctx:
        sb, ps, sem = scope(core, ctx)
        xn = sb(tag + "xn", [P, CT, D])
        xT = sb(tag + "xT", [P, 2, KC, CW])
        silu = sb(tag + "silu", [P, 2, CW])
        silu2 = sb(tag + "silu2", [P, 2, CW])
        silu2_s = sem(tag + "silu2")
        hT = sb(tag + "hT", [P, FB, CW])
        bn = sb(tag + "bn", [P, CT, 6])
        mv4 = sb(tag + "mv4", [P, CT, 2])
        tp = ps(tag + "tp", [P, 2, KC, 2 * P])
        gate = ps(tag + "gate", [P, 2, CW])
        up = ps(tag + "up", [P, 2, CW])
        down = ps(tag + "down", [P, 2, 512])
        root, scales = sem(tag + "root"), sem(tag + "scales")
        normed, turned, xT_ready = sem(tag + "normed"), sem(tag + "turned"), sem(tag + "xT_ready")
        gu_ready, silu_ready, h_ready = sem(tag + "gu"), sem(tag + "silu_s"), sem(tag + "h")
        down_ready, x_done, stats = sem(tag + "down_s"), sem(tag + "x_done"), sem(tag + "stats")
        ident = core.const("ident")

        with nc.Block() as block:
            @block.tensor
            def _(pe):
                def turn(c):
                    for i in range(CT):
                        pe.wait_ge(normed, c * CT + i + 1)
                        if i % 2 == 0:
                            if not (isinstance(c, int) and c == 0):
                                pe.wait_ge(xT_ready, (c - 1) * 2 + i // 2 + 1)
                        for k in range(KC):
                            last = nc.tensor.transpose(tp[:, i // 2, k, (i % 2) * P:(i % 2 + 1) * P],
                                                       xn[:, i, k * P:(k + 1) * P], ident)
                        last.then_inc(turned, 1)

                def gate_up(c, s):
                    pe.wait_ge(xT_ready, c * 2 + 2)
                    for j in range(FB):
                        r = hid(j)
                        pe.wait_ge(h_ready, c * FB + j - 1) if j else pe.wait_ge(h_ready, c * FB)
                        for w, acc in ((core.wgT, gate), (core.wuT, up)):
                            for k in range(KC):
                                last = nc.tensor.matmul(acc[0:r, j % 2, :], w[:, k, j * P:j * P + r], xT[:, s, k, :],
                                                        start=(k == 0), stop=(k == KC - 1))
                        last.then_inc(gu_ready, 1)

                def down_proj(c):
                    pe.wait_ge(h_ready, c * FB + FB)
                    for i in range(CT):
                        if i >= 2:
                            pe.wait_ge(x_done, c * CT + i - 1)
                        else:
                            pe.wait_ge(x_done, c * CT)
                        for j in range(FB):
                            r = hid(j)
                            last = nc.tensor.matmul(down[:, i % 2, 0:D], hT[0:r, j, i * P:(i + 1) * P],
                                                    core.wdT[0:r, j, :], start=(j == 0), stop=(j == FB - 1))
                        last.then_inc(down_ready, 1)

                turn(0)
                with pe.Fori(0, NCH // 2 - 1) as it:
                    for s in range(2):
                        c = it * 2 + s
                        gate_up(c, s)
                        turn(c + 1)
                        down_proj(c)
                gate_up(NCH - 2, 0)
                turn(NCH - 1)
                down_proj(NCH - 2)
                gate_up(NCH - 1, 1)
                down_proj(NCH - 1)

            @block.scalar
            def _(act):
                nc.scalar.activation(core.rstd[:], core.mv[:, :, 1], ACT.Sqrt, bias=core.eps[:, 0:1]).then_inc(root, 1)

                def keep_xT(c, s):
                    for b in range(2):
                        act.wait_ge(turned, c * CT + 2 * b + 2)
                        nc.scalar.activation(xT[:, s, :, b * 2 * P:(b + 1) * 2 * P], tp[:, b], ACT.Copy).then_inc(xT_ready, 1)

                def silus(c):
                    for j in range(FB):
                        r = hid(j)
                        act.wait_ge(gu_ready, c * FB + j + 1)
                        act.wait_ge(h_ready, c * FB + max(j - 1, 0))
                        nc.scalar.activation(silu[0:r, j % 2, :], gate[0:r, j % 2, :], ACT.Tanh, scale=0.5).then_inc(silu_ready, 1)

                keep_xT(0, 0)
                with act.Fori(0, NCH // 2 - 1) as it:
                    for s in range(2):
                        c = it * 2 + s
                        silus(c)
                        keep_xT(c + 1, 1 - s)
                silus(NCH - 2)
                keep_xT(NCH - 1, 1)
                silus(NCH - 1)

            @block.vector
            def _(dve):
                dve.wait_ge(root, 1)
                nc.vector.reciprocal(core.rstd[:], core.rstd[:]).then_inc(scales, 1)
                dve.wait_ge(scales, 1)

                def normalise(c):
                    for i in range(CT):
                        t = c * CT + i
                        if not (isinstance(c, int) and c == 0):
                            dve.wait_ge(turned, (c - 1) * CT + i + 1)
                        nc.vector.tensor_scalar(xn[:, i, :], at(core.x, t), at(core.mv, t)[:, 0:1],
                                                col(core.rstd, t), ALU.subtract, ALU.mult).then_inc(normed, 1)

                def hidden(c, j):
                    r = hid(j)
                    dve.wait_ge(silu_ready, c * FB + j + 1)
                    if j == 0:
                        dve.wait_ge(down_ready, c * CT)
                    nc.vector.scalar_tensor_tensor(out=silu2[0:r, j % 2, :], in0=silu[0:r, j % 2, :], scalar=1.0,
                                                   in1=gate[0:r, j % 2, :], op0=ALU.add, op1=ALU.mult).then_inc(silu2_s, 1)
                    dve.wait_ge(silu2_s, c * FB + j + 1)
                    nc.vector.tensor_tensor(hT[0:r, j, :], silu2[0:r, j % 2, :], up[0:r, j % 2, :],
                                            ALU.mult).then_inc(h_ready, 1)

                def residual(c):
                    seen = 0
                    for i in range(CT):
                        t = c * CT + i
                        dve.wait_ge(down_ready, t + 1)
                        if i:
                            dve.wait_ge(stats, c * 2 * CT + seen)
                        nc.vector.scalar_tensor_tensor(out=at(core.x, t), in0=down[:, i % 2, 0:D], scalar=0.25,
                                                       in1=at(core.x, t), op0=ALU.mult, op1=ALU.add).then_inc(x_done, 1)
                        if i:
                            nc.vector.bn_aggr(mv4[:, i - 1, :], bn[:, i - 1, :]).then_inc(stats, 1)
                            seen += 1
                        dve.wait_ge(scales, 1)
                        dve.wait_ge(x_done, t + 1)
                        nc.vector.bn_stats(bn[:, i, :], at(core.x, t)).then_inc(stats, 1)
                        seen += 1
                    dve.wait_ge(stats, c * 2 * CT + seen)
                    nc.vector.tensor_copy(core.mv[:, bass.ds(c * CT, CT - 1), :], mv4[:, 0:CT - 1, :])
                    nc.vector.bn_aggr(mv4[:, CT - 1, :], bn[:, CT - 1, :]).then_inc(stats, 1)
                    dve.wait_ge(stats, (c + 1) * 2 * CT)
                    nc.vector.tensor_copy(at(core.mv, c * CT + CT - 1), mv4[:, CT - 1, :])

                def chunk(c, ahead):
                    for j in range(FB // 2):
                        hidden(c, j)
                    if ahead:
                        normalise(c + 1)
                    for j in range(FB // 2, FB):
                        hidden(c, j)
                    residual(c)

                normalise(0)
                with dve.Fori(0, NCH - 1) as c:
                    chunk(c, True)
                chunk(NCH - 1, False)


def mixture_dense_phase(core, tag, acc, load):
    nc, dram = core.nc, core.dram
    NR = NE + 1
    with ExitStack() as ctx:
        sb, ps, sem = scope(core, ctx)
        xn = sb(tag + "xn", [P, CT, D])
        xT = sb(tag + "xT", [P, 2, KC, CW])
        silu = sb(tag + "silu", [P, 2, CW])
        silu2 = sb(tag + "silu2", [P, 2, CW])
        silu2_s = sem(tag + "silu2")
        hT = sb(tag + "hT", [P, FB, CW])
        wn = sb(tag + "wn", [P, KC])
        wr = sb(tag + "wr", [P, KC, NR])
        both = sb(tag + "both", [P, NT])
        keep = sb(tag + "keep", [P, NT])
        shift = sb(tag + "shift", [P, NT])
        tmp = sb(tag + "tmp", [P, NT])
        zero = sb(tag + "zero", [P, D])
        empty = sb(tag + "empty", [P, NE, 2], I32)
        tri = sb(tag + "tri", [P, P], BF16)
        ones = sb(tag + "ones", [P, P], BF16)
        lg = sb(tag + "lg", [P, CT, NR])
        lmax = sb(tag + "lmax", [P, CT])
        prob = sb(tag + "prob", [P, CT, NE])
        psum_ = sb(tag + "psum", [P, CT])
        hgate = sb(tag + "hgate", [P, CT])
        top = sb(tag + "top", [P, CT, 8])
        topi = sb(tag + "topi", [P, CT, 8], U32)
        topf = sb(tag + "topf", [P, CT, TOPK])
        hot = sb(tag + "hot", [P, CT, TOPK, NE])
        hotr = sb(tag + "hotr", [P, CT, TOPK, NE])
        count = sb(tag + "count", [P, CT, NE])
        mask = sb(tag + "mask", [P, CT, NE], BF16)
        before_ = sb(tag + "before", [P, CT + 1, NE], BF16)
        pos = sb(tag + "pos", [P, CT, TOPK])
        over = sb(tag + "over", [P, CT, TOPK])
        dest = sb(tag + "dest", [P, CT, TOPK], I32)
        entry = sb(tag + "entry", [P, CT, TOPK, 2], I32)
        tp = ps(tag + "tp", [P, 2, KC, 2 * P])
        gate = ps(tag + "gate", [P, 2, CW])
        up = ps(tag + "up", [P, 2, CW])
        down = ps(tag + "down", [P, 2, 512])
        logits = down[:, 0, D:D + CT * NR].rearrange("p (i e) -> p i e", i=CT)
        ranks = down[:, 1, D:D + CT * NE].rearrange("p (i e) -> p i e", i=CT)
        names = ("w_in root1 root2 scales setup tables normed xn_sent turned xT_ready logit_s gu silu_s h_s down_s x_done "
                 "acc_sent shifted exp_s route masked ranked dest_ready placed lg_kept ranks_used gated posted")
        (w_in, root1, root2, scales, setup, tables, normed, xn_sent, turned, xT_ready, logit_s, gu_ready, silu_ready,
         h_ready, down_ready, x_done, acc_sent, shifted, exp_s, route, masked, ranked, dest_ready,
         placed, lg_kept, ranks_used, gated, posted) = (sem(tag + n) for n in names.split())
        ident = core.const("ident")
        STEPS = 15

        with nc.Block() as block:
            @block.sync
            def _(sp):
                full = (FB - 1) * P
                if load:
                    sp.dma_start(core.wgT[:], dram["L1_ffn_sw_gate"].rearrange("(k p) f -> p k f", p=P)).then_inc(w_in, 16)
                    sp.dma_start(core.wuT[:], dram["L1_ffn_sw_up"].rearrange("(k p) f -> p k f", p=P)).then_inc(w_in, 16)
                    sp.dma_start(core.wdT[:, 0:FB - 1, :], dram["L1_ffn_sw_down"][0:full].rearrange("(j p) d -> p j d", p=P)).then_inc(w_in, 16)
                    sp.dma_start(core.wdT[0:hid(FB - 1), FB - 1, :], dram["L1_ffn_sw_down"][full:FF]).then_inc(w_in, 16)
                sp.dma_start(wr[:, :, 0:NE], dram["L1_ffn_w_router"].rearrange("(k p) e -> p k e", p=P)).then_inc(w_in, 16)
                sp.dma_start(wr[:, :, NE:NR], dram["L1_ffn_w_shared_gate"].rearrange("(k p) e -> p k e", p=P)).then_inc(w_in, 16)
                sp.dma_start(wn[:].rearrange("p (k a) -> p k a", a=1),
                             dram["L1_ffn_w_norm"].rearrange("(k p a) -> p k a", p=P, a=1)).then_inc(w_in, 16)
                sp.wait_ge(setup, 1)
                sp.dma_start(dram["xn"][NTOK:NTOK + TRASH, :], zero[:]).then_inc(tables, 16)
                sp.dma_start(acc[NTOK:NTOK + TRASH, :], zero[:]).then_inc(tables, 16)
                sp.dma_start(dram["table"].rearrange("(e s) w -> s e w", e=NE), empty[:]).then_inc(tables, 16)
                with sp.Fori(0, NCH) as c:
                    sp.wait_ge(normed, (c + 1) * CT)
                    sp.dma_start(dram["xn"][bass.ds(c * CW, CW), :].rearrange("(i p) d -> p i d", p=P), xn[:]).then_inc(xn_sent, 16)
                    sp.wait_ge(x_done, (c + 1) * CT)
                    sp.dma_start(acc[bass.ds(c * CW, CW), :].rearrange("(i p) d -> p i d", p=P),
                                 core.x[:, bass.ds(c * CT, CT), :]).then_inc(acc_sent, 16)
                sp.wait_ge(xn_sent, 16 * NCH)
                sp.wait_ge(acc_sent, 16 * NCH)

            @block.gpsimd
            def _(pool):
                pool.wait_ge(tables, 48)
                with pool.Fori(0, NCH) as c:
                    pool.wait_ge(dest_ready, c + 1)
                    pool.sem_inc(posted, 1)
                    for i in range(CT):
                        for k in range(TOPK):
                            nc.gpsimd.indirect_dma_start(
                                out=dram["table"], out_offset=bass.IndirectOffsetOnAxis(ap=dest[:, i, k:k + 1], axis=0),
                                in_=entry[:, i, k, :], in_offset=None,
                                bounds_check=NE * CAP - 1, oob_is_err=False).then_inc(placed, 16)
                pool.wait_ge(placed, 16 * NCH * CT * TOPK)

            @block.tensor
            def _(pe):
                def turn(c):
                    for i in range(CT):
                        pe.wait_ge(normed, c * CT + i + 1)
                        if i % 2 == 0 and not (isinstance(c, int) and c == 0):
                            pe.wait_ge(xT_ready, (c - 1) * 2 + i // 2 + 1)
                        for k in range(KC):
                            last = nc.tensor.transpose(tp[:, i // 2, k, (i % 2) * P:(i % 2 + 1) * P],
                                                       xn[:, i, k * P:(k + 1) * P], ident)
                        last.then_inc(turned, 1)

                def route_logits(c, s):
                    pe.wait_ge(xT_ready, c * 2 + 2)
                    pe.wait_ge(route, c * STEPS)
                    pe.wait_ge(exp_s, c * 2)
                    pe.wait_ge(x_done, c * CT)
                    for i in range(CT):
                        for k in range(KC):
                            last = nc.tensor.matmul(logits[:, i, :], xT[:, s, k, i * P:(i + 1) * P], wr[:, k, :],
                                                    start=(k == 0), stop=(k == KC - 1))
                    last.then_inc(logit_s, 1)

                def rank(c):
                    pe.wait_ge(masked, c + 1)
                    for i in range(CT):
                        nc.tensor.matmul(ranks[:, i, :], tri[:], mask[:, i, :], start=True, stop=False)
                        last = nc.tensor.matmul(ranks[:, i, :], ones[:], before_[:, i, :], start=False, stop=True)
                    last.then_inc(ranked, 1)

                def gate_up(c, s):
                    for j in range(FB):
                        r = hid(j)
                        pe.wait_ge(h_ready, c * FB + max(j - 1, 0))
                        for w, out in ((core.wgT, gate), (core.wuT, up)):
                            for k in range(KC):
                                last = nc.tensor.matmul(out[0:r, j % 2, :], w[:, k, j * P:j * P + r], xT[:, s, k, :],
                                                        start=(k == 0), stop=(k == KC - 1))
                        last.then_inc(gu_ready, 1)
                        if j == 4:
                            rank(c)

                def down_proj(c):
                    pe.wait_ge(h_ready, c * FB + FB)
                    pe.wait_ge(lg_kept, c + 1)
                    pe.wait_ge(ranks_used, c + 1)
                    for i in range(CT):
                        pe.wait_ge(x_done, c * CT + max(i - 1, 0))
                        for j in range(FB):
                            r = hid(j)
                            last = nc.tensor.matmul(down[:, i % 2, 0:D], hT[0:r, j, i * P:(i + 1) * P],
                                                    core.wdT[0:r, j, :], start=(j == 0), stop=(j == FB - 1))
                        last.then_inc(down_ready, 1)

                def chunk(c, s, ahead):
                    route_logits(c, s)
                    gate_up(c, s)
                    if ahead:
                        turn(c + 1)
                    down_proj(c)

                pe.wait_ge(w_in, 16 * (7 if load else 3))
                pe.wait_ge(setup, 2)
                turn(0)
                with pe.Fori(0, NCH // 2 - 1) as it:
                    for s in range(2):
                        chunk(it * 2 + s, s, True)
                chunk(NCH - 2, 0, True)
                chunk(NCH - 1, 1, False)

            @block.scalar
            def _(act):
                nc.scalar.activation(core.rstd[:], core.mv[:, :, 1], ACT.Sqrt, bias=core.eps[:, 0:1]).then_inc(root1, 1)
                act.wait_ge(scales, 3)
                nc.scalar.activation(both[:], tmp[:], ACT.Sqrt, bias=core.eps[:, 1:2]).then_inc(root2, 1)
                act.wait_ge(w_in, 16 * (7 if load else 3))

                def keep_xT(c, s):
                    for b in range(2):
                        act.wait_ge(turned, c * CT + 2 * b + 2)
                        for k in range(KC):
                            last = nc.scalar.activation(xT[:, s, k, b * 2 * P:(b + 1) * 2 * P], tp[:, b, k, :], ACT.Copy,
                                                        scale=wn[:, k:k + 1])
                        last.then_inc(xT_ready, 1)

                def route_exps(c):
                    act.wait_ge(lg_kept, c + 1)
                    act.wait_ge(x_done, c * CT)
                    nc.scalar.activation(hgate[:], lg[:, :, NE], ACT.Exp, scale=-1.0).then_inc(exp_s, 1)
                    act.wait_ge(shifted, c + 1)
                    nc.scalar.activation(prob[:], prob[:], ACT.Exp).then_inc(exp_s, 1)

                def silus(c):
                    for j in range(FB):
                        r = hid(j)
                        if j == 1:
                            route_exps(c)
                        act.wait_ge(gu_ready, c * FB + j + 1)
                        act.wait_ge(h_ready, c * FB + max(j - 1, 0))
                        nc.scalar.activation(silu[0:r, j % 2, :], gate[0:r, j % 2, :], ACT.Tanh, scale=0.5).then_inc(silu_ready, 1)

                keep_xT(0, 0)
                with act.Fori(0, NCH // 2 - 1) as it:
                    for s in range(2):
                        silus(it * 2 + s)
                        keep_xT(it * 2 + s + 1, 1 - s)
                silus(NCH - 2)
                keep_xT(NCH - 1, 1)
                silus(NCH - 1)

            @block.vector
            def _(dve):
                nc.vector.memset(zero[:], 0.0)
                nc.vector.memset(empty[:, :, 1], 0)
                nc.vector.tensor_copy(empty[:, :, 0], core.const("slot")).then_inc(setup, 1)
                nc.vector.memset(before_[:, CT, :], 0.0)
                nc.vector.memset(ones[:], 1.0)
                nc.vector.tensor_copy(tri[:], core.const("tri")).then_inc(setup, 1)
                steps = 0

                def scale_step(instruction):
                    nonlocal steps
                    steps += 1
                    instruction.then_inc(scales, 1)
                    dve.wait_ge(scales, steps)

                dve.wait_ge(root1, 1)
                scale_step(nc.vector.reciprocal(core.rstd[:], core.rstd[:]))
                scale_step(nc.vector.tensor_tensor(tmp[:], core.rstd[:], core.mv[:, :, 1], ALU.mult))
                scale_step(nc.vector.tensor_tensor(tmp[:], tmp[:], core.rstd[:], ALU.mult))
                dve.wait_ge(root2, 1)
                scale_step(nc.vector.reciprocal(both[:], both[:]))
                scale_step(nc.vector.tensor_tensor(both[:], both[:], core.rstd[:], ALU.mult))
                scale_step(nc.vector.tensor_scalar(keep[:], core.rstd[:], 0.5, 1.0, ALU.mult, ALU.add))
                scale_step(nc.vector.tensor_tensor(shift[:], core.rstd[:], core.mv[:, :, 0], ALU.mult))
                scale_step(nc.vector.tensor_scalar(shift[:], shift[:], -0.5, None, ALU.mult))

                def normalise(c):
                    for i in range(CT):
                        t = c * CT + i
                        if not (isinstance(c, int) and c == 0):
                            dve.wait_ge(turned, (c - 1) * CT + i + 1)
                            dve.wait_ge(xn_sent, c * 16)
                        nc.vector.tensor_scalar(xn[:, i, :], at(core.x, t), at(core.mv, t)[:, 0:1],
                                                col(both, t), ALU.subtract, ALU.mult).then_inc(normed, 1)

                def hidden(c, j):
                    r = hid(j)
                    dve.wait_ge(silu_ready, c * FB + j + 1)
                    if j == 0:
                        dve.wait_ge(down_ready, c * CT)
                    nc.vector.scalar_tensor_tensor(out=silu2[0:r, j % 2, :], in0=silu[0:r, j % 2, :], scalar=1.0,
                                                   in1=gate[0:r, j % 2, :], op0=ALU.add, op1=ALU.mult).then_inc(silu2_s, 1)
                    dve.wait_ge(silu2_s, c * FB + j + 1)
                    nc.vector.tensor_tensor(hT[0:r, j, :], silu2[0:r, j % 2, :], up[0:r, j % 2, :],
                                            ALU.mult).then_inc(h_ready, 1)

                def residual(c):
                    for i in range(CT):
                        t = c * CT + i
                        nc.vector.tensor_scalar(at(core.x, t), at(core.x, t), col(keep, t), col(shift, t),
                                                ALU.mult, ALU.add).then_inc(setup, 1)
                    for i in range(CT):
                        t = c * CT + i
                        dve.wait_ge(setup, t + 3)
                        dve.wait_ge(down_ready, t + 1)
                        nc.vector.scalar_tensor_tensor(out=at(core.x, t), in0=down[:, i % 2, 0:D], scalar=hgate[:, i:i + 1],
                                                       in1=at(core.x, t), op0=ALU.mult, op1=ALU.add).then_inc(x_done, 1)

                done = 0

                def link(c, instruction):
                    nonlocal done
                    done += 1
                    instruction.then_inc(route, 1)
                    dve.wait_ge(route, c * STEPS + done)

                def shift_logits(c):
                    dve.wait_ge(logit_s, c + 1)
                    nc.vector.tensor_copy(lg[:], logits).then_inc(lg_kept, 1)
                    dve.wait_ge(lg_kept, c + 1)
                    link(c, nc.vector.tensor_reduce(lmax[:], lg[:, :, 0:NE], AX.X, ALU.max))
                    nc.vector.tensor_tensor(prob[:], lg[:, :, 0:NE], spread(lmax[:], 2, NE), ALU.subtract).then_inc(shifted, 1)

                def choose(c):
                    dve.wait_ge(exp_s, 2 * c + 2)
                    link(c, nc.vector.tensor_reduce(psum_[:], prob[:], AX.X, ALU.add))
                    link(c, nc.vector.reciprocal(psum_[:], psum_[:]))
                    link(c, nc.vector.tensor_tensor(prob[:], prob[:], spread(psum_[:], 2, NE), ALU.mult))
                    nc.vector.tensor_scalar(hgate[:], hgate[:], 4.0, 4.0, ALU.mult, ALU.add).then_inc(gated, 1)
                    for i in range(CT):
                        last = nc.vector.max(top[:, i, :], prob[:, i, :])
                    link(c, last)
                    dve.wait_ge(gated, c + 1)
                    nc.vector.reciprocal(hgate[:], hgate[:])
                    for i in range(CT):
                        last = nc.vector.max_index(topi[:, i, :], top[:, i, :], prob[:, i, :])
                    link(c, last)

                def count_experts(c):
                    link(c, nc.vector.tensor_copy(topf[:], topi[:, :, 0:TOPK]))
                    expert = spread(spread(core.const("expert"), 1, TOPK), 1, CT)
                    link(c, nc.vector.tensor_tensor(hot[:], expert, spread(topf[:], 3, NE), ALU.is_equal))
                    link(c, nc.vector.tensor_reduce(count[:], hot[:].rearrange("p i k e -> p i e k"), AX.X, ALU.add))
                    nc.vector.tensor_copy(mask[:], count[:])
                    link(c, nc.vector.tensor_copy(before_[:, 0, :], before_[:, CT, :]))
                    for i in range(CT):
                        last = nc.vector.tensor_tensor(before_[:, i + 1, :], before_[:, i, :], mask[:, i, :], ALU.add)
                        if i < CT - 1:
                            link(c, last)
                    last.then_inc(masked, 1)

                def place(c):
                    dve.wait_ge(ranked, c + 1)
                    dve.wait_ge(placed, c * 16 * CT * TOPK)
                    nc.vector.tensor_tensor(hotr[:], hot[:], spread(ranks, 2, TOPK), ALU.mult).then_inc(ranks_used, 1)
                    dve.wait_ge(ranks_used, c + 1)
                    link(c, nc.vector.tensor_reduce(pos[:], hotr[:], AX.X, ALU.add))
                    nc.vector.tensor_scalar(over[:], pos[:], float(CAP), float(2 * NE * CAP), ALU.is_ge, ALU.mult)
                    link(c, nc.vector.scalar_tensor_tensor(out=pos[:], in0=topf[:], scalar=float(CAP), in1=pos[:],
                                                           op0=ALU.mult, op1=ALU.add))
                    nc.vector.tensor_copy(entry[:, :, :, 0], spread(core.const("token")[:, bass.ds(c * CT, CT)], 2, TOPK))
                    nc.vector.tensor_copy(entry[:].bitcast(F32)[:, :, :, 1], top[:, :, 0:TOPK])
                    nc.vector.tensor_tensor(dest[:], pos[:], over[:], ALU.add).then_inc(dest_ready, 1)

                def chunk(c, ahead):
                    nonlocal done
                    done = 0
                    hidden(c, 0)
                    shift_logits(c)
                    hidden(c, 1)
                    choose(c)
                    hidden(c, 2)
                    count_experts(c)
                    hidden(c, 3)
                    if ahead:
                        normalise(c + 1)
                    hidden(c, 4)
                    place(c)
                    assert done == STEPS, done
                    hidden(c, 5)
                    residual(c)

                normalise(0)
                with dve.Fori(0, NCH - 1) as c:
                    chunk(c, True)
                chunk(NCH - 1, False)


def experts_phase(core, tag, acc):
    nc, dram = core.nc, core.dram
    with ExitStack() as ctx:
        sb, ps, sem = scope(core, ctx)
        wn = sb(tag + "wn", [P, KC])
        table = sb(tag + "table", [P, NE, 2], I32)
        gidx = sb(tag + "gidx", [P, 2], I32)
        sidx = sb(tag + "sidx", [P, 2], I32)
        wgu = sb(tag + "wgu", [P, 2, KC, 2 * EF])
        wd = sb(tag + "wd", [EH, 2, 2, D])
        xg = sb(tag + "xg", [P, 2, D])
        xgT = sb(tag + "xgT", [P, 2, KC, P])
        silu = sb(tag + "silu", [P, 2, EF])
        silu2 = sb(tag + "silu2", [P, 2, EF])
        silu2_s = sem(tag + "silu2")
        h = sb(tag + "h", [P, 2, EF])
        hT = sb(tag + "hT", [EH, 2, 2, P])
        ys = sb(tag + "ys", [P, 2, D])
        tp = ps(tag + "tp", [P, 2, 512])
        gu = ps(tag + "gu", [P, 2, 512])
        ht = ps(tag + "ht", [P, 2, 512])
        dn = ps(tag + "dn", [P, 2, 512])
        names = "small_in gidx_s turned xgT_s gu_s silu_s h_s h_turned hT_s dn_s y_s added posted"
        (small_in, gidx_s, turned, xgT_s, gu_s, silu_s, h_s, h_turned, hT_s, dn_s, y_s,
         added, posted) = (sem(tag + n) for n in names.split())
        w_slot = [sem(f"{tag}w_slot{s}") for s in range(2)]
        gathered = [sem(f"{tag}gathered{s}") for s in range(2)]
        ident = core.const("ident")

        def pairs(eng, body):
            body(0, 0, 0, True)
            body(0, 1, 1, True)
            with eng.Fori(1, NE // 2 - 1) as it:
                for s in range(2):
                    body(it, it * 2 + s, s, True)
            body(NE // 2 - 1, NE - 2, 0, True)
            body(NE // 2 - 1, NE - 1, 1, False)

        with nc.Block() as block:
            @block.sync
            def _(sp):
                sp.dma_start(table[:], dram["table"].rearrange("(e s) w -> s e w", e=NE)).then_inc(small_in, 16)
                sp.dma_start(wn[:].rearrange("p (k a) -> p k a", a=1),
                             dram["L1_ffn_w_norm"].rearrange("(k p a) -> p k a", p=P, a=1)).then_inc(small_in, 16)

                def load(e, s):
                    for w, name in enumerate(("L1_ffn_w_gate", "L1_ffn_w_up")):
                        sp.dma_start(wgu[:, s, :, w * EF:(w + 1) * EF],
                                     dram[name][bass.ds(e, 1)].rearrange("a (k p) f -> p (a k) f", p=P)).then_inc(w_slot[s], 16)
                    sp.dma_start(wd[:, s], dram["L1_ffn_w_down"][bass.ds(e, 1)].rearrange("a (h f) d -> f (a h) d", h=2)).then_inc(w_slot[s], 16)

                load(0, 0)
                load(1, 1)
                with sp.Fori(1, NE // 2) as it:
                    for s in range(2):
                        sp.wait_ge(dn_s, it * 2 + s - 1)
                        load(it * 2 + s, s)

            @block.gpsimd
            def _(pool):
                def gather(e, s):
                    pool.wait_ge(gidx_s, e + 1)
                    pool.sem_inc(posted, 1)
                    nc.gpsimd.indirect_dma_start(out=xg[:, s, :], out_offset=None, in_=dram["xn"],
                                                 in_offset=bass.IndirectOffsetOnAxis(ap=gidx[:, s:s + 1], axis=0),
                                                 bounds_check=NTOK + TRASH - 1, oob_is_err=True).then_inc(gathered[s], 16)

                def add(e, s):
                    pool.wait_ge(y_s, e + 1)
                    pool.wait_ge(added, 16 * e)
                    pool.sem_inc(posted, 1)
                    nc.gpsimd.indirect_dma_start(out=acc, out_offset=bass.IndirectOffsetOnAxis(ap=sidx[:, s:s + 1], axis=0),
                                                 in_=ys[:, s, :], in_offset=None, compute_op=ALU.add,
                                                 bounds_check=NTOK + TRASH - 1, oob_is_err=True).then_inc(added, 16)

                gather(0, 0)
                gather(1, 1)
                with pool.Fori(0, NE // 2 - 1) as it:
                    for s in range(2):
                        add(it * 2 + s, s)
                        gather(it * 2 + s + 2, s)
                add(NE - 2, 0)
                add(NE - 1, 1)
                pool.wait_ge(added, 16 * NE)

            @block.tensor
            def _(pe):
                def turn(it, e, s):
                    pe.wait_ge(gathered[s], 16 * (it + 1))
                    for k in range(KC):
                        last = nc.tensor.transpose(tp[:, s, k * P:(k + 1) * P], xg[:, s, k * P:(k + 1) * P], ident)
                    last.then_inc(turned, 1)

                def gate_up(it, e, s):
                    pe.wait_ge(xgT_s, e + 1)
                    pe.wait_ge(w_slot[s], 48 * (it + 1))
                    if not (isinstance(e, int) and e < 2):
                        pe.wait_ge(h_s, e - 1)
                    for k in range(KC):
                        last = nc.tensor.matmul(gu[:, s, 0:2 * EF], xgT[:, s, k, :], wgu[:, s, k, :],
                                                start=(k == 0), stop=(k == KC - 1))
                    last.then_inc(gu_s, 1)

                def turn_h(e, s):
                    pe.wait_ge(h_s, e + 1)
                    for half in range(2):
                        last = nc.tensor.transpose(ht[0:EH, s, half * P:(half + 1) * P], h[:, s, half * EH:(half + 1) * EH], ident)
                    last.then_inc(h_turned, 1)

                def down(e, s):
                    pe.wait_ge(hT_s, e + 1)
                    if not (isinstance(e, int) and e < 2):
                        pe.wait_ge(y_s, e - 1)
                    for half in range(2):
                        last = nc.tensor.matmul(dn[:, s, 0:D], hT[:, s, half, :], wd[:, s, half, :], start=(half == 0), stop=(half == 1))
                    last.then_inc(dn_s, 1)

                def body(it, e, s, more):
                    if more:
                        turn(it + s, e + 1, 1 - s)
                    turn_h(e, s)
                    if more:
                        gate_up(it + s, e + 1, 1 - s)
                    down(e, s)

                turn(0, 0, 0)
                gate_up(0, 0, 0)
                pairs(pe, body)

            @block.scalar
            def _(act):
                act.wait_ge(small_in, 32)

                def keep(e, s):
                    act.wait_ge(turned, e + 1)
                    for k in range(KC):
                        last = nc.scalar.activation(xgT[:, s, k, :], tp[:, s, k * P:(k + 1) * P], ACT.Copy, scale=wn[:, k:k + 1])
                    last.then_inc(xgT_s, 1)

                def body(it, e, s, more):
                    act.wait_ge(gu_s, e + 1)
                    nc.scalar.activation(silu[:, s, :], gu[:, s, 0:EF], ACT.Tanh, scale=0.5).then_inc(silu_s, 1)
                    if more:
                        keep(e + 1, 1 - s)
                    act.wait_ge(h_turned, e + 1)
                    nc.scalar.activation(hT[:, s], ht[0:EH, s, 0:2 * P].rearrange("p (h c) -> p h c", h=2), ACT.Copy).then_inc(hT_s, 1)

                keep(0, 0)
                pairs(act, body)

            @block.vector
            def _(dve):
                dve.wait_ge(small_in, 32)
                for e in range(2):
                    nc.vector.tensor_copy(gidx[:, e:e + 1], table[:, e, 0:1]).then_inc(gidx_s, 1)

                def weigh(e, s):
                    dve.wait_ge(dn_s, e + 1)
                    if not (isinstance(e, int) and e < 2):
                        dve.wait_ge(added, 16 * (e - 1))
                    nc.vector.tensor_copy(sidx[:, s:s + 1], at(table, e)[:, 0:1])
                    nc.vector.tensor_scalar(ys[:, s, :], dn[:, s, 0:D], at(table[:].bitcast(F32), e)[:, 1:2], 0.25,
                                            ALU.mult, ALU.mult).then_inc(y_s, 1)

                def body(it, e, s, more):
                    dve.wait_ge(silu_s, e + 1)
                    nc.vector.scalar_tensor_tensor(out=silu2[:, s, :], in0=silu[:, s, :], scalar=1.0, in1=gu[:, s, 0:EF],
                                                   op0=ALU.add, op1=ALU.mult).then_inc(silu2_s, 1)
                    dve.wait_ge(silu2_s, e + 1)
                    nc.vector.tensor_tensor(h[:, s, :], silu2[:, s, :], gu[:, s, EF:2 * EF], ALU.mult).then_inc(h_s, 1)
                    if not (isinstance(e, int) and e >= NE - 2):
                        dve.wait_ge(gathered[s], 16 * (it + 1))
                        nc.vector.tensor_copy(gidx[:, s:s + 1], at(table, e + 2)[:, 0:1]).then_inc(gidx_s, 1)
                    weigh(e, s)

                pairs(dve, body)


def reload_phase(core, tag, acc):
    nc = core.nc
    with ExitStack() as ctx:
        sb, _, sem = scope(core, ctx)
        bn = sb(tag + "bn", [P, NT, 6])
        back, stats = [sem(f"{tag}back{b}") for b in range(B)], sem(tag + "stats")
        with nc.Block() as block:
            @block.sync
            def _(sp):
                for b in range(B):
                    sp.dma_start(core.x[:, b * TPB:(b + 1) * TPB, :],
                                 acc[b * T:(b + 1) * T, :].rearrange("(i p) d -> p i d", p=P)).then_inc(back[b], 16)

            @block.vector
            def _(dve):
                for t in range(NT):
                    if t % TPB == 0:
                        dve.wait_ge(back[t // TPB], 16)
                    last = nc.vector.bn_stats(bn[:, t, :], core.x[:, t, :])
                last.then_inc(stats, 1)
                dve.wait_ge(stats, 1)
                for t in range(NT):
                    nc.vector.bn_aggr(core.mv[:, t, :], bn[:, t, :])


def spread(ap, axis, n):
    u = ap.unsqueeze(axis)
    shape = list(u.shape)
    shape[axis] = n
    return u.to_broadcast(shape)


def attention_phase(core, tag, second):
    nc, dram = core.nc, core.dram
    W = 6 * HD + (6 if second else 0)
    WM = W + 3
    GH = 4
    NG = NH // GH
    HALF = 512
    QH = T // HALF
    KPH = HALF // P
    units = [(h, kt, max(0, kt - KPH * h) * P if second else 0)
             for h in range(QH) for kt in range(KPH * (h + 1) if second else TPB)]
    U = len(units)
    chunks = [(j, qt, kh, min(HALF, (qt + 1) * P - kh * HALF) if second else HALF)
              for j in range(GH) for qt in range(TPB) for kh in range(2)
              if not second or (qt + 1) * P > kh * HALF]
    C = len(chunks)
    beside = [C * min(u, U - 2) // (U - 2) for u in range(U + 1)]
    NV = 2

    with ExitStack() as ctx:
        sb, ps, sem = scope(core, ctx)
        xn = sb(tag + "xn", [P, TPB, D])
        y = xn
        xT = sb(tag + "xT", [P, KC, T])
        qk = sb(tag + "qk", [P, 2, 2 * NH, HD])
        rot = sb(tag + "rot", [P, 2, 2 * NH, ROPE])
        rest = sb(tag + "rest", [P, 2, NH, HD])
        A = sb(tag + "A", [P, 2, 2, NH, W], BF16)
        QT = sb(tag + "QT", [WM, NH, T], BF16)
        KT = sb(tag + "KT", [WM, NH, T], BF16)
        V = sb(tag + "V", [P, TPB, NH, HD])
        Vg = sb(tag + "Vg", [P, TPB, GH, VW])
        E = sb(tag + "E", [P, 2, GH, HALF])
        Ysb = sb(tag + "Ysb", [P, 2, HALF])
        rden = sb(tag + "rden", [P, KPH, GH])
        mx = sb(tag + "mx", [P, GH, TPB, 2])
        m = sb(tag + "m", [P, GH, TPB])
        mrest = sb(tag + "mrest", [P, GH, TPB])
        mparts = sb(tag + "mparts", [P, GH, 3, TPB], BF16)
        mT = sb(tag + "mT", [GH * 3 * TPB, P], BF16)
        yT = sb(tag + "yT", [P, 2, KC, P])
        bn8 = sb(tag + "bn8", [P, TPB, 6])
        carrier = sb(tag + "carrier", [P, 1])
        mv8 = sb(tag + "mv8", [P, TPB, 2])
        masks = sb(tag + "masks", [P, 2, P], BF16)
        bank = ps(tag + "bank", [P, 8, 512])
        ident, ident_b = core.const("ident"), core.ident_b
        names = ("w_in ones consts_b root scales normed turned xT_kept qkv qk_kept v_kept roped part1 rested "
                 "part2 parts ops_turned ops_dve ops_act chunk_done reduced v_group m_step m_turned mT_kept m_rows "
                 "scored exps pv y_kept y_turned y_step y_normed out_turned yT_kept out_done x_done stats aggregated")
        S = {n: sem(tag + n) for n in names.split()}
        (w_in, ones, consts_b, root, scales, normed, turned, xT_kept, qkv, qk_kept, v_kept, roped, part1, rested,
         part2, parts, ops_turned, ops_dve, ops_act, chunk_done, reduced, v_group, m_step, m_turned, mT_kept, m_rows,
         scored, exps, pv, y_kept, y_turned, y_step, y_normed, out_turned, yT_kept, out_done, x_done,
         stats, aggregated) = (S[n] for n in names.split())

        def tile_bank(i):
            return bank[:, (i // 2) % 2, :].rearrange("p (k h c) -> p k h c", k=KC, h=2)

        def ops_bank(n):
            return bank[:, 5 + n % 2, :].bitcast(BF16).rearrange("p (h c) -> p h c", h=8)

        def before(b, per_batch, n):
            return b * per_batch + max(n, 0)

        with nc.Block() as block:
            @block.sync
            def _(sp):
                if second:
                    sp.dma_start(core.wqkvT[:], dram["L1_attn_W_qkv"].rearrange("(k p) e -> p k e", p=P)).then_inc(w_in, 16)
                    sp.dma_start(core.woT[:], dram["L1_attn_W_o"].rearrange("(k p) e -> p k e", p=P)).then_inc(w_in, 16)

                def rows(b, g):
                    sp.wait_ge(mT_kept, b * NG + g + 1)
                    for j in range(GH):
                        h = g * GH + j
                        dst = QT[W:WM, h, :].rearrange("r (q c) -> r q c", c=P)
                        sp.dma_start(dst, mT[j * 3 * TPB:(j + 1) * 3 * TPB, :]).then_inc(m_rows, 16)

                with sp.Fori(0, B) as b:
                    for g in range(NG):
                        rows(b, g)

            @block.gpsimd
            def _(pool):
                def rope(b, i):
                    tab = core.const("rope").rearrange("p (i s r) -> p i s r", i=TPB, s=2)
                    z = qk[:, i % 2]
                    pool.wait_ge(qk_kept, b * TPB + i + 1)
                    pool.wait_ge(roped, b * 2 * TPB + 2 * i)
                    H2 = ROPE // 2
                    nc.gpsimd.tensor_tensor(rot[:, 1, :, 0:H2], z[:, :, H2:ROPE], spread(tab[:, i, 1, 0:H2], 1, 2 * NH), ALU.mult)
                    nc.gpsimd.tensor_tensor(rot[:, 1, :, H2:ROPE], z[:, :, 0:H2], spread(tab[:, i, 1, H2:ROPE], 1, 2 * NH), ALU.mult)
                    nc.gpsimd.tensor_tensor(rot[:, 0, :, :], z[:, :, 0:ROPE], spread(tab[:, i, 0, :], 1, 2 * NH),
                                            ALU.mult).then_inc(roped, 1)
                    pool.wait_ge(roped, b * 2 * TPB + 2 * i + 1)
                    nc.gpsimd.tensor_tensor(z[:, :, 0:ROPE], rot[:, 0], rot[:, 1], ALU.add).then_inc(roped, 1)

                def rests(b, i):
                    pool.wait_ge(part1, b * TPB + i + 1)
                    pool.wait_ge(parts, b * TPB + i)
                    for q, slot in ((0, 0), (1, 1)):
                        a = A[:, i % 2, q, :, 0:6 * HD].rearrange("p h (s d) -> p h s d", d=HD)
                        nc.gpsimd.tensor_tensor(rest[:, q], qk[:, i % 2, q * NH:(q + 1) * NH, :], a[:, :, slot, :],
                                                ALU.subtract).then_inc(rested, 1)

                def third_parts(b, i):
                    pool.wait_ge(part2, b * TPB + i + 1)
                    for q, low, slot in ((0, 3, 5), (1, 0, 2)):
                        a = A[:, i % 2, q, :, 0:6 * HD].rearrange("p h (s d) -> p h s d", d=HD)
                        last = nc.gpsimd.tensor_tensor(a[:, :, slot, :], rest[:, q], a[:, :, low, :], ALU.subtract)
                    last.then_inc(parts, 1)

                with pool.Fori(0, B) as b:
                    if not second:
                        rope(b, 0)
                    for i in range(TPB):
                        if not second and i + 1 < TPB:
                            rope(b, i + 1)
                        rests(b, i)
                        third_parts(b, i)
                    for g in range(NG):
                        pool.wait_ge(consts_b, 1)
                        pool.wait_ge(v_kept, (b + 1) * TPB)
                        pool.wait_ge(pv, (b * NG + g) * U)
                        own = V[:, :, g * GH:(g + 1) * GH, :]
                        one = Vg[:, :, :, HD:HD + 1].to_broadcast([P, TPB, GH, HD])
                        nc.gpsimd.tensor_tensor(Vg[:, :, :, 0:HD], own, one, ALU.mult).then_inc(v_group, 1)

            @block.tensor
            def _(pe):
                def max_chunks(G, head, lo, hi):
                    for n in range(lo, min(hi, C)):
                        j, qt, kh, w = chunks[n]
                        pe.wait_ge(reduced, G * C + max(n - 1, 0))
                        out = bank[:, 5 + n % 2, 0:w]
                        q = QT[0:W, head + j, qt * P:(qt + 1) * P]
                        k = KT[0:W, head + j, kh * HALF:kh * HALF + w]
                        diag = second and qt * P < kh * HALF + w <= (qt + 1) * P
                        last = nc.tensor.matmul(out, q, k, start=True, stop=not diag)
                        if diag:
                            last = nc.tensor.matmul(out[:, w - P:w], ident_b[:], masks[:, 0, :], start=False, stop=True)
                        last.then_inc(chunk_done, 1)

                def turn_max(G):
                    pe.wait_ge(m_step, (G + 1) * 4)
                    out = bank[0:GH * 3 * TPB, 5, :].bitcast(BF16)[:, 0:P]
                    nc.tensor.transpose(out, mparts[:].rearrange("p j r q -> p (j r q)"), ident_b[:]).then_inc(m_turned, 1)

                def score_pair(G, head, u, pair):
                    half, kt, c0 = units[u]
                    pe.wait_ge(exps, G * 2 * U + (2 * u - 1 + pair if u else 0))
                    for j in (2 * pair, 2 * pair + 1):
                        out = bank[:, j, c0:HALF]
                        k = KT[:, head + j, kt * P:(kt + 1) * P]
                        q = QT[:, head + j, half * HALF + c0:(half + 1) * HALF]
                        diag = second and kt >= KPH * half
                        last = nc.tensor.matmul(out, k, q, start=True, stop=not diag)
                        if diag:
                            last = nc.tensor.matmul(out[:, 0:P], ident_b[:], masks[:, 1, :], start=False, stop=True)
                    last.then_inc(scored, 1)

                def pv_unit(G, u):
                    half, kt, c0 = units[u]
                    first, final = u == 0 or units[u - 1][0] != half, u == U - 1 or units[u + 1][0] != half
                    pe.wait_ge(exps, G * 2 * U + 2 * u + 2)
                    if first:
                        pe.wait_ge(y_kept, G * NV + half)
                    if u == 0:
                        pe.wait_ge(v_group, G + 1)
                    for j in range(GH):
                        last = nc.tensor.matmul(bank[VW * j:VW * (j + 1), 4, c0:HALF], Vg[:, kt, j, :], E[:, u % 2, j, c0:HALF],
                                                start=first, stop=final, tile_position=(0, VW * j))
                    last.then_inc(pv, 1)

                def turn_y(G, half):
                    pe.wait_ge(y_kept, G * NV + half + 1)
                    pe.wait_ge(y_normed, G * NV + half)
                    for i in range(KPH):
                        last = nc.tensor.transpose(bank[:, 7, i * P:(i + 1) * P], Ysb[:, half, i * P:(i + 1) * P], ident)
                    last.then_inc(y_turned, 1)

                def group(b, g, more):
                    G, head = b * NG + g, g * GH
                    pe.wait_ge(m_rows, (G + 1) * GH * 16)
                    def chunk_run(lo, hi):
                        if more:
                            max_chunks(G + 1, head + GH, lo, hi)

                    for u in range(U):
                        lo, hi = beside[u], beside[u + 1]
                        score_pair(G, head, u, 0)
                        chunk_run(lo, min(lo + 1, hi))
                        score_pair(G, head, u, 1)
                        chunk_run(lo + 1, min(lo + 2, hi))
                        if u:
                            pv_unit(G, u - 1)
                            if u > 2 and units[u - 2][0] != units[u - 3][0]:
                                turn_y(G, 0)
                        chunk_run(lo + 2, hi)
                        if more and u == U - 2:
                            turn_max(G + 1)
                    pv_unit(G, U - 1)
                    turn_y(G, 1)

                def turn_tile(b, i):
                    pe.wait_ge(normed, b * TPB + i + 1)
                    if i >= 4:
                        pe.wait_ge(xT_kept, b * (TPB // 2) + i // 2 - 1)
                    for k in range(KC):
                        last = nc.tensor.transpose(tile_bank(i)[:, k, i % 2, :], xn[:, i, k * P:(k + 1) * P], ident)
                    last.then_inc(turned, 1)

                def project(b, i):
                    pe.wait_ge(xT_kept, b * (TPB // 2) + i // 2 + 1)
                    pe.wait_ge(qk_kept, before(b, TPB, i - 1))
                    for k in range(KC):
                        nc.tensor.matmul(bank[:, 2 + i % 2, :], xT[:, k, i * P:(i + 1) * P], core.wqkvT[:, k, 0:2 * D],
                                         start=(k == 0), stop=(k == KC - 1))
                    pe.wait_ge(v_kept, before(b, TPB, i))
                    for k in range(KC):
                        last = nc.tensor.matmul(bank[:, 4, 0:D], xT[:, k, i * P:(i + 1) * P], core.wqkvT[:, k, 2 * D:3 * D],
                                                start=(k == 0), stop=(k == KC - 1))
                    last.then_inc(qkv, 1)

                def turn_ops(b, i):
                    pe.wait_ge(parts, b * TPB + i + 1)
                    for n in range(4):
                        pe.wait_ge(ops_dve, b * 3 * TPB + 3 * i + max(n - 1, 0))
                        if n == 1:
                            pe.wait_ge(ops_act, b * TPB + i)
                        for h in range(8):
                            last = nc.tensor.transpose(ops_bank(n)[0:W, h, :], A[:, i % 2, n // 2, (n % 2) * 8 + h, :], ident_b[:])
                        last.then_inc(ops_turned, 1)

                def turn_out(b, i):
                    pe.wait_ge(yT_kept, before(b, TPB, i - 1))
                    for k in range(KC):
                        last = nc.tensor.transpose(bank[:, i % 2, k * P:(k + 1) * P], y[:, i, k * P:(k + 1) * P], ident)
                    last.then_inc(out_turned, 1)

                def out_proj(b, i):
                    pe.wait_ge(yT_kept, b * TPB + i + 1)
                    pe.wait_ge(x_done, before(b, TPB, i - 1))
                    for k in range(KC):
                        last = nc.tensor.matmul(bank[:, 2 + i % 2, 0:D], yT[:, i % 2, k, :], core.woT[:, k, :],
                                                start=(k == 0), stop=(k == KC - 1))
                    last.then_inc(out_done, 1)

                pe.wait_ge(consts_b, 3 if second else 1)
                if second:
                    pe.wait_ge(w_in, 32)
                with pe.Fori(0, B) as b:
                    for i in range(4):
                        turn_tile(b, i)
                    project(b, 0)
                    project(b, 1)
                    for i in range(4, TPB):
                        turn_tile(b, i)
                    for i in range(TPB):
                        if i + 2 < TPB:
                            project(b, i + 2)
                        turn_ops(b, i)
                    pe.wait_ge(ops_dve, (b + 1) * 3 * TPB)
                    pe.wait_ge(ops_act, (b + 1) * TPB)
                    max_chunks(b * NG, 0, 0, C)
                    turn_max(b * NG)
                    for g in range(NG):
                        group(b, g, g + 1 < NG)
                    pe.wait_ge(y_normed, (b + 1) * NG * NV)
                    turn_out(b, 0)
                    for i in range(TPB):
                        if i + 1 < TPB:
                            turn_out(b, i + 1)
                        out_proj(b, i)

            @block.scalar
            def _(act):
                nc.scalar.activation(core.rstd[:], core.mv[:, :, 1], ACT.Sqrt, bias=core.eps[:, 0:1]).then_inc(root, 1)

                def take(b, i):
                    act.wait_ge(qkv, b * TPB + i + 1)
                    act.wait_ge(rested, before(b, 2 * TPB, 2 * (i - 1)))
                    nc.scalar.activation(V[:, i, :, :], bank[:, 4, 0:D].rearrange("p (h d) -> p h d", d=HD),
                                         ACT.Copy).then_inc(v_kept, 1)
                    pq = bank[:, 2 + i % 2, :].rearrange("p (h d) -> p h d", d=HD)
                    nc.scalar.activation(qk[:, i % 2, 0:NH, :], pq[:, 0:NH], ACT.Copy, scale=HD ** -0.5)
                    nc.scalar.activation(qk[:, i % 2, NH:2 * NH, :], pq[:, NH:2 * NH], ACT.Copy).then_inc(qk_kept, 1)

                def first_parts(b, i):
                    act.wait_ge(qk_kept if second else roped, b * TPB * (1 if second else 2) + (i + 1) * (1 if second else 2))
                    act.wait_ge(ops_turned, before(b, 4 * TPB, 4 * (i - 1)))
                    for q, slots in ((0, slice(0, 3)), (1, slice(1, 6, 2))):
                        dst = A[:, i % 2, q, :, 0:6 * HD].rearrange("p h (s d) -> p h s d", d=HD)[:, :, slots, :]
                        last = nc.scalar.activation(dst, spread(qk[:, i % 2, q * NH:(q + 1) * NH, :], 2, 3), ACT.Copy)
                    last.then_inc(part1, 1)

                def keep_ops(b, i):
                    act.wait_ge(ops_turned, b * 4 * TPB + 4 * i + 4)
                    nc.scalar.activation(KT[0:W, 8:16, i * P:(i + 1) * P], ops_bank(3)[0:W], ACT.Copy).then_inc(ops_act, 1)

                def exp_unit(G, u):
                    half, kt, c0 = units[u]
                    act.wait_ge(pv, G * U + max(u - 1, 0))
                    for pair in range(2):
                        act.wait_ge(scored, G * 2 * U + 2 * u + pair + 1)
                        nc.scalar.activation(E[:, u % 2, 2 * pair:2 * pair + 2, c0:HALF], bank[:, 2 * pair:2 * pair + 2, c0:HALF],
                                             ACT.Exp).then_inc(exps, 1)

                def keep_y(G, half):
                    done = sum(1 for h, _, _ in units if h <= half)
                    act.wait_ge(pv, G * U + done)
                    act.wait_ge(y_turned, G * NV + half)
                    nc.scalar.activation(Ysb[:, half, :], bank[:, 4, :], ACT.Copy).then_inc(y_kept, 1)

                def group(b, g):
                    for u in range(U):
                        exp_unit(b * NG + g, u)
                        if u and units[u][0] != units[u - 1][0]:
                            keep_y(b * NG + g, 0)
                    keep_y(b * NG + g, 1)

                with act.Fori(0, B) as b:
                    def keep_tiles(k):
                        act.wait_ge(turned, b * TPB + 2 * k + 2)
                        dst = xT[:, :, 2 * k * P:2 * (k + 1) * P].rearrange("p k (h c) -> p k h c", h=2)
                        nc.scalar.activation(dst, tile_bank(2 * k), ACT.Copy).then_inc(xT_kept, 1)

                    keep_tiles(0)
                    keep_tiles(1)
                    take(b, 0)
                    keep_tiles(2)
                    keep_tiles(3)
                    for i in range(TPB + 1):
                        if i + 1 < TPB:
                            take(b, i + 1)
                        if i < TPB:
                            first_parts(b, i)
                        if i:
                            keep_ops(b, i - 1)
                    for g in range(NG):
                        group(b, g)
                    for i in range(TPB):
                        act.wait_ge(out_turned, b * TPB + i + 1)
                        act.wait_ge(out_done, before(b, TPB, i - 1))
                        nc.scalar.activation(yT[:, i % 2], bank[:, i % 2, 0:D].rearrange("p (k c) -> p k c", k=KC),
                                             ACT.Copy).then_inc(yT_kept, 1)

            @block.vector
            def _(dve):
                dve.wait_ge(root, 1)
                nc.vector.reciprocal(core.rstd[:], core.rstd[:]).then_inc(scales, 1)
                nc.vector.memset(KT[96:WM, :, :], 1.0).then_inc(ones, 1)
                nc.vector.memset(Vg[:], 0.0).then_inc(ones, 1)
                dve.wait_ge(ones, 2)
                nc.vector.memset(Vg[:, :, :, HD:HD + 1], 1.0).then_inc(consts_b, 1)
                if second:
                    nc.vector.memset(mx[:], NEG)
                    nc.vector.tensor_copy(masks[:, 0, :], core.const("mask_qk"))
                    nc.vector.tensor_copy(masks[:, 1, :], core.const("mask_kq")).then_inc(consts_b, 1)
                    for s in range(2):
                        nc.vector.tensor_copy(A[:, s, 0, :, 6 * HD:W], core.const("slopes").rearrange("p (h s) -> p h s", h=NH))
                        last = nc.vector.tensor_copy(A[:, s, 1, :, 6 * HD + 3:W], spread(core.const("kpos"), 1, NH))
                    last.then_inc(consts_b, 1)
                dve.wait_ge(scales, 1)

                def second_parts(b, i):
                    if second:
                        nc.vector.tensor_copy(A[:, i % 2, 1, :, 6 * HD:6 * HD + 3],
                                              spread(core.const("kbase")[:, 3 * i:3 * i + 3], 1, NH))
                    for q, slots in ((0, slice(3, 5)), (1, slice(0, 5, 4))):
                        dve.wait_ge(rested, b * 2 * TPB + 2 * i + q + 1)
                        dst = A[:, i % 2, q, :, 0:6 * HD].rearrange("p h (s d) -> p h s d", d=HD)[:, :, slots, :]
                        last = nc.vector.tensor_copy(dst, spread(rest[:, q], 2, 2))
                    last.then_inc(part2, 1)

                def keep_ops(b, i):
                    for n in range(3):
                        dve.wait_ge(ops_turned, b * 4 * TPB + 4 * i + n + 1)
                        dst = (QT if n // 2 == 0 else KT)[0:W, (n % 2) * 8:(n % 2) * 8 + 8, i * P:(i + 1) * P]
                        nc.vector.tensor_copy(dst, ops_bank(n)[0:W]).then_inc(ops_dve, 1)

                def reduce_chunks(G, lo, hi):
                    for n in range(lo, min(hi, C)):
                        j, qt, kh, w = chunks[n]
                        dve.wait_ge(chunk_done, G * C + n + 1)
                        nc.vector.tensor_reduce(mx[:, j, qt, kh:kh + 1], bank[:, 5 + n % 2, 0:w], AX.X, ALU.max).then_inc(reduced, 1)

                def maxima(G):
                    dve.wait_ge(reduced, (G + 1) * C)
                    nc.vector.tensor_reduce(m[:], mx[:], AX.X, ALU.max).then_inc(m_step, 1)
                    dve.wait_ge(m_step, G * 4 + 1)
                    nc.vector.tensor_scalar(mparts[:, :, 0, :], m[:], -1.0, None, ALU.mult).then_inc(m_step, 1)
                    dve.wait_ge(m_step, G * 4 + 2)
                    nc.vector.scalar_tensor_tensor(out=mrest[:], in0=m[:], scalar=-1.0, in1=mparts[:, :, 0, :],
                                                   op0=ALU.mult, op1=ALU.subtract).then_inc(m_step, 1)
                    dve.wait_ge(m_step, G * 4 + 3)
                    nc.vector.tensor_copy(mparts[:, :, 1, :], mrest[:]).then_inc(ones, 1)
                    dve.wait_ge(ones, 2 + G + 1)
                    nc.vector.tensor_tensor(mparts[:, :, 2, :], mrest[:], mparts[:, :, 1, :], ALU.subtract).then_inc(m_step, 1)

                def keep_max(G):
                    dve.wait_ge(m_turned, G + 1)
                    dve.wait_ge(m_rows, G * GH * 16)
                    nc.vector.tensor_copy(mT[:], bank[0:GH * 3 * TPB, 5, :].bitcast(BF16)[:, 0:P]).then_inc(mT_kept, 1)

                def norm_y(G, g, half):
                    z = bank[:, 7, :].rearrange("p (i j v) -> p i j v", i=KPH, j=GH)
                    dve.wait_ge(y_turned, G * NV + half + 1)
                    dve.wait_ge(y_normed, G * NV + half)
                    nc.vector.reciprocal(rden[:], z[:, :, :, HD]).then_inc(y_step, 1)
                    dve.wait_ge(y_step, G * NV + half + 1)
                    dst = y[:, half * KPH:(half + 1) * KPH, bass.ds(g * GH * HD, GH * HD)].rearrange("p i (j d) -> p i j d", d=HD)
                    nc.vector.tensor_tensor(dst, z[:, :, :, 0:HD], spread(rden[:], 3, HD), ALU.mult).then_inc(y_normed, 1)

                def group(b, g, more):
                    G = b * NG + g
                    for u in range(U):
                        if u > 2 and units[u - 2][0] != units[u - 3][0]:
                            norm_y(G, g, 0)
                        if more:
                            if u == U - 2:
                                maxima(G + 1)
                                keep_max(G + 1)
                            reduce_chunks(G + 1, beside[u], beside[u + 1])
                    norm_y(G, g, 1)

                with dve.Fori(0, B) as b:
                    for i in range(TPB):
                        t = b * TPB + i
                        dve.wait_ge(out_turned, b * TPB)
                        nc.vector.tensor_scalar(xn[:, i, :], at(core.x, t), at(core.mv, t)[:, 0:1], col(core.rstd, t),
                                                ALU.subtract, ALU.mult).then_inc(normed, 1)
                    for i in range(TPB + 1):
                        if i:
                            keep_ops(b, i - 1)
                        if i < TPB:
                            second_parts(b, i)
                    reduce_chunks(b * NG, 0, C)
                    maxima(b * NG)
                    keep_max(b * NG)
                    for g in range(NG):
                        group(b, g, g + 1 < NG)
                    for i in range(TPB):
                        t = b * TPB + i
                        dve.wait_ge(out_done, t + 1)
                        nc.vector.tensor_tensor(at(core.x, t), bank[:, 2 + i % 2, 0:D], at(core.x, t), ALU.add).then_inc(x_done, 1)
                    for i in range(TPB):
                        dve.wait_ge(scales, 1)
                        dve.wait_ge(x_done, b * TPB + i + 1)
                        nc.vector.bn_stats(bn8[:, i, :], at(core.x, b * TPB + i)).then_inc(stats, 1)
                    dve.wait_ge(stats, (b + 1) * TPB)
                    nc.vector.memset(carrier[:], 0.0)
                    for i in range(TPB):
                        last = nc.vector.bn_aggr(mv8[:, i, :], bn8[:, i, :])
                    last.then_inc(aggregated, 1)
                    dve.wait_ge(aggregated, b + 1)
                    nc.vector.tensor_copy(core.mv[:, bass.ds(b * TPB, TPB), :], mv8[:])


def at(tensor, t):
    return tensor[:, t] if isinstance(t, int) else tensor[:, bass.ds(t, 1)].rearrange("p a d -> p (a d)")


def col(tensor, t):
    return tensor[:, t:t + 1] if isinstance(t, int) else tensor[:, bass.ds(t, 1)]


OUT_SHAPE = (NTOK + TRASH, D)


def store_phase(core):
    nc = core.nc
    with ExitStack() as ctx:
        _, _, sem = scope(core, ctx)
        stored = sem("stored")
        with nc.Block() as block:
            @block.sync
            def _(sp):
                sp.dma_start(core.dram["out"][0:NTOK, :].rearrange("(t p) d -> p t d", p=P), core.x[:]).then_inc(stored, 16)
                sp.wait_ge(stored, 16)


PHASES = ("prep", "ffn0", "attn0", "ffn0", "moe1", "attn1", "moe2")


def program(nc, dram, phases=PHASES):
    nc.disable_value_cache = True
    with ExitStack() as ctx:
        ctx.enter_context(nc.allow_non_contiguous_dma(reason="per-channel scales, once"))
        core = Core(nc, ctx, dram)
        dram["xn"] = nc.dram_tensor("normalised", (NTOK + TRASH, D), F32, kind="Internal").ap()
        dram["table"] = nc.dram_tensor("table", (NE * CAP, 2), I32, kind="Internal").ap()
        dram["acc"] = nc.dram_tensor("acc", (NTOK + TRASH, D), F32, kind="Internal").ap()
        for n, name in enumerate(phases):
            if name == "prep":
                prepare_phase(core)
            elif name == "ffn0":
                ffn0_phase(core, f"f{n}_")
            elif name in ("attn0", "attn1"):
                attention_phase(core, f"a{n}_", name == "attn1")
            elif name == "moe1":
                mixture_dense_phase(core, f"d{n}_", dram["acc"], True)
                experts_phase(core, f"e{n}_", dram["acc"])
                reload_phase(core, f"r{n}_", dram["acc"])
                core.clear_semaphores()
            elif name == "moe2":
                mixture_dense_phase(core, f"d{n}_", dram["out"], False)
                experts_phase(core, f"e{n}_", dram["out"])
            elif name == "store":
                store_phase(core)


_INS = ['L0_attn_x', 'L0_attn_wq', 'L0_attn_wk', 'L0_attn_wv', 'L0_attn_wo', 'L0_ffn_wq_gate', 'L0_ffn_s_gate',
        'L0_ffn_wq_up', 'L0_ffn_s_up', 'L0_ffn_wq_down', 'L0_ffn_s_down', 'L1_attn_W_qkv', 'L1_attn_W_o',
        'L1_ffn_w_norm', 'L1_ffn_w_router', 'L1_ffn_w_gate', 'L1_ffn_w_up', 'L1_ffn_w_down', 'L1_ffn_sw_gate',
        'L1_ffn_sw_up', 'L1_ffn_sw_down', 'L1_ffn_w_shared_gate']


def kernel(**inputs):
    import concourse.bacc as _bacc
    from concourse.bass_utils import run_bass_kernel_spmd as _run

    nc = _bacc.Bacc("TRN2", target_bir_lowering=False, num_devices=1)
    arrays, dram = {}, {}
    for name in _INS:
        arrays[f"in_{name}"] = np.ascontiguousarray(inputs[name])
    arrays["in_consts"] = constants()
    for name, a in arrays.items():
        dram[name[3:]] = nc.dram_tensor(name, a.shape, mybir.dt.from_np(a.dtype), kind="ExternalInput").ap()
    dram["out"] = nc.dram_tensor("out_0", OUT_SHAPE, F32, kind="ExternalOutput").ap()
    program(nc, dram)
    r = _run(nc, [arrays], core_ids=[0])
    return r.results[0]["out_0"][:NTOK].reshape(B, T, D)
```

```python
from contextlib import ExitStack

import concourse.bass as bass
from concourse import mybir
import numpy as np

F32 = mybir.dt.float32
BF16 = mybir.dt.bfloat16
F16 = mybir.dt.float16
I32 = mybir.dt.int32
U32 = mybir.dt.uint32
ALU = mybir.AluOpType
ACT = mybir.ActivationFunctionType
AX = mybir.AxisListType

P = 128
B, T, D = 4, 1024, 256
NTOK = B * T
NT = NTOK // P
TPB = T // P
KC = D // P
NH, HD = 16, 16
FF = 704
FB = -(-FF // P)
NE, TOPK, CAP, EF = 32, 4, 128, 176
EH = EF // 2
DEEP = 4
CT = 4
NCH = NT // CT
CW = CT * P
SUMS = 16
TRASH = P
ZERO_POINT = 128.0
LN_EPS, RMS_EPS = 1e-5, 1e-6
NEG = -1e30
VW = 32
ROPE = HD // 2
LIFT = 1024.0
START = 1

CONST = {}
_at = 0
for _name, _w in (("ident", P), ("tri", P), ("mask_qk", P), ("mask_kq", P), ("expert", NE), ("token", NT),
                  ("slopes", NH * 6), ("kbase", TPB * 3), ("kpos", 3), ("rope", TPB * 2 * ROPE), ("slot", NE)):
    CONST[_name] = (_at, _at + _w)
    _at += _w
NCONST = _at


def hid(j):
    return min(P, FF - j * P)


def constants():
    c = np.zeros((P, NCONST), np.float32)
    p = np.arange(P)

    def put(name, a):
        lo, hi = CONST[name]
        c[:, lo:hi] = a.reshape(P, hi - lo)

    put("ident", np.eye(P))
    put("tri", (p[:, None] < p[None, :]) * 1.0)
    put("mask_qk", np.where(p[None, :] > p[:, None], NEG, 0.0))
    put("mask_kq", np.where(p[:, None] > p[None, :], NEG, 0.0))
    put("expert", np.tile(np.arange(NE), (P, 1)))
    put("token", p[:, None] + P * np.arange(NT)[None, :])
    put("slot", NTOK + np.tile(p[:, None], (1, NE)))
    slopes = (2.0 ** (-8.0 / np.arange(1, NH + 1, dtype=np.float32))).astype(np.float32)
    parts, rest = [], slopes.copy()
    for _ in range(3):
        part = (rest.view(np.uint32) & np.uint32(0xFFFF0000)).view(np.float32)
        parts.append(part)
        rest = rest - part
    put("slopes", np.tile(np.stack(parts + parts, 1).reshape(-1), (P, 1)))
    put("kbase", np.tile(np.repeat(P * (np.arange(TPB) - TPB // 2), 3), (P, 1)))
    put("kpos", np.tile(p[:, None], (1, 3)))
    inv = (1.0 / 10000.0 ** (np.arange(0, HD, 2, dtype=np.float32) / np.float32(HD))).astype(np.float32)
    ang = (np.arange(T, dtype=np.float32)[:, None] * inv[None, :]).astype(np.float32)
    sin = np.sin(ang)
    sin[:, :ROPE // 2] *= -1
    tab = np.concatenate([np.cos(ang), sin], 1).astype(np.float32)
    put("rope", tab.reshape(TPB, P, 2 * ROPE).transpose(1, 0, 2))
    return c


class Core:

    def __init__(self, nc, ctx, dram):
        self.nc, self.dram, self.sems = nc, dram, []

        def sb(name, shape, dt=F32):
            return ctx.enter_context(nc.sbuf_tensor(name, shape, dt))

        self.x = sb("x", [P, NT, D])
        self.mv = sb("mv", [P, NT, 2])
        self.rstd = sb("rstd", [P, NT])
        self.consts = sb("consts", [P, NCONST])
        self.ident_b = sb("ident_b", [P, P], BF16)
        self.eps = sb("eps", [P, 2])
        self.wgT = sb("wgT", [P, KC, FF])
        self.wuT = sb("wuT", [P, KC, FF])
        self.wdT = sb("wdT", [P, FB, D])
        self.cgT = self.wgT[:].bitcast(F16)[:, :, 0:FF]
        self.cuT = self.wuT[:].bitcast(F16)[:, :, 0:FF]
        self.hscale = sb("hscale", [P, FB, 2])
        self.wqkvT = sb("wqkvT", [P, KC, 3 * D])
        self.woT = sb("woT", [P, KC, D])

    def clear_semaphores(self):
        self.nc.clear_and_free_semaphores(self.sems)
        self.nc.all_engine_barrier()
        self.sems = []

    def const(self, name):
        lo, hi = CONST[name]
        return self.consts[:, lo:hi]


def scope(core, ctx):
    nc = core.nc

    def sb(name, shape, dt=F32):
        return ctx.enter_context(nc.sbuf_tensor(name, shape, dt))

    def ps(name, shape, dt=F32):
        return ctx.enter_context(nc.psum_tensor(name, shape, dt))

    def sem(name, start=START):
        semaphore = nc.alloc_semaphore(name=name)
        if start:
            nc.sync.sem_inc(semaphore, start)
        core.sems.append(semaphore)
        return semaphore

    return sb, ps, sem


def prepare_phase(core):
    nc, dram = core.nc, core.dram
    with ExitStack() as ctx:
        sb, ps, sem = scope(core, ctx)
        qg = sb("p_qg", [P, FB, D], I32)
        qu = sb("p_qu", [P, FB, D], I32)
        qd = sb("p_qd", [P, KC, FF], I32)
        sg = sb("p_sg", [P, FB])
        su = sb("p_su", [P, FB])
        sd = sb("p_sd", [P, KC])
        wn = sb("p_wn", [P, 4, KC, D])
        fg = sb("p_fg", [P, FB, D])
        fu = sb("p_fu", [P, FB, D])
        fd = sb("p_fd", [P, KC, FF])
        bn = sb("p_bn", [P, NT, 6])
        tp = [ps(f"p_tp{i}", [P, 4, P]) for i in range(4)]
        c_in, q_in, s_in, w_in, x_in = sem("p_c_in"), sem("p_q_in"), sem("p_s_in", 0), sem("p_w_in"), sem("p_x_in")
        deq, turned, kept, stat = sem("p_deq"), sem("p_turned"), sem("p_kept"), sem("p_stat")

        jobs = []
        for q, (src, dst) in enumerate(((fg, core.cgT), (fu, core.cuT))):
            for kc in range(KC):
                for j in range(FB):
                    jobs.append((src[0:hid(j), j, kc * P:(kc + 1) * P], hid(j), P,
                                 dst[:, kc, j * P:j * P + hid(j)]))
        for j in range(FB):
            for kc in range(KC):
                jobs.append((fd[:, kc, j * P:j * P + hid(j)], P, hid(j), core.wdT[0:hid(j), j, kc * P:(kc + 1) * P]))
        nq = len(jobs)
        for w in range(4):
            dst = core.wqkvT if w < 3 else core.woT
            off = w * D if w < 3 else 0
            for kc in range(KC):
                for m in range(KC):
                    jobs.append((wn[:, w, m, kc * P:(kc + 1) * P], P, P,
                                 dst[:, kc, off + m * P:off + (m + 1) * P]))
        assert len(jobs) % 4 == 0

        nc.all_engine_barrier()
        with nc.Block() as block:
            @block.sync
            def _(sp):
                sp.dma_start(core.consts[:], dram["consts"]).then_inc(c_in, 16)
                for q, s, a, b in (("L0_ffn_wq_gate", "L0_ffn_s_gate", qg, sg), ("L0_ffn_wq_up", "L0_ffn_s_up", qu, su)):
                    full = (FB - 1) * P
                    sp.dma_start(a[:, 0:FB - 1, :], dram[q][0:full, :].rearrange("(j p) d -> p j d", p=P)).then_inc(q_in, 16)
                    sp.dma_start(a[0:hid(FB - 1), FB - 1, :], dram[q][full:FF, :]).then_inc(q_in, 16)
                sp.dma_start(qd[:], dram["L0_ffn_wq_down"].rearrange("(k p) f -> p k f", p=P)).then_inc(q_in, 16)
                for w, name in enumerate(("L0_attn_wq", "L0_attn_wk", "L0_attn_wv", "L0_attn_wo")):
                    sp.dma_start(wn[:, w], dram[name].rearrange("(m p) d -> p m d", p=P)).then_inc(w_in, 16)

            @block.gpsimd
            def _(pool):
                full = (FB - 1) * P
                for s, b in (("L0_ffn_s_gate", sg), ("L0_ffn_s_up", su)):
                    v = dram[s].rearrange("(f a) -> f a", a=1)
                    pool.dma_start(b[:, 0:FB - 1].rearrange("p (j a) -> p j a", a=1),
                                   v[0:full].rearrange("(j p) a -> p j a", p=P)).then_inc(s_in, 16)
                    pool.dma_start(b[0:hid(FB - 1), FB - 1:FB], v[full:FF]).then_inc(s_in, 16)
                pool.dma_start(sd[:].rearrange("p (k a) -> p k a", a=1),
                               dram["L0_ffn_s_down"].rearrange("(k p a) -> p k a", p=P, a=1)).then_inc(s_in, 16)

            @block.scalar
            def _(act):
                for b in range(B):
                    act.dma_start(core.x[:, b * TPB:(b + 1) * TPB, :],
                                  dram["L0_attn_x"][b].rearrange("(i p) d -> p i d", p=P)).then_inc(x_in, 16)
                for n in range(1, len(jobs) // 4, 2):
                    act.wait_ge(turned, START + n + 1)
                    for i in range(4):
                        _, rows, cols, dst = jobs[4 * n + i]
                        last = nc.scalar.activation(dst, tp[n % 4][0:cols, i, 0:rows], ACT.Copy)
                    last.then_inc(kept, 1)

            @block.vector
            def _(dve):
                nc.vector.memset(core.eps[:, 0:1], LN_EPS)
                nc.vector.memset(core.eps[:, 1:2], RMS_EPS)
                dve.wait_ge(c_in, START + 16)
                nc.vector.tensor_copy(core.ident_b[:], core.const("ident"))
                dve.wait_ge(q_in, START + 16 * 5)
                dve.wait_ge(s_in, 16 * 5)
                for q, f in ((qg, fg), (qu, fu)):
                    for j in range(FB):
                        r = hid(j)
                        nc.vector.tensor_scalar(f[0:r, j, :], q[0:r, j, :], ZERO_POINT, None, ALU.subtract).then_inc(deq, 1)
                for r, j in ((P, slice(0, FB - 1)), (hid(FB - 1), slice(FB - 1, FB))):
                    nc.vector.tensor_scalar(core.hscale[0:r, j, 0], sg[0:r, j], 0.5 / LIFT, None, ALU.mult)
                    nc.vector.scalar_tensor_tensor(out=core.hscale[0:r, j, 1], in0=sg[0:r, j], scalar=1.0 / LIFT ** 2,
                                                   in1=su[0:r, j], op0=ALU.mult, op1=ALU.mult)
                for k in range(KC):
                    nc.vector.tensor_scalar(fd[:, k, :], qd[:, k, :], ZERO_POINT, sd[:, k:k + 1],
                                            ALU.subtract, ALU.mult).then_inc(deq, 1)
                for n in range(0, len(jobs) // 4, 2):
                    dve.wait_ge(turned, START + n + 1)
                    for i in range(4):
                        _, rows, cols, dst = jobs[4 * n + i]
                        last = nc.vector.tensor_copy(dst, tp[n % 4][0:cols, i, 0:rows])
                    last.then_inc(stat, 1)
                for t in range(NT):
                    if t % TPB == 0:
                        dve.wait_ge(x_in, START + 16 * B)
                    nc.vector.bn_stats(bn[:, t, :], core.x[:, t, :]).then_inc(deq, 1)
                for t in range(NT):
                    dve.wait_ge(deq, START + 2 * FB + KC + t + 1)
                    nc.vector.bn_aggr(core.mv[:, t, :], bn[:, t, :])

            @block.tensor
            def _(pe):
                pe.wait_ge(c_in, START + 16)
                for n in range(len(jobs) // 4):
                    if 4 * n < nq:
                        pe.wait_ge(deq, START + 2 * FB + KC)
                    else:
                        pe.wait_ge(w_in, START + 16 * 4)
                    if n >= 4:
                        k = n - 4
                        pe.wait_ge(stat if k % 2 == 0 else kept, START + k // 2 + 1)
                    for i in range(4):
                        src, rows, cols, _ = jobs[4 * n + i]
                        last = nc.tensor.transpose(tp[n % 4][0:cols, i, 0:rows], src, core.const("ident")[0:rows, 0:rows])
                    last.then_inc(turned, 1)


def ffn0_phase(core, tag):
    nc = core.nc
    with ExitStack() as ctx:
        sb, ps, sem = scope(core, ctx)
        xn = sb(tag + "xn", [P, CT, D])
        xh = sb(tag + "xh", [P, 2, KC, CW], F16)
        xl = sb(tag + "xl", [P, 2, KC, CW], F16)
        silu = sb(tag + "silu", [P, 2, CW])
        silu2 = sb(tag + "silu2", [P, 2, CW])
        silu2_s = sem(tag + "silu2")
        hT = sb(tag + "hT", [P, FB, CW])
        bn = sb(tag + "bn", [P, CT, 6])
        mv4 = sb(tag + "mv4", [P, CT, 2])
        sums = sb(tag + "sums", [P, CT, SUMS])
        mean = sb(tag + "mean", [P, CT])
        meaned = sem(tag + "meaned")
        tp = ps(tag + "tp", [P, 2, KC, 2 * P])
        gate = ps(tag + "gate", [P, 2, CW])
        up = ps(tag + "up", [P, 2, CW])
        down = ps(tag + "down", [P, 2, 512])
        root, scales = sem(tag + "root"), sem(tag + "scales")
        normed, turned, xh_ready, xT_ready = (sem(tag + n) for n in ("normed", "turned", "xh_ready", "xT_ready"))
        gu_ready, silu_ready, h_ready = sem(tag + "gu"), sem(tag + "silu_s"), sem(tag + "h")
        down_ready, x_done, stats = sem(tag + "down_s"), sem(tag + "x_done"), sem(tag + "stats")
        ident = core.const("ident")

        nc.all_engine_barrier()
        with nc.Block() as block:
            @block.tensor
            def _(pe):
                def turn(c):
                    for i in range(CT):
                        pe.wait_ge(normed, START + c * CT + i + 1)
                        if i % 2 == 0:
                            if not (isinstance(c, int) and c == 0):
                                pe.wait_ge(xT_ready, START + (c - 1) * 2 + i // 2 + 1)
                        for k in range(KC):
                            last = nc.tensor.transpose(tp[:, i // 2, k, (i % 2) * P:(i % 2 + 1) * P],
                                                       xn[:, i, k * P:(k + 1) * P], ident)
                        last.then_inc(turned, 1)

                def gate_up(c, s):
                    pe.wait_ge(xT_ready, START + c * 2 + 2)
                    for j in range(FB):
                        r = hid(j)
                        pe.wait_ge(h_ready, START + c * FB + j - 1) if j else pe.wait_ge(h_ready, START + c * FB)
                        for w, acc in ((core.cgT, gate), (core.cuT, up)):
                            for k in range(KC):
                                for part in (xh, xl):
                                    last = nc.tensor.matmul(acc[0:r, j % 2, :], w[:, k, j * P:j * P + r], part[:, s, k, :],
                                                            start=(k == 0 and part is xh), stop=(k == KC - 1 and part is xl))
                        last.then_inc(gu_ready, 1)

                def down_proj(c):
                    for i in range(CT):
                        if i >= 2:
                            pe.wait_ge(x_done, START + c * CT + i - 1)
                        else:
                            pe.wait_ge(x_done, START + c * CT)
                        for j in range(FB):
                            r = hid(j)
                            if i == 0:
                                pe.wait_ge(h_ready, START + c * FB + j + 1)
                            last = nc.tensor.matmul(down[:, i % 2, 0:D], hT[0:r, j, i * P:(i + 1) * P],
                                                    core.wdT[0:r, j, :], start=(j == 0), stop=(j == FB - 1))
                        last.then_inc(down_ready, 1)

                turn(0)
                with pe.Fori(0, NCH // 2 - 1) as it:
                    for s in range(2):
                        c = it * 2 + s
                        gate_up(c, s)
                        turn(c + 1)
                        down_proj(c)
                gate_up(NCH - 2, 0)
                turn(NCH - 1)
                down_proj(NCH - 2)
                gate_up(NCH - 1, 1)
                down_proj(NCH - 1)

            @block.scalar
            def _(act):
                nc.scalar.activation(core.rstd[:], core.mv[:, :, 1], ACT.Sqrt, bias=core.eps[:, 0:1]).then_inc(root, 1)

                def keep_xT(c, s):
                    for b in range(2):
                        act.wait_ge(turned, START + c * CT + 2 * b + 2)
                        nc.scalar.activation(xh[:, s, :, b * 2 * P:(b + 1) * 2 * P], tp[:, b], ACT.Copy).then_inc(xh_ready, 1)

                def silus(c):
                    for j in range(FB):
                        r = hid(j)
                        act.wait_ge(gu_ready, START + c * FB + j + 1)
                        act.wait_ge(h_ready, START + c * FB + max(j - 1, 0))
                        nc.scalar.activation(silu[0:r, j % 2, :], gate[0:r, j % 2, :], ACT.Tanh,
                                             scale=core.hscale[0:r, j, 0:1]).then_inc(silu_ready, 1)

                keep_xT(0, 0)
                with act.Fori(0, NCH // 2 - 1) as it:
                    for s in range(2):
                        c = it * 2 + s
                        silus(c)
                        keep_xT(c + 1, 1 - s)
                silus(NCH - 2)
                keep_xT(NCH - 1, 1)
                silus(NCH - 1)

            @block.vector
            def _(dve):
                dve.wait_ge(root, START + 1)
                nc.vector.reciprocal(core.rstd[:], core.rstd[:]).then_inc(scales, 1)
                dve.wait_ge(scales, START + 1)
                nc.vector.tensor_scalar(core.rstd[:], core.rstd[:], LIFT, None, ALU.mult).then_inc(scales, 1)
                dve.wait_ge(scales, START + 2)

                def means(c):
                    dve.wait_ge(normed, START + c * CT)
                    own = core.x[:, bass.ds(c * CT, CT), :].rearrange("p i (a d) -> p i a d", a=SUMS)
                    nc.vector.tensor_reduce(sums[:], own, AX.X, ALU.add).then_inc(meaned, 1)
                    dve.wait_ge(meaned, START + c * 3 + 1)
                    nc.vector.tensor_reduce(mean[:], sums[:], AX.X, ALU.add).then_inc(meaned, 1)
                    dve.wait_ge(meaned, START + c * 3 + 2)
                    nc.vector.tensor_scalar(mean[:], mean[:], 1.0 / D, None, ALU.mult).then_inc(meaned, 1)

                def normalise(c, i):
                    t = c * CT + i
                    if not (isinstance(c, int) and c == 0):
                        dve.wait_ge(turned, START + (c - 1) * CT + i + 1)
                    dve.wait_ge(meaned, START + (c + 1) * 3)
                    nc.vector.tensor_scalar(xn[:, i, :], at(core.x, t), mean[:, i:i + 1],
                                            col(core.rstd, t), ALU.subtract, ALU.mult).then_inc(normed, 1)

                def hidden(c, j):
                    r = hid(j)
                    dve.wait_ge(silu_ready, START + c * FB + j + 1)
                    if j == 0:
                        dve.wait_ge(down_ready, START + c * CT)
                    nc.vector.scalar_tensor_tensor(out=silu2[0:r, j % 2, :], in0=silu[0:r, j % 2, :], scalar=1.0,
                                                   in1=gate[0:r, j % 2, :], op0=ALU.add, op1=ALU.mult).then_inc(silu2_s, 1)
                    dve.wait_ge(silu2_s, START + c * FB + j + 1)
                    nc.vector.scalar_tensor_tensor(out=hT[0:r, j, :], in0=silu2[0:r, j % 2, :], scalar=core.hscale[0:r, j, 1:2],
                                                   in1=up[0:r, j % 2, :], op0=ALU.mult, op1=ALU.mult).then_inc(h_ready, 1)

                def lower_parts(c, s):
                    for b in range(2):
                        dve.wait_ge(xh_ready, START + c * 2 + b + 1)
                        cols = slice(b * 2 * P, (b + 1) * 2 * P)
                        nc.vector.tensor_tensor(xl[:, s, :, cols], tp[:, b], xh[:, s, :, cols], ALU.subtract).then_inc(xT_ready, 1)

                def residual(c, ahead):
                    seen = 0
                    for i in range(CT):
                        t = c * CT + i
                        dve.wait_ge(down_ready, START + t + 1)
                        if i:
                            dve.wait_ge(stats, START + c * 2 * CT + seen)
                        nc.vector.scalar_tensor_tensor(out=at(core.x, t), in0=down[:, i % 2, 0:D], scalar=0.25,
                                                       in1=at(core.x, t), op0=ALU.mult, op1=ALU.add).then_inc(x_done, 1)
                        if i:
                            nc.vector.bn_aggr(mv4[:, i - 1, :], bn[:, i - 1, :]).then_inc(stats, 1)
                            seen += 1
                        dve.wait_ge(scales, START + 1)
                        dve.wait_ge(x_done, START + t + 1)
                        nc.vector.bn_stats(bn[:, i, :], at(core.x, t)).then_inc(stats, 1)
                        seen += 1
                        if ahead:
                            normalise(c + 2, i)
                    dve.wait_ge(stats, START + c * 2 * CT + seen)
                    nc.vector.tensor_copy(core.mv[:, bass.ds(c * CT, CT - 1), :], mv4[:, 0:CT - 1, :])
                    nc.vector.bn_aggr(mv4[:, CT - 1, :], bn[:, CT - 1, :]).then_inc(stats, 1)
                    dve.wait_ge(stats, START + (c + 1) * 2 * CT)
                    nc.vector.tensor_copy(at(core.mv, c * CT + CT - 1), mv4[:, CT - 1, :])

                def chunk(c, s, ahead):
                    for j in range(FB):
                        hidden(c, j)
                    if ahead:
                        lower_parts(c + 1, 1 - s)
                    if ahead > 1:
                        means(c + 2)
                    residual(c, ahead > 1)

                means(0)
                for i in range(CT):
                    normalise(0, i)
                means(1)
                lower_parts(0, 0)
                for i in range(CT):
                    normalise(1, i)
                with dve.Fori(0, NCH // 2 - 1) as it:
                    for s in range(2):
                        chunk(it * 2 + s, s, 2)
                chunk(NCH - 2, 0, 1)
                chunk(NCH - 1, 1, 0)


def mixture_dense_phase(core, tag, acc, load):
    nc, dram = core.nc, core.dram
    NR = NE + 1
    with ExitStack() as ctx:
        sb, ps, sem = scope(core, ctx)
        xn = sb(tag + "xn", [P, CT, D])
        xT = sb(tag + "xT", [P, 2, KC, CW])
        silu = sb(tag + "silu", [P, 2, CW])
        silu2 = sb(tag + "silu2", [P, 2, CW])
        silu2_s = sem(tag + "silu2")
        hT = sb(tag + "hT", [P, FB, CW])
        wn = sb(tag + "wn", [P, KC])
        wr = sb(tag + "wr", [P, KC, NR])
        both = sb(tag + "both", [P, NT])
        keep = sb(tag + "keep", [P, NT])
        shift = sb(tag + "shift", [P, NT])
        tmp = sb(tag + "tmp", [P, NT])
        zero = sb(tag + "zero", [P, D])
        empty = sb(tag + "empty", [P, NE, 2], I32)
        tri = sb(tag + "tri", [P, P], BF16)
        ones = sb(tag + "ones", [P, P], BF16)
        lg = sb(tag + "lg", [P, CT, NR])
        lmax = sb(tag + "lmax", [P, CT])
        prob = sb(tag + "prob", [P, CT, NE])
        psum_ = sb(tag + "psum", [P, CT])
        hgate = sb(tag + "hgate", [P, CT])
        top = sb(tag + "top", [P, CT, 8])
        topi = sb(tag + "topi", [P, CT, 8], U32)
        topf = sb(tag + "topf", [P, CT, TOPK])
        hot = sb(tag + "hot", [P, CT, TOPK, NE])
        hotr = sb(tag + "hotr", [P, CT, TOPK, NE])
        count = sb(tag + "count", [P, CT, NE])
        mask = sb(tag + "mask", [P, CT, NE], BF16)
        before_ = sb(tag + "before", [P, CT + 1, NE], BF16)
        pos = sb(tag + "pos", [P, CT, TOPK])
        over = sb(tag + "over", [P, CT, TOPK])
        dest = sb(tag + "dest", [P, CT, TOPK], I32)
        entry = sb(tag + "entry", [P, CT, TOPK, 2], I32)
        tp = ps(tag + "tp", [P, 2, KC, 2 * P])
        gate = ps(tag + "gate", [P, 2, CW])
        up = ps(tag + "up", [P, 2, CW])
        down = ps(tag + "down", [P, 2, 512])
        logits = down[:, 0, D:D + CT * NR].rearrange("p (i e) -> p i e", i=CT)
        ranks = down[:, 1, D:D + CT * NE].rearrange("p (i e) -> p i e", i=CT)
        names = ("w_in root1 root2 scales setup tables normed xn_sent turned xT_ready logit_s gu silu_s h_s down_s x_done "
                 "acc_sent shifted exp_s route masked ranked dest_ready placed lg_kept ranks_used gated posted")
        (w_in, root1, root2, scales, setup, tables, normed, xn_sent, turned, xT_ready, logit_s, gu_ready, silu_ready,
         h_ready, down_ready, x_done, acc_sent, shifted, exp_s, route, masked, ranked, dest_ready,
         placed, lg_kept, ranks_used, gated, posted) = (sem(tag + n, 0 if n == "placed" else START) for n in names.split())
        ident = core.const("ident")
        STEPS = 15

        nc.all_engine_barrier()
        with nc.Block() as block:
            @block.sync
            def _(sp):
                full = (FB - 1) * P
                if load:
                    sp.dma_start(core.wgT[:], dram["L1_ffn_sw_gate"].rearrange("(k p) f -> p k f", p=P)).then_inc(w_in, 16)
                    sp.dma_start(core.wuT[:], dram["L1_ffn_sw_up"].rearrange("(k p) f -> p k f", p=P)).then_inc(w_in, 16)
                    sp.dma_start(core.wdT[:, 0:FB - 1, :], dram["L1_ffn_sw_down"][0:full].rearrange("(j p) d -> p j d", p=P)).then_inc(w_in, 16)
                    sp.dma_start(core.wdT[0:hid(FB - 1), FB - 1, :], dram["L1_ffn_sw_down"][full:FF]).then_inc(w_in, 16)
                sp.dma_start(wr[:, :, 0:NE], dram["L1_ffn_w_router"].rearrange("(k p) e -> p k e", p=P)).then_inc(w_in, 16)
                sp.dma_start(wr[:, :, NE:NR], dram["L1_ffn_w_shared_gate"].rearrange("(k p) e -> p k e", p=P)).then_inc(w_in, 16)
                sp.dma_start(wn[:].rearrange("p (k a) -> p k a", a=1),
                             dram["L1_ffn_w_norm"].rearrange("(k p a) -> p k a", p=P, a=1)).then_inc(w_in, 16)
                sp.wait_ge(setup, START + 1)
                sp.dma_start(dram["xn"][NTOK:NTOK + TRASH, :], zero[:]).then_inc(tables, 16)
                sp.dma_start(acc[NTOK:NTOK + TRASH, :], zero[:]).then_inc(tables, 16)
                sp.dma_start(dram["table"].rearrange("(e s) w -> s e w", e=NE), empty[:]).then_inc(tables, 16)

                def send_xn(c):
                    sp.wait_ge(normed, START + (c + 1) * CT)
                    sp.dma_start(dram["xn"][bass.ds(c * CW, CW), :].rearrange("(i p) d -> p i d", p=P), xn[:]).then_inc(xn_sent, 16)

                def send_x(c):
                    sp.wait_ge(x_done, START + (c + 1) * CT)
                    sp.dma_start(acc[bass.ds(c * CW, CW), :].rearrange("(i p) d -> p i d", p=P),
                                 core.x[:, bass.ds(c * CT, CT), :]).then_inc(acc_sent, 16)

                send_xn(0)
                with sp.Fori(0, NCH - 1) as c:
                    send_xn(c + 1)
                    send_x(c)
                send_x(NCH - 1)
                sp.wait_ge(xn_sent, START + 16 * NCH)
                sp.wait_ge(acc_sent, START + 16 * NCH)

            @block.gpsimd
            def _(pool):
                pool.wait_ge(tables, START + 48)
                with pool.Fori(0, NCH) as c:
                    pool.wait_ge(dest_ready, START + c + 1)
                    pool.sem_inc(posted, 1)
                    for i in range(CT):
                        for k in range(TOPK):
                            nc.gpsimd.indirect_dma_start(
                                out=dram["table"], out_offset=bass.IndirectOffsetOnAxis(ap=dest[:, i, k:k + 1], axis=0),
                                in_=entry[:, i, k, :], in_offset=None,
                                bounds_check=NE * CAP - 1, oob_is_err=False).then_inc(placed, 16)
                pool.wait_ge(placed, 16 * NCH * CT * TOPK)

            @block.tensor
            def _(pe):
                def turn(c):
                    for i in range(CT):
                        pe.wait_ge(normed, START + c * CT + i + 1)
                        if i % 2 == 0 and not (isinstance(c, int) and c == 0):
                            pe.wait_ge(xT_ready, START + (c - 1) * 2 + i // 2 + 1)
                        for k in range(KC):
                            last = nc.tensor.transpose(tp[:, i // 2, k, (i % 2) * P:(i % 2 + 1) * P],
                                                       xn[:, i, k * P:(k + 1) * P], ident)
                        last.then_inc(turned, 1)

                def route_logits(c, s):
                    pe.wait_ge(xT_ready, START + c * 2 + 2)
                    pe.wait_ge(route, START + c * STEPS)
                    pe.wait_ge(exp_s, START + c * 2)
                    pe.wait_ge(x_done, START + c * CT)
                    for i in range(CT):
                        for k in range(KC):
                            last = nc.tensor.matmul(logits[:, i, :], xT[:, s, k, i * P:(i + 1) * P], wr[:, k, :],
                                                    start=(k == 0), stop=(k == KC - 1))
                    last.then_inc(logit_s, 1)

                def rank(c):
                    pe.wait_ge(masked, START + c + 1)
                    for i in range(CT):
                        nc.tensor.matmul(ranks[:, i, :], tri[:], mask[:, i, :], start=True, stop=False)
                        last = nc.tensor.matmul(ranks[:, i, :], ones[:], before_[:, i, :], start=False, stop=True)
                    last.then_inc(ranked, 1)

                def gate_up(c, s):
                    for j in range(FB):
                        r = hid(j)
                        pe.wait_ge(h_ready, START + c * FB + max(j - 1, 0))
                        for w, out in ((core.wgT, gate), (core.wuT, up)):
                            for k in range(KC):
                                last = nc.tensor.matmul(out[0:r, j % 2, :], w[:, k, j * P:j * P + r], xT[:, s, k, :],
                                                        start=(k == 0), stop=(k == KC - 1))
                        last.then_inc(gu_ready, 1)
                        if j == 4:
                            rank(c)

                def down_proj(c):
                    pe.wait_ge(lg_kept, START + c + 1)
                    pe.wait_ge(ranks_used, START + c + 1)
                    for i in range(CT):
                        pe.wait_ge(x_done, START + c * CT + max(i - 1, 0))
                        for j in range(FB):
                            r = hid(j)
                            if i == 0:
                                pe.wait_ge(h_ready, START + c * FB + j + 1)
                            last = nc.tensor.matmul(down[:, i % 2, 0:D], hT[0:r, j, i * P:(i + 1) * P],
                                                    core.wdT[0:r, j, :], start=(j == 0), stop=(j == FB - 1))
                        last.then_inc(down_ready, 1)

                def chunk(c, s, ahead):
                    route_logits(c, s)
                    gate_up(c, s)
                    if ahead:
                        turn(c + 1)
                    down_proj(c)

                pe.wait_ge(w_in, START + 16 * (7 if load else 3))
                pe.wait_ge(setup, START + 2)
                turn(0)
                with pe.Fori(0, NCH // 2 - 1) as it:
                    for s in range(2):
                        chunk(it * 2 + s, s, True)
                chunk(NCH - 2, 0, True)
                chunk(NCH - 1, 1, False)

            @block.scalar
            def _(act):
                nc.scalar.activation(core.rstd[:], core.mv[:, :, 1], ACT.Sqrt, bias=core.eps[:, 0:1]).then_inc(root1, 1)
                act.wait_ge(scales, START + 3)
                nc.scalar.activation(both[:], tmp[:], ACT.Sqrt, bias=core.eps[:, 1:2]).then_inc(root2, 1)
                act.wait_ge(w_in, START + 16 * (7 if load else 3))

                def keep_xT(c, s):
                    for b in range(2):
                        act.wait_ge(turned, START + c * CT + 2 * b + 2)
                        for k in range(KC):
                            last = nc.scalar.activation(xT[:, s, k, b * 2 * P:(b + 1) * 2 * P], tp[:, b, k, :], ACT.Copy,
                                                        scale=wn[:, k:k + 1])
                        last.then_inc(xT_ready, 1)

                def route_exps(c):
                    act.wait_ge(lg_kept, START + c + 1)
                    act.wait_ge(x_done, START + c * CT)
                    nc.scalar.activation(hgate[:], lg[:, :, NE], ACT.Exp, scale=-1.0).then_inc(exp_s, 1)
                    act.wait_ge(shifted, START + c + 1)
                    nc.scalar.activation(prob[:], prob[:], ACT.Exp).then_inc(exp_s, 1)

                def silus(c):
                    for j in range(FB):
                        r = hid(j)
                        if j == 1:
                            route_exps(c)
                        act.wait_ge(gu_ready, START + c * FB + j + 1)
                        act.wait_ge(h_ready, START + c * FB + max(j - 1, 0))
                        nc.scalar.activation(silu[0:r, j % 2, :], gate[0:r, j % 2, :], ACT.Tanh, scale=0.5).then_inc(silu_ready, 1)

                keep_xT(0, 0)
                with act.Fori(0, NCH // 2 - 1) as it:
                    for s in range(2):
                        silus(it * 2 + s)
                        keep_xT(it * 2 + s + 1, 1 - s)
                silus(NCH - 2)
                keep_xT(NCH - 1, 1)
                silus(NCH - 1)

            @block.vector
            def _(dve):
                nc.vector.memset(zero[:], 0.0)
                nc.vector.memset(empty[:, :, 1], 0)
                nc.vector.tensor_copy(empty[:, :, 0], core.const("slot")).then_inc(setup, 1)
                nc.vector.memset(before_[:, CT, :], 0.0)
                nc.vector.memset(ones[:], 1.0)
                nc.vector.tensor_copy(tri[:], core.const("tri")).then_inc(setup, 1)
                steps = 0

                def scale_step(instruction):
                    nonlocal steps
                    steps += 1
                    instruction.then_inc(scales, 1)
                    dve.wait_ge(scales, START + steps)

                dve.wait_ge(root1, START + 1)
                scale_step(nc.vector.reciprocal(core.rstd[:], core.rstd[:]))
                scale_step(nc.vector.tensor_tensor(tmp[:], core.rstd[:], core.mv[:, :, 1], ALU.mult))
                scale_step(nc.vector.tensor_tensor(tmp[:], tmp[:], core.rstd[:], ALU.mult))
                dve.wait_ge(root2, START + 1)
                scale_step(nc.vector.reciprocal(both[:], both[:]))
                scale_step(nc.vector.tensor_tensor(both[:], both[:], core.rstd[:], ALU.mult))
                scale_step(nc.vector.tensor_scalar(keep[:], core.rstd[:], 0.5, 1.0, ALU.mult, ALU.add))
                scale_step(nc.vector.tensor_tensor(shift[:], core.rstd[:], core.mv[:, :, 0], ALU.mult))
                scale_step(nc.vector.tensor_scalar(shift[:], shift[:], -0.5, None, ALU.mult))

                def normalise(c, i):
                    t = c * CT + i
                    if not (isinstance(c, int) and c == 0):
                        dve.wait_ge(turned, START + (c - 1) * CT + i + 1)
                        dve.wait_ge(xn_sent, START + c * 16)
                    nc.vector.tensor_scalar(xn[:, i, :], at(core.x, t), at(core.mv, t)[:, 0:1],
                                            col(both, t), ALU.subtract, ALU.mult).then_inc(normed, 1)

                def hidden(c, j):
                    r = hid(j)
                    dve.wait_ge(silu_ready, START + c * FB + j + 1)
                    if j == 0:
                        dve.wait_ge(down_ready, START + c * CT)
                    nc.vector.scalar_tensor_tensor(out=silu2[0:r, j % 2, :], in0=silu[0:r, j % 2, :], scalar=1.0,
                                                   in1=gate[0:r, j % 2, :], op0=ALU.add, op1=ALU.mult).then_inc(silu2_s, 1)
                    dve.wait_ge(silu2_s, START + c * FB + j + 1)
                    nc.vector.tensor_tensor(hT[0:r, j, :], silu2[0:r, j % 2, :], up[0:r, j % 2, :],
                                            ALU.mult).then_inc(h_ready, 1)

                def residual(c, ahead):
                    for i in range(CT):
                        t = c * CT + i
                        nc.vector.tensor_scalar(at(core.x, t), at(core.x, t), col(keep, t), col(shift, t),
                                                ALU.mult, ALU.add).then_inc(setup, 1)
                    for i in range(CT):
                        t = c * CT + i
                        dve.wait_ge(setup, START + t + 3)
                        dve.wait_ge(down_ready, START + t + 1)
                        nc.vector.scalar_tensor_tensor(out=at(core.x, t), in0=down[:, i % 2, 0:D], scalar=hgate[:, i:i + 1],
                                                       in1=at(core.x, t), op0=ALU.mult, op1=ALU.add).then_inc(x_done, 1)
                        if ahead:
                            normalise(c + 2, i)

                done = 0

                def link(c, instruction):
                    nonlocal done
                    done += 1
                    instruction.then_inc(route, 1)
                    dve.wait_ge(route, START + c * STEPS + done)

                def shift_logits(c):
                    dve.wait_ge(logit_s, START + c + 1)
                    nc.vector.tensor_copy(lg[:], logits).then_inc(lg_kept, 1)
                    dve.wait_ge(lg_kept, START + c + 1)
                    link(c, nc.vector.tensor_reduce(lmax[:], lg[:, :, 0:NE], AX.X, ALU.max))
                    nc.vector.tensor_tensor(prob[:], lg[:, :, 0:NE], spread(lmax[:], 2, NE), ALU.subtract).then_inc(shifted, 1)

                def choose(c):
                    dve.wait_ge(exp_s, START + 2 * c + 2)
                    link(c, nc.vector.tensor_reduce(psum_[:], prob[:], AX.X, ALU.add))
                    link(c, nc.vector.reciprocal(psum_[:], psum_[:]))
                    link(c, nc.vector.tensor_tensor(prob[:], prob[:], spread(psum_[:], 2, NE), ALU.mult))
                    nc.vector.tensor_scalar(hgate[:], hgate[:], 4.0, 4.0, ALU.mult, ALU.add).then_inc(gated, 1)
                    for i in range(CT):
                        last = nc.vector.max(top[:, i, :], prob[:, i, :])
                    link(c, last)
                    dve.wait_ge(gated, START + c + 1)
                    nc.vector.reciprocal(hgate[:], hgate[:])
                    for i in range(CT):
                        last = nc.vector.max_index(topi[:, i, :], top[:, i, :], prob[:, i, :])
                    link(c, last)

                def count_experts(c):
                    link(c, nc.vector.tensor_copy(topf[:], topi[:, :, 0:TOPK]))
                    expert = spread(spread(core.const("expert"), 1, TOPK), 1, CT)
                    link(c, nc.vector.tensor_tensor(hot[:], expert, spread(topf[:], 3, NE), ALU.is_equal))
                    link(c, nc.vector.tensor_reduce(count[:], hot[:].rearrange("p i k e -> p i e k"), AX.X, ALU.add))
                    nc.vector.tensor_copy(mask[:], count[:])
                    link(c, nc.vector.tensor_copy(before_[:, 0, :], before_[:, CT, :]))
                    for i in range(CT):
                        last = nc.vector.tensor_tensor(before_[:, i + 1, :], before_[:, i, :], mask[:, i, :], ALU.add)
                        if i < CT - 1:
                            link(c, last)
                    last.then_inc(masked, 1)

                def place(c):
                    dve.wait_ge(ranked, START + c + 1)
                    if not (isinstance(c, int) and c == 0):
                        dve.wait_ge(placed, c * 16 * CT * TOPK)
                    nc.vector.tensor_tensor(hotr[:], hot[:], spread(ranks, 2, TOPK), ALU.mult).then_inc(ranks_used, 1)
                    dve.wait_ge(ranks_used, START + c + 1)
                    link(c, nc.vector.tensor_reduce(pos[:], hotr[:], AX.X, ALU.add))
                    nc.vector.tensor_scalar(over[:], pos[:], float(CAP), float(2 * NE * CAP), ALU.is_ge, ALU.mult)
                    link(c, nc.vector.scalar_tensor_tensor(out=pos[:], in0=topf[:], scalar=float(CAP), in1=pos[:],
                                                           op0=ALU.mult, op1=ALU.add))
                    nc.vector.tensor_copy(entry[:, :, :, 0], spread(core.const("token")[:, bass.ds(c * CT, CT)], 2, TOPK))
                    nc.vector.tensor_copy(entry[:].bitcast(F32)[:, :, :, 1], top[:, :, 0:TOPK])
                    nc.vector.tensor_tensor(dest[:], pos[:], over[:], ALU.add).then_inc(dest_ready, 1)

                def chunk(c, ahead):
                    nonlocal done
                    done = 0
                    hidden(c, 0)
                    shift_logits(c)
                    hidden(c, 1)
                    choose(c)
                    hidden(c, 2)
                    count_experts(c)
                    hidden(c, 3)
                    hidden(c, 4)
                    place(c)
                    assert done == STEPS, done
                    hidden(c, 5)
                    residual(c, ahead > 1)

                for c in range(2):
                    for i in range(CT):
                        normalise(c, i)
                chunk(0, NCH - 1)
                with dve.Fori(1, NCH - 2) as c:
                    chunk(c, 2)
                chunk(NCH - 2, 1)
                chunk(NCH - 1, 0)


def experts_phase(core, tag, acc):
    nc, dram = core.nc, core.dram
    with ExitStack() as ctx:
        sb, ps, sem = scope(core, ctx)
        wn = sb(tag + "wn", [P, KC])
        table = sb(tag + "table", [P, NE, 2], I32)
        gidx = sb(tag + "gidx", [P, DEEP], I32)
        sidx = sb(tag + "sidx", [P, 2], I32)
        wgu = sb(tag + "wgu", [P, DEEP, KC, 2 * EF])
        wd = sb(tag + "wd", [EH, DEEP, 2, D])
        xg = sb(tag + "xg", [P, DEEP, D])
        xgT = sb(tag + "xgT", [P, 2, KC, P])
        silu = sb(tag + "silu", [P, 2, EF])
        silu2 = sb(tag + "silu2", [P, 2, EF])
        silu2_s = sem(tag + "silu2")
        h = sb(tag + "h", [P, 2, EF])
        hT = sb(tag + "hT", [EH, 2, 2, P])
        ys = sb(tag + "ys", [P, 2, D])
        tp = ps(tag + "tp", [P, 2, 512])
        gu = ps(tag + "gu", [P, 2, 512])
        ht = ps(tag + "ht", [P, 2, 512])
        dn = ps(tag + "dn", [P, 2, 512])
        names = "small_in gidx_s turned xgT_s gu_s silu_s h_s h_turned hT_s dn_s y_s added posted"
        (small_in, gidx_s, turned, xgT_s, gu_s, silu_s, h_s, h_turned, hT_s, dn_s, y_s,
         added, posted) = (sem(tag + n, 0 if n == "added" else START) for n in names.split())
        w_slot = [sem(f"{tag}w_slot{s}") for s in range(DEEP)]
        gathered = [sem(f"{tag}gathered{s}", 0) for s in range(DEEP)]
        ident = core.const("ident")

        def every(eng, body):
            for s in range(DEEP):
                body(0, s, s)
            with eng.Fori(1, NE // DEEP - 1) as it:
                for s in range(DEEP):
                    body(it, it * DEEP + s, s)
            for s in range(DEEP):
                body(NE // DEEP - 1, NE - DEEP + s, s)

        def within(e, n):
            return not isinstance(e, int) or e + n < NE

        nc.all_engine_barrier()
        with nc.Block() as block:
            @block.sync
            def _(sp):
                sp.dma_start(table[:], dram["table"].rearrange("(e s) w -> s e w", e=NE)).then_inc(small_in, 16)
                sp.dma_start(wn[:].rearrange("p (k a) -> p k a", a=1),
                             dram["L1_ffn_w_norm"].rearrange("(k p a) -> p k a", p=P, a=1)).then_inc(small_in, 16)

                def load(e, s):
                    for w, name in enumerate(("L1_ffn_w_gate", "L1_ffn_w_up")):
                        sp.dma_start(wgu[:, s, :, w * EF:(w + 1) * EF],
                                     dram[name][bass.ds(e, 1)].rearrange("a (k p) f -> p (a k) f", p=P)).then_inc(w_slot[s], 16)
                    sp.dma_start(wd[:, s], dram["L1_ffn_w_down"][bass.ds(e, 1)].rearrange("a (h f) d -> f (a h) d", h=2)).then_inc(w_slot[s], 16)

                for s in range(DEEP):
                    load(s, s)
                with sp.Fori(1, NE // DEEP) as it:
                    for s in range(DEEP):
                        sp.wait_ge(dn_s, START + (it - 1) * DEEP + s + 1)
                        load(it * DEEP + s, s)

            @block.gpsimd
            def _(pool):
                def gather(e, s):
                    pool.wait_ge(gidx_s, START + e + 1)
                    pool.sem_inc(posted, 1)
                    nc.gpsimd.indirect_dma_start(out=xg[:, s, :], out_offset=None, in_=dram["xn"],
                                                 in_offset=bass.IndirectOffsetOnAxis(ap=gidx[:, s:s + 1], axis=0),
                                                 bounds_check=NTOK + TRASH - 1, oob_is_err=True).then_inc(gathered[s], 16)

                def add(e, s):
                    pool.wait_ge(y_s, START + e + 1)
                    if not (isinstance(e, int) and e == 0):
                        pool.wait_ge(added, 16 * e)
                    pool.sem_inc(posted, 1)
                    nc.gpsimd.indirect_dma_start(out=acc, out_offset=bass.IndirectOffsetOnAxis(ap=sidx[:, s % 2:s % 2 + 1], axis=0),
                                                 in_=ys[:, s % 2, :], in_offset=None, compute_op=ALU.add,
                                                 bounds_check=NTOK + TRASH - 1, oob_is_err=True).then_inc(added, 16)

                for s in range(DEEP):
                    gather(s, s)

                def body(it, e, s):
                    add(e, s)
                    if within(e, DEEP):
                        gather(e + DEEP, s)

                every(pool, body)
                pool.wait_ge(added, 16 * NE)

            @block.tensor
            def _(pe):
                def turn(it, e, s):
                    pe.wait_ge(gathered[s], 16 * (it + 1))
                    for k in range(KC):
                        last = nc.tensor.transpose(tp[:, s % 2, k * P:(k + 1) * P], xg[:, s, k * P:(k + 1) * P], ident)
                    last.then_inc(turned, 1)

                def gate_up(it, e, s):
                    pe.wait_ge(xgT_s, START + e + 1)
                    pe.wait_ge(w_slot[s], START + 48 * (it + 1))
                    if not (isinstance(e, int) and e < 2):
                        pe.wait_ge(h_s, START + e - 1)
                    for k in range(KC):
                        last = nc.tensor.matmul(gu[:, s % 2, 0:2 * EF], xgT[:, s % 2, k, :], wgu[:, s, k, :],
                                                start=(k == 0), stop=(k == KC - 1))
                    last.then_inc(gu_s, 1)

                def turn_h(e, s):
                    pe.wait_ge(h_s, START + e + 1)
                    for half in range(2):
                        last = nc.tensor.transpose(ht[0:EH, s % 2, half * P:(half + 1) * P],
                                                   h[:, s % 2, half * EH:(half + 1) * EH], ident)
                    last.then_inc(h_turned, 1)

                def down(e, s):
                    pe.wait_ge(hT_s, START + e + 1)
                    if not (isinstance(e, int) and e < 2):
                        pe.wait_ge(y_s, START + e - 1)
                    for half in range(2):
                        last = nc.tensor.matmul(dn[:, s % 2, 0:D], hT[:, s % 2, half, :], wd[:, s, half, :],
                                                start=(half == 0), stop=(half == 1))
                    last.then_inc(dn_s, 1)

                def body(it, e, s):
                    if within(e, 1):
                        gate_up(it + (s + 1) // DEEP, e + 1, (s + 1) % DEEP)
                    turn_h(e, s)
                    if within(e, 2):
                        turn(it + (s + 2) // DEEP, e + 2, (s + 2) % DEEP)
                    down(e, s)

                turn(0, 0, 0)
                turn(0, 1, 1)
                gate_up(0, 0, 0)
                every(pe, body)

            @block.scalar
            def _(act):
                act.wait_ge(small_in, START + 32)

                def keep(e, s):
                    act.wait_ge(turned, START + e + 1)
                    for k in range(KC):
                        last = nc.scalar.activation(xgT[:, s % 2, k, :], tp[:, s % 2, k * P:(k + 1) * P], ACT.Copy, scale=wn[:, k:k + 1])
                    last.then_inc(xgT_s, 1)

                def tanh(e, s):
                    act.wait_ge(gu_s, START + e + 1)
                    nc.scalar.activation(silu[:, s % 2, :], gu[:, s % 2, 0:EF], ACT.Tanh, scale=0.5).then_inc(silu_s, 1)

                def keep_h(e, s):
                    act.wait_ge(h_turned, START + e + 1)
                    nc.scalar.activation(hT[:, s % 2], ht[0:EH, s % 2, 0:2 * P].rearrange("p (h c) -> p h c", h=2), ACT.Copy).then_inc(hT_s, 1)

                def body(it, e, s):
                    if within(e, 1):
                        tanh(e + 1, (s + 1) % DEEP)
                    keep_h(e, s)
                    if within(e, 2):
                        keep(e + 2, (s + 2) % DEEP)

                keep(0, 0)
                tanh(0, 0)
                keep(1, 1)
                every(act, body)

            @block.vector
            def _(dve):
                dve.wait_ge(small_in, START + 32)
                for e in range(DEEP):
                    nc.vector.tensor_copy(gidx[:, e:e + 1], table[:, e, 0:1]).then_inc(gidx_s, 1)

                def hidden(e, s):
                    dve.wait_ge(silu_s, START + e + 1)
                    nc.vector.scalar_tensor_tensor(out=silu2[:, s % 2, :], in0=silu[:, s % 2, :], scalar=1.0,
                                                   in1=gu[:, s % 2, 0:EF], op0=ALU.add, op1=ALU.mult).then_inc(silu2_s, 1)
                    dve.wait_ge(silu2_s, START + e + 1)
                    nc.vector.tensor_tensor(h[:, s % 2, :], silu2[:, s % 2, :], gu[:, s % 2, EF:2 * EF], ALU.mult).then_inc(h_s, 1)

                def weigh(e, s):
                    dve.wait_ge(dn_s, START + e + 1)
                    if not (isinstance(e, int) and e < 2):
                        dve.wait_ge(added, 16 * (e - 1))
                    nc.vector.tensor_copy(sidx[:, s % 2:s % 2 + 1], at(table, e)[:, 0:1])
                    nc.vector.tensor_scalar(ys[:, s % 2, :], dn[:, s % 2, 0:D], at(table[:].bitcast(F32), e)[:, 1:2], 0.25,
                                            ALU.mult, ALU.mult).then_inc(y_s, 1)

                def body(it, e, s):
                    if within(e, 1):
                        hidden(e + 1, (s + 1) % DEEP)
                    if within(e, DEEP):
                        dve.wait_ge(gathered[s], 16 * (it + 1))
                        nc.vector.tensor_copy(gidx[:, s:s + 1], at(table, e + DEEP)[:, 0:1]).then_inc(gidx_s, 1)
                    weigh(e, s)

                hidden(0, 0)
                every(dve, body)


def reload_phase(core, tag, acc):
    nc = core.nc
    with ExitStack() as ctx:
        sb, _, sem = scope(core, ctx)
        bn = sb(tag + "bn", [P, NT, 6])
        back, stats = [sem(f"{tag}back{b}") for b in range(B)], sem(tag + "stats")
        nc.all_engine_barrier()
        with nc.Block() as block:
            @block.sync
            def _(sp):
                for b in range(B):
                    sp.dma_start(core.x[:, b * TPB:(b + 1) * TPB, :],
                                 acc[b * T:(b + 1) * T, :].rearrange("(i p) d -> p i d", p=P)).then_inc(back[b], 16)

            @block.vector
            def _(dve):
                for t in range(NT):
                    if t % TPB == 0:
                        dve.wait_ge(back[t // TPB], START + 16)
                    last = nc.vector.bn_stats(bn[:, t, :], core.x[:, t, :])
                last.then_inc(stats, 1)
                dve.wait_ge(stats, START + 1)
                for t in range(NT):
                    nc.vector.bn_aggr(core.mv[:, t, :], bn[:, t, :])


def spread(ap, axis, n):
    u = ap.unsqueeze(axis)
    shape = list(u.shape)
    shape[axis] = n
    return u.to_broadcast(shape)


def attention_phase(core, tag, second):
    nc, dram = core.nc, core.dram
    W = 6 * HD + (6 if second else 0)
    WM = W + 3
    GH = 4
    NG = NH // GH
    HALF = 512
    QH = T // HALF
    KPH = HALF // P
    units = [(h, kt, max(0, kt - KPH * h) * P if second else 0)
             for h in range(QH) for kt in range(KPH * (h + 1) if second else TPB)]
    U = len(units)
    chunks = [(j, qt, kh, min(HALF, (qt + 1) * P - kh * HALF) if second else HALF)
              for j in range(GH) for qt in range(TPB) for kh in range(2)
              if not second or (qt + 1) * P > kh * HALF]
    C = len(chunks)
    beside = [C * min(u, U - 2) // (U - 2) for u in range(U + 1)]
    NV = 2
    SB = 3
    y_unit = 2 + next(u for u in range(U) if units[u][0])
    after_y = [n for n in (SB - 1 + SB * -(-(max(beside[y_unit] - SB + 1, 0)) // SB),) if n < C]

    with ExitStack() as ctx:
        sb, ps, sem = scope(core, ctx)
        xn = sb(tag + "xn", [P, TPB, D])
        y = xn
        xT = sb(tag + "xT", [P, KC, T])
        qk = sb(tag + "qk", [P, 2, 2 * NH, HD])
        rot = sb(tag + "rot", [P, 2, 2 * NH, ROPE])
        rest = sb(tag + "rest", [P, 2, NH, HD])
        A = sb(tag + "A", [P, 2, 2, NH, W], BF16)
        QT = sb(tag + "QT", [WM, NH, T], BF16)
        KT = sb(tag + "KT", [WM, NH, T], BF16)
        V = sb(tag + "V", [P, TPB, NH, HD])
        Vg = sb(tag + "Vg", [P, TPB, GH, VW])
        E = sb(tag + "E", [P, 2, GH, HALF])
        Ysb = sb(tag + "Ysb", [P, 2, HALF])
        rden = sb(tag + "rden", [P, KPH, GH])
        mx = sb(tag + "mx", [P, GH, TPB, 2])
        m = sb(tag + "m", [P, GH, TPB])
        mrest = sb(tag + "mrest", [P, GH, TPB])
        mparts = sb(tag + "mparts", [P, GH, 3, TPB], BF16)
        mT = sb(tag + "mT", [GH * 3 * TPB, P], BF16)
        yT = sb(tag + "yT", [P, 2, KC, P])
        bn8 = sb(tag + "bn8", [P, TPB, 6])
        carrier = sb(tag + "carrier", [P, 1])
        mv8 = sb(tag + "mv8", [P, TPB, 2])
        masks = sb(tag + "masks", [P, 2, P], BF16)
        bank = ps(tag + "bank", [P, 8, 512])
        ident, ident_b = core.const("ident"), core.ident_b
        names = ("w_in ones consts_b root scales normed turned xT_kept qkv qk_kept v_kept roped part1 rested "
                 "part2 parts ops_turned ops_dve ops_act chunk_done reduced v_group m_step m_turned mT_kept m_rows "
                 "scored exps pv y_kept y_turned y_step y_normed out_turned yT_kept out_done x_done stats aggregated")
        S = {n: sem(tag + n) for n in names.split()}
        (w_in, ones, consts_b, root, scales, normed, turned, xT_kept, qkv, qk_kept, v_kept, roped, part1, rested,
         part2, parts, ops_turned, ops_dve, ops_act, chunk_done, reduced, v_group, m_step, m_turned, mT_kept, m_rows,
         scored, exps, pv, y_kept, y_turned, y_step, y_normed, out_turned, yT_kept, out_done, x_done,
         stats, aggregated) = (S[n] for n in names.split())

        def tile_bank(i):
            return bank[:, (i // 2) % 2, :].rearrange("p (k h c) -> p k h c", k=KC, h=2)

        def ops_bank(n):
            return bank[:, 5 + n % 2, :].bitcast(BF16).rearrange("p (h c) -> p h c", h=8)

        def before(b, per_batch, n):
            return b * per_batch + max(n, 0)

        nc.all_engine_barrier()
        with nc.Block() as block:
            @block.sync
            def _(sp):
                if second:
                    sp.dma_start(core.wqkvT[:], dram["L1_attn_W_qkv"].rearrange("(k p) e -> p k e", p=P)).then_inc(w_in, 16)
                    sp.dma_start(core.woT[:], dram["L1_attn_W_o"].rearrange("(k p) e -> p k e", p=P)).then_inc(w_in, 16)

                def rows(b, g):
                    sp.wait_ge(mT_kept, START + b * NG + g + 1)
                    for j in range(GH):
                        h = g * GH + j
                        dst = QT[W:WM, h, :].rearrange("r (q c) -> r q c", c=P)
                        sp.dma_start(dst, mT[j * 3 * TPB:(j + 1) * 3 * TPB, :]).then_inc(m_rows, 16)

                with sp.Fori(0, B) as b:
                    for g in range(NG):
                        rows(b, g)

            @block.gpsimd
            def _(pool):
                def rope(b, i):
                    tab = core.const("rope").rearrange("p (i s r) -> p i s r", i=TPB, s=2)
                    z = qk[:, i % 2]
                    pool.wait_ge(qk_kept, START + b * TPB + i + 1)
                    pool.wait_ge(roped, START + b * 2 * TPB + 2 * i)
                    H2 = ROPE // 2
                    nc.gpsimd.tensor_tensor(rot[:, 1, :, 0:H2], z[:, :, H2:ROPE], spread(tab[:, i, 1, 0:H2], 1, 2 * NH), ALU.mult)
                    nc.gpsimd.tensor_tensor(rot[:, 1, :, H2:ROPE], z[:, :, 0:H2], spread(tab[:, i, 1, H2:ROPE], 1, 2 * NH), ALU.mult)
                    nc.gpsimd.tensor_tensor(rot[:, 0, :, :], z[:, :, 0:ROPE], spread(tab[:, i, 0, :], 1, 2 * NH),
                                            ALU.mult).then_inc(roped, 1)
                    pool.wait_ge(roped, START + b * 2 * TPB + 2 * i + 1)
                    nc.gpsimd.tensor_tensor(z[:, :, 0:ROPE], rot[:, 0], rot[:, 1], ALU.add).then_inc(roped, 1)

                def rests(b, i):
                    pool.wait_ge(part1, START + b * TPB + i + 1)
                    pool.wait_ge(parts, START + b * TPB + i)
                    for q, slot in ((0, 0), (1, 1)):
                        a = A[:, i % 2, q, :, 0:6 * HD].rearrange("p h (s d) -> p h s d", d=HD)
                        nc.gpsimd.tensor_tensor(rest[:, q], qk[:, i % 2, q * NH:(q + 1) * NH, :], a[:, :, slot, :],
                                                ALU.subtract).then_inc(rested, 1)

                def third_parts(b, i):
                    pool.wait_ge(part2, START + b * TPB + i + 1)
                    for q, low, slot in ((0, 3, 5), (1, 0, 2)):
                        a = A[:, i % 2, q, :, 0:6 * HD].rearrange("p h (s d) -> p h s d", d=HD)
                        last = nc.gpsimd.tensor_tensor(a[:, :, slot, :], rest[:, q], a[:, :, low, :], ALU.subtract)
                    last.then_inc(parts, 1)

                with pool.Fori(0, B) as b:
                    if not second:
                        rope(b, 0)
                    for i in range(TPB):
                        if not second and i + 1 < TPB:
                            rope(b, i + 1)
                        rests(b, i)
                        third_parts(b, i)
                    for g in range(NG):
                        pool.wait_ge(consts_b, START + 1)
                        pool.wait_ge(v_kept, START + (b + 1) * TPB)
                        pool.wait_ge(pv, START + (b * NG + g) * U)
                        own = V[:, :, g * GH:(g + 1) * GH, :]
                        one = Vg[:, :, :, HD:HD + 1].to_broadcast([P, TPB, GH, HD])
                        nc.gpsimd.tensor_tensor(Vg[:, :, :, 0:HD], own, one, ALU.mult).then_inc(v_group, 1)

            @block.tensor
            def _(pe):
                def max_chunks(G, head, lo, hi, y_count=None):
                    for n in range(lo, min(hi, C)):
                        j, qt, kh, w = chunks[n]
                        pe.wait_ge(reduced, START + G * C + max(n - SB + 1, 0))
                        if y_count is not None and n in [SB - 1] + after_y:
                            pe.wait_ge(y_normed, START + y_count)
                        out = bank[:, 5 + n % SB, 0:w]
                        q = QT[0:W, head + j, qt * P:(qt + 1) * P]
                        k = KT[0:W, head + j, kh * HALF:kh * HALF + w]
                        diag = second and qt * P < kh * HALF + w <= (qt + 1) * P
                        last = nc.tensor.matmul(out, q, k, start=True, stop=not diag)
                        if diag:
                            last = nc.tensor.matmul(out[:, w - P:w], ident_b[:], masks[:, 0, :], start=False, stop=True)
                        last.then_inc(chunk_done, 1)

                def turn_max(G):
                    pe.wait_ge(m_step, START + (G + 1) * 4)
                    out = bank[0:GH * 3 * TPB, 5, :].bitcast(BF16)[:, 0:P]
                    nc.tensor.transpose(out, mparts[:].rearrange("p j r q -> p (j r q)"), ident_b[:]).then_inc(m_turned, 1)

                def score_pair(G, head, u, pair):
                    half, kt, c0 = units[u]
                    pe.wait_ge(exps, START + G * 2 * U + (2 * u - 1 + pair if u else 0))
                    for j in (2 * pair, 2 * pair + 1):
                        out = bank[:, j, c0:HALF]
                        k = KT[:, head + j, kt * P:(kt + 1) * P]
                        q = QT[:, head + j, half * HALF + c0:(half + 1) * HALF]
                        diag = second and kt >= KPH * half
                        last = nc.tensor.matmul(out, k, q, start=True, stop=not diag)
                        if diag:
                            last = nc.tensor.matmul(out[:, 0:P], ident_b[:], masks[:, 1, :], start=False, stop=True)
                    last.then_inc(scored, 1)

                def pv_unit(G, u):
                    half, kt, c0 = units[u]
                    first, final = u == 0 or units[u - 1][0] != half, u == U - 1 or units[u + 1][0] != half
                    pe.wait_ge(exps, START + G * 2 * U + 2 * u + 2)
                    if first:
                        pe.wait_ge(y_kept, START + G * NV + half)
                    if u == 0:
                        pe.wait_ge(v_group, START + G + 1)
                    for j in range(GH):
                        last = nc.tensor.matmul(bank[VW * j:VW * (j + 1), 4, c0:HALF], Vg[:, kt, j, :], E[:, u % 2, j, c0:HALF],
                                                start=first, stop=final, tile_position=(0, VW * j))
                    last.then_inc(pv, 1)

                def turn_y(G, half):
                    pe.wait_ge(y_kept, START + G * NV + half + 1)
                    pe.wait_ge(y_normed, START + G * NV + half)
                    for i in range(KPH):
                        last = nc.tensor.transpose(bank[:, 7, i * P:(i + 1) * P], Ysb[:, half, i * P:(i + 1) * P], ident)
                    last.then_inc(y_turned, 1)

                def group(b, g, more):
                    G, head = b * NG + g, g * GH
                    pe.wait_ge(m_rows, START + (G + 1) * GH * 16)
                    def chunk_run(lo, hi):
                        if more:
                            max_chunks(G + 1, head + GH, lo, hi, G * NV + (1 if lo >= beside[y_unit] else 0))

                    for u in range(U):
                        lo, hi = beside[u], beside[u + 1]
                        if u == y_unit:
                            if more:
                                pe.wait_ge(reduced, START + (G + 1) * C + lo)
                            turn_y(G, 0)
                        score_pair(G, head, u, 0)
                        chunk_run(lo, min(lo + 1, hi))
                        score_pair(G, head, u, 1)
                        chunk_run(lo + 1, min(lo + 2, hi))
                        if u:
                            pv_unit(G, u - 1)
                        chunk_run(lo + 2, hi)
                        if more and u == U - 2:
                            turn_max(G + 1)
                    pv_unit(G, U - 1)
                    turn_y(G, 1)

                def turn_tile(b, i):
                    pe.wait_ge(normed, START + b * TPB + i + 1)
                    if i >= 4:
                        pe.wait_ge(xT_kept, START + b * (TPB // 2) + i // 2 - 1)
                    for k in range(KC):
                        last = nc.tensor.transpose(tile_bank(i)[:, k, i % 2, :], xn[:, i, k * P:(k + 1) * P], ident)
                    last.then_inc(turned, 1)

                def project(b, i):
                    pe.wait_ge(xT_kept, START + b * (TPB // 2) + i // 2 + 1)
                    pe.wait_ge(qk_kept, START + before(b, TPB, i - 1))
                    for k in range(KC):
                        nc.tensor.matmul(bank[:, 2 + i % 2, :], xT[:, k, i * P:(i + 1) * P], core.wqkvT[:, k, 0:2 * D],
                                         start=(k == 0), stop=(k == KC - 1))
                    pe.wait_ge(v_kept, START + before(b, TPB, i))
                    for k in range(KC):
                        last = nc.tensor.matmul(bank[:, 4, 0:D], xT[:, k, i * P:(i + 1) * P], core.wqkvT[:, k, 2 * D:3 * D],
                                                start=(k == 0), stop=(k == KC - 1))
                    last.then_inc(qkv, 1)

                def turn_ops(b, i):
                    pe.wait_ge(parts, START + b * TPB + i + 1)
                    for n in range(4):
                        pe.wait_ge(ops_dve, START + b * 3 * TPB + 3 * i + max(n - 1, 0))
                        if n == 1:
                            pe.wait_ge(ops_act, START + b * TPB + i)
                        for h in range(8):
                            last = nc.tensor.transpose(ops_bank(n)[0:W, h, :], A[:, i % 2, n // 2, (n % 2) * 8 + h, :], ident_b[:])
                        last.then_inc(ops_turned, 1)

                def turn_out(b, i):
                    pe.wait_ge(yT_kept, START + before(b, TPB, i - 1))
                    for k in range(KC):
                        last = nc.tensor.transpose(bank[:, i % 2, k * P:(k + 1) * P], y[:, i, k * P:(k + 1) * P], ident)
                    last.then_inc(out_turned, 1)

                def out_proj(b, i):
                    pe.wait_ge(yT_kept, START + b * TPB + i + 1)
                    pe.wait_ge(x_done, START + before(b, TPB, i - 1))
                    for k in range(KC):
                        last = nc.tensor.matmul(bank[:, 2 + i % 2, 0:D], yT[:, i % 2, k, :], core.woT[:, k, :],
                                                start=(k == 0), stop=(k == KC - 1))
                    last.then_inc(out_done, 1)

                pe.wait_ge(consts_b, START + 3 if second else 1)
                if second:
                    pe.wait_ge(w_in, START + 32)
                with pe.Fori(0, B) as b:
                    for i in range(4):
                        turn_tile(b, i)
                    project(b, 0)
                    project(b, 1)
                    for i in range(4, TPB):
                        turn_tile(b, i)
                    for i in range(TPB):
                        if i + 2 < TPB:
                            project(b, i + 2)
                        turn_ops(b, i)
                    pe.wait_ge(ops_dve, START + (b + 1) * 3 * TPB)
                    pe.wait_ge(ops_act, START + (b + 1) * TPB)
                    max_chunks(b * NG, 0, 0, C)
                    turn_max(b * NG)
                    for g in range(NG):
                        group(b, g, g + 1 < NG)
                    pe.wait_ge(y_normed, START + (b + 1) * NG * NV)
                    turn_out(b, 0)
                    for i in range(TPB):
                        if i + 1 < TPB:
                            turn_out(b, i + 1)
                        out_proj(b, i)

            @block.scalar
            def _(act):
                nc.scalar.activation(core.rstd[:], core.mv[:, :, 1], ACT.Sqrt, bias=core.eps[:, 0:1]).then_inc(root, 1)

                def take(b, i):
                    act.wait_ge(qkv, START + b * TPB + i + 1)
                    act.wait_ge(rested, START + before(b, 2 * TPB, 2 * (i - 1)))
                    nc.scalar.activation(V[:, i, :, :], bank[:, 4, 0:D].rearrange("p (h d) -> p h d", d=HD),
                                         ACT.Copy).then_inc(v_kept, 1)
                    pq = bank[:, 2 + i % 2, :].rearrange("p (h d) -> p h d", d=HD)
                    nc.scalar.activation(qk[:, i % 2, 0:NH, :], pq[:, 0:NH], ACT.Copy, scale=HD ** -0.5)
                    nc.scalar.activation(qk[:, i % 2, NH:2 * NH, :], pq[:, NH:2 * NH], ACT.Copy).then_inc(qk_kept, 1)

                def first_parts(b, i):
                    act.wait_ge(qk_kept if second else roped, START + b * TPB * (1 if second else 2) + (i + 1) * (1 if second else 2))
                    act.wait_ge(ops_turned, START + before(b, 4 * TPB, 4 * (i - 1)))
                    for q, slots in ((0, slice(0, 3)), (1, slice(1, 6, 2))):
                        dst = A[:, i % 2, q, :, 0:6 * HD].rearrange("p h (s d) -> p h s d", d=HD)[:, :, slots, :]
                        last = nc.scalar.activation(dst, spread(qk[:, i % 2, q * NH:(q + 1) * NH, :], 2, 3), ACT.Copy)
                    last.then_inc(part1, 1)

                def keep_ops(b, i):
                    act.wait_ge(ops_turned, START + b * 4 * TPB + 4 * i + 4)
                    nc.scalar.activation(KT[0:W, 8:16, i * P:(i + 1) * P], ops_bank(3)[0:W], ACT.Copy).then_inc(ops_act, 1)

                def exp_unit(G, u):
                    half, kt, c0 = units[u]
                    act.wait_ge(pv, START + G * U + max(u - 1, 0))
                    for pair in range(2):
                        act.wait_ge(scored, START + G * 2 * U + 2 * u + pair + 1)
                        nc.scalar.activation(E[:, u % 2, 2 * pair:2 * pair + 2, c0:HALF], bank[:, 2 * pair:2 * pair + 2, c0:HALF],
                                             ACT.Exp).then_inc(exps, 1)

                def keep_y(G, half):
                    done = sum(1 for h, _, _ in units if h <= half)
                    act.wait_ge(pv, START + G * U + done)
                    act.wait_ge(y_turned, START + G * NV + half)
                    nc.scalar.activation(Ysb[:, half, :], bank[:, 4, :], ACT.Copy).then_inc(y_kept, 1)

                def group(b, g):
                    for u in range(U):
                        exp_unit(b * NG + g, u)
                        if u and units[u][0] != units[u - 1][0]:
                            keep_y(b * NG + g, 0)
                    keep_y(b * NG + g, 1)

                with act.Fori(0, B) as b:
                    def keep_tiles(k):
                        act.wait_ge(turned, START + b * TPB + 2 * k + 2)
                        dst = xT[:, :, 2 * k * P:2 * (k + 1) * P].rearrange("p k (h c) -> p k h c", h=2)
                        nc.scalar.activation(dst, tile_bank(2 * k), ACT.Copy).then_inc(xT_kept, 1)

                    keep_tiles(0)
                    keep_tiles(1)
                    take(b, 0)
                    keep_tiles(2)
                    keep_tiles(3)
                    for i in range(TPB + 1):
                        if i + 1 < TPB:
                            take(b, i + 1)
                        if i < TPB:
                            first_parts(b, i)
                        if i:
                            keep_ops(b, i - 1)
                    for g in range(NG):
                        group(b, g)
                    for i in range(TPB):
                        act.wait_ge(out_turned, START + b * TPB + i + 1)
                        act.wait_ge(out_done, START + before(b, TPB, i - 1))
                        nc.scalar.activation(yT[:, i % 2], bank[:, i % 2, 0:D].rearrange("p (k c) -> p k c", k=KC),
                                             ACT.Copy).then_inc(yT_kept, 1)

            @block.vector
            def _(dve):
                dve.wait_ge(root, START + 1)
                nc.vector.reciprocal(core.rstd[:], core.rstd[:]).then_inc(scales, 1)
                nc.vector.memset(KT[96:WM, :, :], 1.0).then_inc(ones, 1)
                nc.vector.memset(Vg[:], 0.0).then_inc(ones, 1)
                dve.wait_ge(ones, START + 2)
                nc.vector.memset(Vg[:, :, :, HD:HD + 1], 1.0).then_inc(consts_b, 1)
                if second:
                    nc.vector.memset(mx[:], NEG)
                    nc.vector.tensor_copy(masks[:, 0, :], core.const("mask_qk"))
                    nc.vector.tensor_copy(masks[:, 1, :], core.const("mask_kq")).then_inc(consts_b, 1)
                    for s in range(2):
                        nc.vector.tensor_copy(A[:, s, 0, :, 6 * HD:W], core.const("slopes").rearrange("p (h s) -> p h s", h=NH))
                        last = nc.vector.tensor_copy(A[:, s, 1, :, 6 * HD + 3:W], spread(core.const("kpos"), 1, NH))
                    last.then_inc(consts_b, 1)
                dve.wait_ge(scales, START + 1)

                def second_parts(b, i):
                    if second:
                        nc.vector.tensor_copy(A[:, i % 2, 1, :, 6 * HD:6 * HD + 3],
                                              spread(core.const("kbase")[:, 3 * i:3 * i + 3], 1, NH))
                    for q, slots in ((0, slice(3, 5)), (1, slice(0, 5, 4))):
                        dve.wait_ge(rested, START + b * 2 * TPB + 2 * i + q + 1)
                        dst = A[:, i % 2, q, :, 0:6 * HD].rearrange("p h (s d) -> p h s d", d=HD)[:, :, slots, :]
                        last = nc.vector.tensor_copy(dst, spread(rest[:, q], 2, 2))
                    last.then_inc(part2, 1)

                def keep_ops(b, i):
                    for n in range(3):
                        dve.wait_ge(ops_turned, START + b * 4 * TPB + 4 * i + n + 1)
                        dst = (QT if n // 2 == 0 else KT)[0:W, (n % 2) * 8:(n % 2) * 8 + 8, i * P:(i + 1) * P]
                        nc.vector.tensor_copy(dst, ops_bank(n)[0:W]).then_inc(ops_dve, 1)

                def reduce_chunks(G, lo, hi):
                    for n in range(lo, min(hi, C)):
                        j, qt, kh, w = chunks[n]
                        dve.wait_ge(chunk_done, START + G * C + n + 1)
                        nc.vector.tensor_reduce(mx[:, j, qt, kh:kh + 1], bank[:, 5 + n % SB, 0:w], AX.X, ALU.max).then_inc(reduced, 1)

                def maxima(G):
                    dve.wait_ge(reduced, START + (G + 1) * C)
                    nc.vector.tensor_reduce(m[:], mx[:], AX.X, ALU.max).then_inc(m_step, 1)
                    dve.wait_ge(m_step, START + G * 4 + 1)
                    nc.vector.tensor_scalar(mparts[:, :, 0, :], m[:], -1.0, None, ALU.mult).then_inc(m_step, 1)
                    dve.wait_ge(m_step, START + G * 4 + 2)
                    nc.vector.scalar_tensor_tensor(out=mrest[:], in0=m[:], scalar=-1.0, in1=mparts[:, :, 0, :],
                                                   op0=ALU.mult, op1=ALU.subtract).then_inc(m_step, 1)
                    dve.wait_ge(m_step, START + G * 4 + 3)
                    nc.vector.tensor_copy(mparts[:, :, 1, :], mrest[:]).then_inc(ones, 1)
                    dve.wait_ge(ones, START + 2 + G + 1)
                    nc.vector.tensor_tensor(mparts[:, :, 2, :], mrest[:], mparts[:, :, 1, :], ALU.subtract).then_inc(m_step, 1)

                def keep_max(G):
                    dve.wait_ge(m_turned, START + G + 1)
                    dve.wait_ge(m_rows, START + G * GH * 16)
                    nc.vector.tensor_copy(mT[:], bank[0:GH * 3 * TPB, 5, :].bitcast(BF16)[:, 0:P]).then_inc(mT_kept, 1)

                def norm_y(G, g, half):
                    z = bank[:, 7, :].rearrange("p (i j v) -> p i j v", i=KPH, j=GH)
                    dve.wait_ge(y_turned, START + G * NV + half + 1)
                    dve.wait_ge(y_normed, START + G * NV + half)
                    nc.vector.reciprocal(rden[:], z[:, :, :, HD]).then_inc(y_step, 1)
                    dve.wait_ge(y_step, START + G * NV + half + 1)
                    dst = y[:, half * KPH:(half + 1) * KPH, bass.ds(g * GH * HD, GH * HD)].rearrange("p i (j d) -> p i j d", d=HD)
                    nc.vector.tensor_tensor(dst, z[:, :, :, 0:HD], spread(rden[:], 3, HD), ALU.mult).then_inc(y_normed, 1)

                def group(b, g, more):
                    G = b * NG + g
                    for u in range(U):
                        if u == y_unit:
                            norm_y(G, g, 0)
                        if more:
                            if u == U - 2:
                                maxima(G + 1)
                                keep_max(G + 1)
                            reduce_chunks(G + 1, beside[u], beside[u + 1])
                    norm_y(G, g, 1)

                with dve.Fori(0, B) as b:
                    for i in range(TPB):
                        t = b * TPB + i
                        dve.wait_ge(out_turned, START + b * TPB)
                        nc.vector.tensor_scalar(xn[:, i, :], at(core.x, t), at(core.mv, t)[:, 0:1], col(core.rstd, t),
                                                ALU.subtract, ALU.mult).then_inc(normed, 1)
                    for i in range(TPB + 1):
                        if i:
                            keep_ops(b, i - 1)
                        if i < TPB:
                            second_parts(b, i)
                    reduce_chunks(b * NG, 0, C)
                    maxima(b * NG)
                    keep_max(b * NG)
                    for g in range(NG):
                        group(b, g, g + 1 < NG)
                    for i in range(TPB):
                        t = b * TPB + i
                        dve.wait_ge(out_done, START + t + 1)
                        nc.vector.tensor_tensor(at(core.x, t), bank[:, 2 + i % 2, 0:D], at(core.x, t), ALU.add).then_inc(x_done, 1)
                    for i in range(TPB):
                        dve.wait_ge(scales, START + 1)
                        dve.wait_ge(x_done, START + b * TPB + i + 1)
                        nc.vector.bn_stats(bn8[:, i, :], at(core.x, b * TPB + i)).then_inc(stats, 1)
                    dve.wait_ge(stats, START + (b + 1) * TPB)
                    nc.vector.memset(carrier[:], 0.0)
                    for i in range(TPB):
                        last = nc.vector.bn_aggr(mv8[:, i, :], bn8[:, i, :])
                    last.then_inc(aggregated, 1)
                    dve.wait_ge(aggregated, START + b + 1)
                    nc.vector.tensor_copy(core.mv[:, bass.ds(b * TPB, TPB), :], mv8[:])


def at(tensor, t):
    return tensor[:, t] if isinstance(t, int) else tensor[:, bass.ds(t, 1)].rearrange("p a d -> p (a d)")


def col(tensor, t):
    return tensor[:, t:t + 1] if isinstance(t, int) else tensor[:, bass.ds(t, 1)]


OUT_SHAPE = (NTOK + TRASH, D)


def store_phase(core):
    nc = core.nc
    with ExitStack() as ctx:
        _, _, sem = scope(core, ctx)
        stored = sem("stored")
        nc.all_engine_barrier()
        with nc.Block() as block:
            @block.sync
            def _(sp):
                sp.dma_start(core.dram["out"][0:NTOK, :].rearrange("(t p) d -> p t d", p=P), core.x[:]).then_inc(stored, 16)
                sp.wait_ge(stored, START + 16)


PHASES = ("prep", "ffn0", "attn0", "ffn0", "moe1", "attn1", "moe2")


def program(nc, dram, phases=PHASES):
    nc.disable_value_cache = True
    with ExitStack() as ctx:
        ctx.enter_context(nc.allow_non_contiguous_dma(reason="per-channel scales, once"))
        core = Core(nc, ctx, dram)
        dram["xn"] = nc.dram_tensor("normalised", (NTOK + TRASH, D), F32, kind="Internal").ap()
        dram["table"] = nc.dram_tensor("table", (NE * CAP, 2), I32, kind="Internal").ap()
        dram["acc"] = nc.dram_tensor("acc", (NTOK + TRASH, D), F32, kind="Internal").ap()
        for n, name in enumerate(phases):
            if name == "prep":
                prepare_phase(core)
            elif name == "ffn0":
                ffn0_phase(core, f"f{n}_")
            elif name in ("attn0", "attn1"):
                attention_phase(core, f"a{n}_", name == "attn1")
            elif name == "moe1":
                mixture_dense_phase(core, f"d{n}_", dram["acc"], True)
                experts_phase(core, f"e{n}_", dram["acc"])
                reload_phase(core, f"r{n}_", dram["acc"])
                core.clear_semaphores()
            elif name == "moe2":
                mixture_dense_phase(core, f"d{n}_", dram["out"], False)
                experts_phase(core, f"e{n}_", dram["out"])
            elif name == "store":
                store_phase(core)


_INS = ['L0_attn_x', 'L0_attn_wq', 'L0_attn_wk', 'L0_attn_wv', 'L0_attn_wo', 'L0_ffn_wq_gate', 'L0_ffn_s_gate',
        'L0_ffn_wq_up', 'L0_ffn_s_up', 'L0_ffn_wq_down', 'L0_ffn_s_down', 'L1_attn_W_qkv', 'L1_attn_W_o',
        'L1_ffn_w_norm', 'L1_ffn_w_router', 'L1_ffn_w_gate', 'L1_ffn_w_up', 'L1_ffn_w_down', 'L1_ffn_sw_gate',
        'L1_ffn_sw_up', 'L1_ffn_sw_down', 'L1_ffn_w_shared_gate']


def kernel(**inputs):
    import concourse.bacc as _bacc
    from concourse.bass_utils import run_bass_kernel_spmd as _run

    nc = _bacc.Bacc("TRN2", target_bir_lowering=False, num_devices=1)
    arrays, dram = {}, {}
    for name in _INS:
        arrays[f"in_{name}"] = np.ascontiguousarray(inputs[name])
    arrays["in_consts"] = constants()
    for name, a in arrays.items():
        dram[name[3:]] = nc.dram_tensor(name, a.shape, mybir.dt.from_np(a.dtype), kind="ExternalInput").ap()
    dram["out"] = nc.dram_tensor("out_0", OUT_SHAPE, F32, kind="ExternalOutput").ap()
    program(nc, dram)
    r = _run(nc, [arrays], core_ids=[0])
    return r.results[0]["out_0"][:NTOK].reshape(B, T, D)
```

```python
from contextlib import ExitStack

import concourse.bass as bass
from concourse import mybir
import numpy as np

F32 = mybir.dt.float32
BF16 = mybir.dt.bfloat16
F16 = mybir.dt.float16
I32 = mybir.dt.int32
U32 = mybir.dt.uint32
ALU = mybir.AluOpType
ACT = mybir.ActivationFunctionType
AX = mybir.AxisListType

P = 128
B, T, D = 4, 1024, 256
NTOK = B * T
NT = NTOK // P
TPB = T // P
KC = D // P
NH, HD = 16, 16
FF = 704
FB = -(-FF // P)
NE, TOPK, CAP, EF = 32, 4, 128, 176
EH = EF // 2
DEEP = 4
CT = 4
NCH = NT // CT
CW = CT * P
SUMS = 16
TRASH = P
ZERO_POINT = 128.0
LN_EPS, RMS_EPS = 1e-5, 1e-6
NEG = -1e30
VW = 32
ROPE = HD // 2
LIFT = 1024.0
HLIFT = 2.0 ** -16
START = 1

CONST = {}
_at = 0
for _name, _w in (("ident", P), ("tri", P), ("mask_qk", P), ("mask_kq", P), ("expert", NE), ("token", NT),
                  ("slopes", NH * 6), ("kbase", TPB * 3), ("kpos", 3), ("rope", TPB * 2 * ROPE), ("slot", NE)):
    CONST[_name] = (_at, _at + _w)
    _at += _w
NCONST = _at


def hid(j):
    return min(P, FF - j * P)


def constants():
    c = np.zeros((P, NCONST), np.float32)
    p = np.arange(P)

    def put(name, a):
        lo, hi = CONST[name]
        c[:, lo:hi] = a.reshape(P, hi - lo)

    put("ident", np.eye(P))
    put("tri", (p[:, None] < p[None, :]) * 1.0)
    put("mask_qk", np.where(p[None, :] > p[:, None], NEG, 0.0))
    put("mask_kq", np.where(p[:, None] > p[None, :], NEG, 0.0))
    put("expert", np.tile(np.arange(NE), (P, 1)))
    put("token", p[:, None] + P * np.arange(NT)[None, :])
    put("slot", NTOK + np.tile(p[:, None], (1, NE)))
    slopes = (2.0 ** (-8.0 / np.arange(1, NH + 1, dtype=np.float32))).astype(np.float32)
    parts, rest = [], slopes.copy()
    for _ in range(3):
        part = (rest.view(np.uint32) & np.uint32(0xFFFF0000)).view(np.float32)
        parts.append(part)
        rest = rest - part
    put("slopes", np.tile(np.stack(parts + parts, 1).reshape(-1), (P, 1)))
    put("kbase", np.tile(np.repeat(P * (np.arange(TPB) - TPB // 2), 3), (P, 1)))
    put("kpos", np.tile(p[:, None], (1, 3)))
    inv = (1.0 / 10000.0 ** (np.arange(0, HD, 2, dtype=np.float32) / np.float32(HD))).astype(np.float32)
    ang = (np.arange(T, dtype=np.float32)[:, None] * inv[None, :]).astype(np.float32)
    sin = np.sin(ang)
    sin[:, :ROPE // 2] *= -1
    tab = np.concatenate([np.cos(ang), sin], 1).astype(np.float32)
    put("rope", tab.reshape(TPB, P, 2 * ROPE).transpose(1, 0, 2))
    return c


class Core:

    def __init__(self, nc, ctx, dram):
        self.nc, self.dram, self.sems = nc, dram, []

        def sb(name, shape, dt=F32):
            return ctx.enter_context(nc.sbuf_tensor(name, shape, dt))

        self.x = sb("x", [P, NT, D])
        self.mv = sb("mv", [P, NT, 2])
        self.rstd = sb("rstd", [P, NT])
        self.consts = sb("consts", [P, NCONST])
        self.ident_b = sb("ident_b", [P, P], BF16)
        self.eps = sb("eps", [P, 2])
        self.wgT = sb("wgT", [P, KC, FF])
        self.wuT = sb("wuT", [P, KC, FF])
        self.wdT = sb("wdT", [P, FB, D])
        self.cgT = self.wgT[:].bitcast(F16)[:, :, 0:FF]
        self.cuT = self.wuT[:].bitcast(F16)[:, :, 0:FF]
        self.cdT = self.wdT[:].bitcast(F16)[:, :, 0:D]
        self.hscale = sb("hscale", [P, FB, 2])
        self.oscale = sb("oscale", [P, D])
        self.wqkvT = sb("wqkvT", [P, KC, 3 * D])
        self.woT = sb("woT", [P, KC, D])

    def clear_semaphores(self):
        self.nc.clear_and_free_semaphores(self.sems)
        self.nc.all_engine_barrier()
        self.sems = []

    def const(self, name):
        lo, hi = CONST[name]
        return self.consts[:, lo:hi]


def scope(core, ctx):
    nc = core.nc

    def sb(name, shape, dt=F32):
        return ctx.enter_context(nc.sbuf_tensor(name, shape, dt))

    def ps(name, shape, dt=F32):
        return ctx.enter_context(nc.psum_tensor(name, shape, dt))

    def sem(name, start=START):
        semaphore = nc.alloc_semaphore(name=name)
        if start:
            nc.sync.sem_inc(semaphore, start)
        core.sems.append(semaphore)
        return semaphore

    return sb, ps, sem


def prepare_phase(core):
    nc, dram = core.nc, core.dram
    with ExitStack() as ctx:
        sb, ps, sem = scope(core, ctx)
        qg = sb("p_qg", [P, FB, D], I32)
        qu = sb("p_qu", [P, FB, D], I32)
        qd = sb("p_qd", [P, KC, FF], I32)
        sg = sb("p_sg", [P, FB])
        su = sb("p_su", [P, FB])
        wn = sb("p_wn", [P, 4, KC, D])
        fg = sb("p_fg", [P, FB, D])
        fu = sb("p_fu", [P, FB, D])
        fd = sb("p_fd", [P, KC, FF])
        bn = sb("p_bn", [P, NT, 6])
        srows = sb("p_rows", [P, 3, FF])
        prod = sb("p_prod", [P, FF])
        ends = sb("p_ends", [P, 2])
        top = sb("p_top", [P, 1])
        inv = sb("p_inv", [P, 1])
        r_in, scaled, bned = sem("p_r_in"), sem("p_scaled"), sem("p_bned")
        tp = [ps(f"p_tp{i}", [P, 4, P]) for i in range(4)]
        c_in, q_in, s_in, w_in, x_in = sem("p_c_in"), sem("p_q_in"), sem("p_s_in", 0), sem("p_w_in"), [sem(f"p_x_in{b}") for b in range(B)]
        deq, turned, kept, stat = sem("p_deq"), sem("p_turned"), sem("p_kept"), sem("p_stat")

        jobs = []
        for q, (src, dst) in enumerate(((fg, core.cgT), (fu, core.cuT))):
            for kc in range(KC):
                for j in range(FB):
                    jobs.append((src[0:hid(j), j, kc * P:(kc + 1) * P], hid(j), P,
                                 dst[:, kc, j * P:j * P + hid(j)]))
        for j in range(FB):
            for kc in range(KC):
                jobs.append((fd[:, kc, j * P:j * P + hid(j)], P, hid(j), core.cdT[0:hid(j), j, kc * P:(kc + 1) * P]))
        nq = len(jobs)
        for w in range(4):
            dst = core.wqkvT if w < 3 else core.woT
            off = w * D if w < 3 else 0
            for kc in range(KC):
                for m in range(KC):
                    jobs.append((wn[:, w, m, kc * P:(kc + 1) * P], P, P,
                                 dst[:, kc, off + m * P:off + (m + 1) * P]))
        assert len(jobs) % 4 == 0

        nc.all_engine_barrier()
        with nc.Block() as block:
            @block.sync
            def _(sp):
                sp.dma_start(core.consts[:], dram["consts"]).then_inc(c_in, 16)
                for q, s, a, b in (("L0_ffn_wq_gate", "L0_ffn_s_gate", qg, sg), ("L0_ffn_wq_up", "L0_ffn_s_up", qu, su)):
                    full = (FB - 1) * P
                    sp.dma_start(a[:, 0:FB - 1, :], dram[q][0:full, :].rearrange("(j p) d -> p j d", p=P)).then_inc(q_in, 16)
                    sp.dma_start(a[0:hid(FB - 1), FB - 1, :], dram[q][full:FF, :]).then_inc(q_in, 16)
                sp.dma_start(qd[:], dram["L0_ffn_wq_down"].rearrange("(k p) f -> p k f", p=P)).then_inc(q_in, 16)
                for i, (name, w) in enumerate((("L0_ffn_s_gate", FF), ("L0_ffn_s_up", FF), ("L0_ffn_s_down", D))):
                    sp.dma_start(srows[:, i, 0:w], dram[name].rearrange("(a f) -> a f", a=1).to_broadcast([P, w])).then_inc(r_in, 16)
                for w, name in enumerate(("L0_attn_wq", "L0_attn_wk", "L0_attn_wv", "L0_attn_wo")):
                    sp.dma_start(wn[:, w], dram[name].rearrange("(m p) d -> p m d", p=P)).then_inc(w_in, 16)

            @block.gpsimd
            def _(pool):
                full = (FB - 1) * P
                for s, b in (("L0_ffn_s_gate", sg), ("L0_ffn_s_up", su)):
                    v = dram[s].rearrange("(f a) -> f a", a=1)
                    pool.dma_start(b[:, 0:FB - 1].rearrange("p (j a) -> p j a", a=1),
                                   v[0:full].rearrange("(j p) a -> p j a", p=P)).then_inc(s_in, 16)
                    pool.dma_start(b[0:hid(FB - 1), FB - 1:FB], v[full:FF]).then_inc(s_in, 16)

            @block.scalar
            def _(act):
                for b in range(B):
                    act.dma_start(core.x[:, b * TPB:(b + 1) * TPB, :],
                                  dram["L0_attn_x"][b].rearrange("(i p) d -> p i d", p=P)).then_inc(x_in[b], 16)
                for n in range(1, len(jobs) // 4, 2):
                    act.wait_ge(turned, START + n + 1)
                    for i in range(4):
                        _, rows, cols, dst = jobs[4 * n + i]
                        last = nc.scalar.activation(dst, tp[n % 4][0:cols, i, 0:rows], ACT.Copy)
                    last.then_inc(kept, 1)

            @block.vector
            def _(dve):
                nc.vector.memset(core.eps[:, 0:1], LN_EPS)
                nc.vector.memset(core.eps[:, 1:2], RMS_EPS)
                dve.wait_ge(c_in, START + 16)
                nc.vector.tensor_copy(core.ident_b[:], core.const("ident"))
                for t in range(NT):
                    if t % TPB == 0:
                        dve.wait_ge(x_in[t // TPB], START + 16)
                    nc.vector.bn_stats(bn[:, t, :], core.x[:, t, :]).then_inc(bned, 1)
                dve.wait_ge(q_in, START + 16 * 5)
                for q, f in ((qg, fg), (qu, fu)):
                    for j in range(FB):
                        r = hid(j)
                        nc.vector.tensor_scalar(f[0:r, j, :], q[0:r, j, :], ZERO_POINT, None, ALU.subtract).then_inc(deq, 1)
                for k in range(KC):
                    nc.vector.tensor_scalar(fd[:, k, :], qd[:, k, :], ZERO_POINT, None, ALU.subtract).then_inc(deq, 1)
                for n in range(0, len(jobs) // 4, 2):
                    dve.wait_ge(turned, START + n + 1)
                    for i in range(4):
                        _, rows, cols, dst = jobs[4 * n + i]
                        last = nc.vector.tensor_copy(dst, tp[n % 4][0:cols, i, 0:rows])
                    last.then_inc(stat, 1)
                dve.wait_ge(s_in, 16 * 4)
                for r, j in ((P, slice(0, FB - 1)), (hid(FB - 1), slice(FB - 1, FB))):
                    nc.vector.tensor_scalar(core.hscale[0:r, j, 0], sg[0:r, j], 0.5 / LIFT, None, ALU.mult)
                    nc.vector.scalar_tensor_tensor(out=core.hscale[0:r, j, 1], in0=sg[0:r, j], scalar=HLIFT / LIFT ** 2,
                                                   in1=su[0:r, j], op0=ALU.mult, op1=ALU.mult).then_inc(scaled, 1)
                dve.wait_ge(r_in, START + 16 * 3)
                nc.vector.tensor_tensor(prod[:], srows[:, 0], srows[:, 1], ALU.mult).then_inc(scaled, 1)
                dve.wait_ge(scaled, START + 3)
                nc.vector.tensor_reduce(ends[:, 0:1], prod[:], AX.X, ALU.max)
                nc.vector.tensor_reduce(ends[:, 1:2], prod[:], AX.X, ALU.min).then_inc(scaled, 1)
                dve.wait_ge(scaled, START + 4)
                nc.vector.scalar_tensor_tensor(out=top[:], in0=ends[:, 1:2], scalar=-1.0, in1=ends[:, 0:1],
                                               op0=ALU.mult, op1=ALU.max).then_inc(scaled, 1)
                dve.wait_ge(scaled, START + 5)
                nc.vector.tensor_scalar(top[:], top[:], 1e-30, None, ALU.max).then_inc(scaled, 1)
                dve.wait_ge(scaled, START + 6)
                nc.vector.reciprocal(inv[:], top[:]).then_inc(scaled, 1)
                dve.wait_ge(scaled, START + 7)
                for r, j in ((P, slice(0, FB - 1)), (hid(FB - 1), slice(FB - 1, FB))):
                    nc.vector.tensor_scalar(core.hscale[0:r, j, 1], core.hscale[0:r, j, 1], inv[0:r], None, ALU.mult)
                nc.vector.tensor_scalar(core.oscale[:], srows[:, 2, 0:D], top[:], 0.25 / HLIFT, ALU.mult, ALU.mult)
                for t in range(NT):
                    dve.wait_ge(bned, START + t + 1)
                    nc.vector.bn_aggr(core.mv[:, t, :], bn[:, t, :])

            @block.tensor
            def _(pe):
                pe.wait_ge(c_in, START + 16)
                for n in range(len(jobs) // 4):
                    if 4 * n < nq:
                        pe.wait_ge(deq, START + 2 * FB + KC)
                    else:
                        pe.wait_ge(w_in, START + 16 * 4)
                    if n >= 4:
                        k = n - 4
                        pe.wait_ge(stat if k % 2 == 0 else kept, START + k // 2 + 1)
                    for i in range(4):
                        src, rows, cols, _ = jobs[4 * n + i]
                        last = nc.tensor.transpose(tp[n % 4][0:cols, i, 0:rows], src, core.const("ident")[0:rows, 0:rows])
                    last.then_inc(turned, 1)


def ffn0_phase(core, tag):
    nc = core.nc
    with ExitStack() as ctx:
        sb, ps, sem = scope(core, ctx)
        xn = sb(tag + "xn", [P, CT, D])
        xh = sb(tag + "xh", [P, 2, KC, CW], F16)
        xl = sb(tag + "xl", [P, 2, KC, CW], F16)
        silu = sb(tag + "silu", [P, 2, CW])
        silu2 = sb(tag + "silu2", [P, 2, CW])
        silu2_s = sem(tag + "silu2")
        hT = sb(tag + "hT", [P, 2, CW])
        hh = sb(tag + "hh", [P, 2, FB, CW], F16)
        hl = sb(tag + "hl", [P, 2, FB, CW], F16)
        out = sb(tag + "out", [P, 2, D])
        hh_ready, hl_ready, out_s = sem(tag + "hh_s"), sem(tag + "hl_s"), sem(tag + "out_s")
        bn = sb(tag + "bn", [P, CT, 6])
        mv4 = sb(tag + "mv4", [P, CT, 2])
        sums = sb(tag + "sums", [P, CT, SUMS])
        mean = sb(tag + "mean", [P, CT])
        carrier = sb(tag + "carrier", [P, 1])
        meaned = sem(tag + "meaned")
        tp = ps(tag + "tp", [P, 2, KC, 2 * P])
        gate = ps(tag + "gate", [P, 2, CW])
        up = ps(tag + "up", [P, 2, CW])
        down = ps(tag + "down", [P, 2, 512])
        root, scales = sem(tag + "root"), sem(tag + "scales")
        normed, turned, xh_ready, xT_ready = (sem(tag + n) for n in ("normed", "turned", "xh_ready", "xT_ready"))
        gu_ready, silu_ready, h_ready = sem(tag + "gu"), sem(tag + "silu_s"), sem(tag + "h")
        down_ready, x_done, stats = sem(tag + "down_s"), sem(tag + "x_done"), sem(tag + "stats")
        ident = core.const("ident")

        nc.all_engine_barrier()
        with nc.Block() as block:
            def every(eng, chunk):
                chunk(0, 0, 2)
                with eng.Fori(0, (NCH - 4) // 2) as it:
                    for n in range(2):
                        chunk(it * 2 + n + 1, 1 - n, 2)
                for c in range(NCH - 3, NCH):
                    chunk(c, c % 2, NCH - 1 - c)

            @block.tensor
            def _(pe):
                def turn(c):
                    for i in range(CT):
                        pe.wait_ge(normed, START + c * CT + i + 1)
                        if i % 2 == 0:
                            if not (isinstance(c, int) and c == 0):
                                pe.wait_ge(xT_ready, START + (c - 1) * 2 + i // 2 + 1)
                        for k in range(KC):
                            last = nc.tensor.transpose(tp[:, i // 2, k, (i % 2) * P:(i % 2 + 1) * P],
                                                       xn[:, i, k * P:(k + 1) * P], ident)
                        last.then_inc(turned, 1)

                def gate_up(c, s, j):
                    r = hid(j)
                    if j == 0:
                        pe.wait_ge(xT_ready, START + c * 2 + 2)
                    if j or not (isinstance(c, int) and c == 0):
                        pe.wait_ge(h_ready, START + c * FB + j - 1)
                    for w, acc in ((core.cgT, gate), (core.cuT, up)):
                        for k in range(KC):
                            for part in (xh, xl):
                                last = nc.tensor.matmul(acc[0:r, j % 2, :], w[:, k, j * P:j * P + r], part[:, s, k, :],
                                                        start=(k == 0 and part is xh), stop=(k == KC - 1 and part is xl))
                    last.then_inc(gu_ready, 1)

                def down_proj(c, s, i):
                    if i == 0:
                        pe.wait_ge(hl_ready, START + c * FB + FB)
                    pe.wait_ge(out_s, START + c * CT + max(i - 1, 0))
                    for j in range(FB):
                        r = hid(j)
                        for part in (hh, hl):
                            last = nc.tensor.matmul(down[:, i % 2, 0:D], part[0:r, s, j, i * P:(i + 1) * P], core.cdT[0:r, j, :],
                                                    start=(j == 0 and part is hh), stop=(j == FB - 1 and part is hl))
                    last.then_inc(down_ready, 1)

                def chunk(c, s, ahead):
                    for j in range(FB):
                        gate_up(c, s, j)
                        if 1 <= j <= CT and not (isinstance(c, int) and c == 0):
                            down_proj(c - 1, 1 - s, j - 1)
                        if j == 2 and ahead:
                            turn(c + 1)

                turn(0)
                every(pe, chunk)
                for i in range(CT):
                    down_proj(NCH - 1, 1, i)

            @block.gpsimd
            def _(pool):
                def add(c, i):
                    t = c * CT + i
                    pool.wait_ge(out_s, START + t + 1)
                    nc.gpsimd.tensor_tensor(at(core.x, t), out[:, i % 2, :], at(core.x, t), ALU.add).then_inc(x_done, 1)

                def chunk(c, s, ahead):
                    for j in range(FB):
                        if 1 <= j <= CT and not (isinstance(c, int) and c == 0):
                            add(c - 1, j - 1)
                        r = hid(j)
                        pool.wait_ge(hh_ready, START + c * FB + j + 1)
                        nc.gpsimd.tensor_tensor(hl[0:r, s, j, :], hT[0:r, j % 2, :], hh[0:r, s, j, :], ALU.subtract).then_inc(hl_ready, 1)

                every(pool, chunk)
                for i in range(CT):
                    add(NCH - 1, i)

            @block.scalar
            def _(act):
                nc.scalar.activation(core.rstd[:], core.mv[:, :, 1], ACT.Sqrt, bias=core.eps[:, 0:1]).then_inc(root, 1)

                def keep_xT(c, s):
                    for b in range(2):
                        act.wait_ge(turned, START + c * CT + 2 * b + 2)
                        nc.scalar.activation(xh[:, s, :, b * 2 * P:(b + 1) * 2 * P], tp[:, b], ACT.Copy).then_inc(xh_ready, 1)

                def upper_part(c, s, j):
                    r = hid(j)
                    act.wait_ge(h_ready, START + c * FB + j + 1)
                    nc.scalar.activation(hh[0:r, s, j, :], hT[0:r, j % 2, :], ACT.Copy).then_inc(hh_ready, 1)

                def tanh(c, j):
                    r = hid(j)
                    act.wait_ge(gu_ready, START + c * FB + j + 1)
                    if j or not (isinstance(c, int) and c == 0):
                        act.wait_ge(h_ready, START + c * FB + j - 1)
                    nc.scalar.activation(silu[0:r, j % 2, :], gate[0:r, j % 2, :], ACT.Tanh,
                                         scale=core.hscale[0:r, j, 0:1]).then_inc(silu_ready, 1)

                def chunk(c, s, ahead):
                    for j in range(FB):
                        tanh(c, j)
                        if j:
                            upper_part(c, s, j - 1)
                        if j == 3 and ahead:
                            keep_xT(c + 1, 1 - s)
                    upper_part(c, s, FB - 1)

                keep_xT(0, 0)
                every(act, chunk)

            @block.vector
            def _(dve):
                dve.wait_ge(root, START + 1)
                nc.vector.reciprocal(core.rstd[:], core.rstd[:]).then_inc(scales, 1)
                dve.wait_ge(scales, START + 1)
                nc.vector.tensor_scalar(core.rstd[:], core.rstd[:], LIFT, None, ALU.mult).then_inc(scales, 1)
                dve.wait_ge(scales, START + 2)

                def means(c):
                    dve.wait_ge(normed, START + c * CT)
                    own = core.x[:, bass.ds(c * CT, CT), :].rearrange("p i (a d) -> p i a d", a=SUMS)
                    nc.vector.tensor_reduce(sums[:], own, AX.X, ALU.add).then_inc(meaned, 1)
                    dve.wait_ge(meaned, START + c * 3 + 1)
                    nc.vector.tensor_reduce(mean[:], sums[:], AX.X, ALU.add).then_inc(meaned, 1)
                    dve.wait_ge(meaned, START + c * 3 + 2)
                    nc.vector.tensor_scalar(mean[:], mean[:], 1.0 / D, None, ALU.mult).then_inc(meaned, 1)

                def normalise(c, i):
                    t = c * CT + i
                    if i == 0:
                        if not (isinstance(c, int) and c == 0):
                            dve.wait_ge(turned, START + c * CT)
                        dve.wait_ge(meaned, START + (c + 1) * 3)
                    nc.vector.tensor_scalar(xn[:, i, :], at(core.x, t), mean[:, i:i + 1],
                                            col(core.rstd, t), ALU.subtract, ALU.mult).then_inc(normed, 1)

                def hidden(c, j):
                    r = hid(j)
                    dve.wait_ge(silu_ready, START + c * FB + j + 1)
                    nc.vector.scalar_tensor_tensor(out=silu2[0:r, j % 2, :], in0=silu[0:r, j % 2, :], scalar=1.0,
                                                   in1=gate[0:r, j % 2, :], op0=ALU.add, op1=ALU.mult).then_inc(silu2_s, 1)
                    dve.wait_ge(silu2_s, START + c * FB + j + 1)
                    if j or not (isinstance(c, int) and c == 0):
                        dve.wait_ge(hl_ready, START + c * FB + j - 1)
                    nc.vector.scalar_tensor_tensor(out=hT[0:r, j % 2, :], in0=silu2[0:r, j % 2, :], scalar=core.hscale[0:r, j, 1:2],
                                                   in1=up[0:r, j % 2, :], op0=ALU.mult, op1=ALU.mult).then_inc(h_ready, 1)

                def lower_parts(c, s):
                    for b in range(2):
                        dve.wait_ge(xh_ready, START + c * 2 + b + 1)
                        cols = slice(b * 2 * P, (b + 1) * 2 * P)
                        nc.vector.tensor_tensor(xl[:, s, :, cols], tp[:, b], xh[:, s, :, cols], ALU.subtract).then_inc(xT_ready, 1)

                def residual(c, i):
                    t = c * CT + i
                    dve.wait_ge(down_ready, START + t + 1)
                    dve.wait_ge(x_done, START + c * CT + max(i - 1, 0))
                    nc.vector.tensor_tensor(out[:, i % 2, :], down[:, i % 2, 0:D], core.oscale[:], ALU.mult).then_inc(out_s, 1)

                def statistics(c, i):
                    dve.wait_ge(scales, START + 1)
                    dve.wait_ge(x_done, START + c * CT + i + 1)
                    nc.vector.bn_stats(bn[:, i, :], at(core.x, c * CT + i)).then_inc(stats, 1)

                def aggregate(c):
                    dve.wait_ge(stats, START + c * (CT + 1) + CT)
                    nc.vector.memset(carrier[:], 0.0)
                    for i in range(CT):
                        last = nc.vector.bn_aggr(mv4[:, i, :], bn[:, i, :])
                    last.then_inc(stats, 1)
                    dve.wait_ge(stats, START + (c + 1) * (CT + 1))
                    nc.vector.tensor_copy(core.mv[:, bass.ds(c * CT, CT), :], mv4[:])

                def chunk(c, s, ahead):
                    for j in range(FB):
                        hidden(c, j)
                        before = not (isinstance(c, int) and c == 0)
                        if 1 <= j <= CT and before:
                            residual(c - 1, j - 1)
                            if j > 1:
                                statistics(c - 1, j - 2)
                        if j == 4 and ahead:
                            lower_parts(c + 1, 1 - s)
                        if j == 2 and ahead > 1:
                            means(c + 2)
                        if j in (3, 5) and ahead > 1:
                            normalise(c + 2, j - 3)
                            normalise(c + 2, j - 2)
                    if before:
                        statistics(c - 1, CT - 1)
                        aggregate(c - 1)

                means(0)
                for i in range(CT):
                    normalise(0, i)
                means(1)
                lower_parts(0, 0)
                for i in range(CT):
                    normalise(1, i)
                every(dve, chunk)
                for i in range(CT):
                    residual(NCH - 1, i)
                for i in range(CT):
                    statistics(NCH - 1, i)
                aggregate(NCH - 1)


def mixture_dense_phase(core, tag, acc, load):
    nc, dram = core.nc, core.dram
    NR = NE + 1
    with ExitStack() as ctx:
        sb, ps, sem = scope(core, ctx)
        xn = sb(tag + "xn", [P, CT, D])
        xT = sb(tag + "xT", [P, 2, KC, CW])
        silu = sb(tag + "silu", [P, 2, CW])
        silu2 = sb(tag + "silu2", [P, 2, CW])
        silu2_s = sem(tag + "silu2")
        hT = sb(tag + "hT", [P, FB, CW])
        wn = sb(tag + "wn", [P, KC])
        wr = sb(tag + "wr", [P, KC, NR])
        both = sb(tag + "both", [P, NT])
        keep = sb(tag + "keep", [P, NT])
        shift = sb(tag + "shift", [P, NT])
        tmp = sb(tag + "tmp", [P, NT])
        zero = sb(tag + "zero", [P, D])
        empty = sb(tag + "empty", [P, NE, 2], I32)
        tri = sb(tag + "tri", [P, P], BF16)
        ones = sb(tag + "ones", [P, P], BF16)
        lg = sb(tag + "lg", [P, CT, NR])
        lmax = sb(tag + "lmax", [P, CT])
        prob = sb(tag + "prob", [P, CT, NE])
        psum_ = sb(tag + "psum", [P, CT])
        hgate = sb(tag + "hgate", [P, CT])
        top = sb(tag + "top", [P, CT, 8])
        topi = sb(tag + "topi", [P, CT, 8], U32)
        topf = sb(tag + "topf", [P, CT, TOPK])
        hot = sb(tag + "hot", [P, CT, TOPK, NE])
        hotr = sb(tag + "hotr", [P, CT, TOPK, NE])
        count = sb(tag + "count", [P, CT, NE])
        mask = sb(tag + "mask", [P, CT, NE], BF16)
        before_ = sb(tag + "before", [P, CT + 1, NE], BF16)
        pos = sb(tag + "pos", [P, CT, TOPK])
        over = sb(tag + "over", [P, CT, TOPK])
        dest = sb(tag + "dest", [P, CT, TOPK], I32)
        entry = sb(tag + "entry", [P, CT, TOPK, 2], I32)
        tp = ps(tag + "tp", [P, 2, KC, 2 * P])
        gate = ps(tag + "gate", [P, 2, CW])
        up = ps(tag + "up", [P, 2, CW])
        down = ps(tag + "down", [P, 2, 512])
        logits = down[:, 0, D:D + CT * NR].rearrange("p (i e) -> p i e", i=CT)
        ranks = down[:, 1, D:D + CT * NE].rearrange("p (i e) -> p i e", i=CT)
        names = ("w_in root1 root2 scales setup tables normed xn_sent turned xT_ready logit_s gu silu_s h_s down_s x_done "
                 "acc_sent shifted exp_s route masked ranked dest_ready placed lg_kept ranks_used gated posted")
        (w_in, root1, root2, scales, setup, tables, normed, xn_sent, turned, xT_ready, logit_s, gu_ready, silu_ready,
         h_ready, down_ready, x_done, acc_sent, shifted, exp_s, route, masked, ranked, dest_ready,
         placed, lg_kept, ranks_used, gated, posted) = (sem(tag + n, 0 if n == "placed" else START) for n in names.split())
        ident = core.const("ident")
        STEPS = 15

        nc.all_engine_barrier()
        with nc.Block() as block:
            @block.sync
            def _(sp):
                full = (FB - 1) * P
                if load:
                    sp.dma_start(core.wgT[:], dram["L1_ffn_sw_gate"].rearrange("(k p) f -> p k f", p=P)).then_inc(w_in, 16)
                    sp.dma_start(core.wuT[:], dram["L1_ffn_sw_up"].rearrange("(k p) f -> p k f", p=P)).then_inc(w_in, 16)
                    sp.dma_start(core.wdT[:, 0:FB - 1, :], dram["L1_ffn_sw_down"][0:full].rearrange("(j p) d -> p j d", p=P)).then_inc(w_in, 16)
                    sp.dma_start(core.wdT[0:hid(FB - 1), FB - 1, :], dram["L1_ffn_sw_down"][full:FF]).then_inc(w_in, 16)
                sp.dma_start(wr[:, :, 0:NE], dram["L1_ffn_w_router"].rearrange("(k p) e -> p k e", p=P)).then_inc(w_in, 16)
                sp.dma_start(wr[:, :, NE:NR], dram["L1_ffn_w_shared_gate"].rearrange("(k p) e -> p k e", p=P)).then_inc(w_in, 16)
                sp.dma_start(wn[:].rearrange("p (k a) -> p k a", a=1),
                             dram["L1_ffn_w_norm"].rearrange("(k p a) -> p k a", p=P, a=1)).then_inc(w_in, 16)
                sp.wait_ge(setup, START + 1)
                sp.dma_start(dram["xn"][NTOK:NTOK + TRASH, :], zero[:]).then_inc(tables, 16)
                sp.dma_start(acc[NTOK:NTOK + TRASH, :], zero[:]).then_inc(tables, 16)
                sp.dma_start(dram["table"].rearrange("(e s) w -> s e w", e=NE), empty[:]).then_inc(tables, 16)

                def send_xn(c):
                    sp.wait_ge(normed, START + (c + 1) * CT)
                    sp.dma_start(dram["xn"][bass.ds(c * CW, CW), :].rearrange("(i p) d -> p i d", p=P), xn[:]).then_inc(xn_sent, 16)

                def send_x(c):
                    sp.wait_ge(x_done, START + (c + 1) * CT)
                    sp.dma_start(acc[bass.ds(c * CW, CW), :].rearrange("(i p) d -> p i d", p=P),
                                 core.x[:, bass.ds(c * CT, CT), :]).then_inc(acc_sent, 16)

                send_xn(0)
                with sp.Fori(0, NCH - 1) as c:
                    send_xn(c + 1)
                    send_x(c)
                send_x(NCH - 1)
                sp.wait_ge(xn_sent, START + 16 * NCH)
                sp.wait_ge(acc_sent, START + 16 * NCH)

            @block.gpsimd
            def _(pool):
                pool.wait_ge(tables, START + 48)
                with pool.Fori(0, NCH) as c:
                    pool.wait_ge(dest_ready, START + c + 1)
                    pool.sem_inc(posted, 1)
                    for i in range(CT):
                        for k in range(TOPK):
                            nc.gpsimd.indirect_dma_start(
                                out=dram["table"], out_offset=bass.IndirectOffsetOnAxis(ap=dest[:, i, k:k + 1], axis=0),
                                in_=entry[:, i, k, :], in_offset=None,
                                bounds_check=NE * CAP - 1, oob_is_err=False).then_inc(placed, 16)
                pool.wait_ge(placed, 16 * NCH * CT * TOPK)

            @block.tensor
            def _(pe):
                def turn(c):
                    for i in range(CT):
                        pe.wait_ge(normed, START + c * CT + i + 1)
                        if i % 2 == 0 and not (isinstance(c, int) and c == 0):
                            pe.wait_ge(xT_ready, START + (c - 1) * 2 + i // 2 + 1)
                        for k in range(KC):
                            last = nc.tensor.transpose(tp[:, i // 2, k, (i % 2) * P:(i % 2 + 1) * P],
                                                       xn[:, i, k * P:(k + 1) * P], ident)
                        last.then_inc(turned, 1)

                def route_logits(c, s):
                    pe.wait_ge(xT_ready, START + c * 2 + 2)
                    pe.wait_ge(route, START + c * STEPS)
                    pe.wait_ge(exp_s, START + c * 2)
                    pe.wait_ge(x_done, START + c * CT)
                    for i in range(CT):
                        for k in range(KC):
                            last = nc.tensor.matmul(logits[:, i, :], xT[:, s, k, i * P:(i + 1) * P], wr[:, k, :],
                                                    start=(k == 0), stop=(k == KC - 1))
                    last.then_inc(logit_s, 1)

                def rank(c):
                    pe.wait_ge(masked, START + c + 1)
                    for i in range(CT):
                        nc.tensor.matmul(ranks[:, i, :], tri[:], mask[:, i, :], start=True, stop=False)
                        last = nc.tensor.matmul(ranks[:, i, :], ones[:], before_[:, i, :], start=False, stop=True)
                    last.then_inc(ranked, 1)

                def gate_up(c, s):
                    for j in range(FB):
                        r = hid(j)
                        pe.wait_ge(h_ready, START + c * FB + max(j - 1, 0))
                        for w, out in ((core.wgT, gate), (core.wuT, up)):
                            for k in range(KC):
                                last = nc.tensor.matmul(out[0:r, j % 2, :], w[:, k, j * P:j * P + r], xT[:, s, k, :],
                                                        start=(k == 0), stop=(k == KC - 1))
                        last.then_inc(gu_ready, 1)
                        if j == 4:
                            rank(c)

                def down_proj(c):
                    pe.wait_ge(lg_kept, START + c + 1)
                    pe.wait_ge(ranks_used, START + c + 1)
                    for i in range(CT):
                        pe.wait_ge(x_done, START + c * CT + max(i - 1, 0))
                        for j in range(FB):
                            r = hid(j)
                            if i == 0:
                                pe.wait_ge(h_ready, START + c * FB + j + 1)
                            last = nc.tensor.matmul(down[:, i % 2, 0:D], hT[0:r, j, i * P:(i + 1) * P],
                                                    core.wdT[0:r, j, :], start=(j == 0), stop=(j == FB - 1))
                        last.then_inc(down_ready, 1)

                def chunk(c, s, ahead):
                    route_logits(c, s)
                    gate_up(c, s)
                    if ahead:
                        turn(c + 1)
                    down_proj(c)

                pe.wait_ge(w_in, START + 16 * (7 if load else 3))
                pe.wait_ge(setup, START + 2)
                turn(0)
                with pe.Fori(0, NCH // 2 - 1) as it:
                    for s in range(2):
                        chunk(it * 2 + s, s, True)
                chunk(NCH - 2, 0, True)
                chunk(NCH - 1, 1, False)

            @block.scalar
            def _(act):
                nc.scalar.activation(core.rstd[:], core.mv[:, :, 1], ACT.Sqrt, bias=core.eps[:, 0:1]).then_inc(root1, 1)
                act.wait_ge(scales, START + 3)
                nc.scalar.activation(both[:], tmp[:], ACT.Sqrt, bias=core.eps[:, 1:2]).then_inc(root2, 1)
                act.wait_ge(w_in, START + 16 * (7 if load else 3))

                def keep_xT(c, s):
                    for b in range(2):
                        act.wait_ge(turned, START + c * CT + 2 * b + 2)
                        for k in range(KC):
                            last = nc.scalar.activation(xT[:, s, k, b * 2 * P:(b + 1) * 2 * P], tp[:, b, k, :], ACT.Copy,
                                                        scale=wn[:, k:k + 1])
                        last.then_inc(xT_ready, 1)

                def route_exps(c):
                    act.wait_ge(lg_kept, START + c + 1)
                    act.wait_ge(x_done, START + c * CT)
                    nc.scalar.activation(hgate[:], lg[:, :, NE], ACT.Exp, scale=-1.0).then_inc(exp_s, 1)
                    act.wait_ge(shifted, START + c + 1)
                    nc.scalar.activation(prob[:], prob[:], ACT.Exp).then_inc(exp_s, 1)

                def silus(c):
                    for j in range(FB):
                        r = hid(j)
                        if j == 1:
                            route_exps(c)
                        act.wait_ge(gu_ready, START + c * FB + j + 1)
                        act.wait_ge(h_ready, START + c * FB + max(j - 1, 0))
                        nc.scalar.activation(silu[0:r, j % 2, :], gate[0:r, j % 2, :], ACT.Tanh, scale=0.5).then_inc(silu_ready, 1)

                keep_xT(0, 0)
                with act.Fori(0, NCH // 2 - 1) as it:
                    for s in range(2):
                        silus(it * 2 + s)
                        keep_xT(it * 2 + s + 1, 1 - s)
                silus(NCH - 2)
                keep_xT(NCH - 1, 1)
                silus(NCH - 1)

            @block.vector
            def _(dve):
                nc.vector.memset(zero[:], 0.0)
                nc.vector.memset(empty[:, :, 1], 0)
                nc.vector.tensor_copy(empty[:, :, 0], core.const("slot")).then_inc(setup, 1)
                nc.vector.memset(before_[:, CT, :], 0.0)
                nc.vector.memset(ones[:], 1.0)
                nc.vector.tensor_copy(tri[:], core.const("tri")).then_inc(setup, 1)
                steps = 0

                def scale_step(instruction):
                    nonlocal steps
                    steps += 1
                    instruction.then_inc(scales, 1)
                    dve.wait_ge(scales, START + steps)

                dve.wait_ge(root1, START + 1)
                scale_step(nc.vector.reciprocal(core.rstd[:], core.rstd[:]))
                scale_step(nc.vector.tensor_tensor(tmp[:], core.rstd[:], core.mv[:, :, 1], ALU.mult))
                scale_step(nc.vector.tensor_tensor(tmp[:], tmp[:], core.rstd[:], ALU.mult))
                dve.wait_ge(root2, START + 1)
                scale_step(nc.vector.reciprocal(both[:], both[:]))
                scale_step(nc.vector.tensor_tensor(both[:], both[:], core.rstd[:], ALU.mult))
                scale_step(nc.vector.tensor_scalar(keep[:], core.rstd[:], 0.5, 1.0, ALU.mult, ALU.add))
                scale_step(nc.vector.tensor_tensor(shift[:], core.rstd[:], core.mv[:, :, 0], ALU.mult))
                scale_step(nc.vector.tensor_scalar(shift[:], shift[:], -0.5, None, ALU.mult))

                def normalise(c, i):
                    t = c * CT + i
                    if not (isinstance(c, int) and c == 0):
                        dve.wait_ge(turned, START + (c - 1) * CT + i + 1)
                        dve.wait_ge(xn_sent, START + c * 16)
                    nc.vector.tensor_scalar(xn[:, i, :], at(core.x, t), at(core.mv, t)[:, 0:1],
                                            col(both, t), ALU.subtract, ALU.mult).then_inc(normed, 1)

                def hidden(c, j):
                    r = hid(j)
                    dve.wait_ge(silu_ready, START + c * FB + j + 1)
                    if j == 0:
                        dve.wait_ge(down_ready, START + c * CT)
                    nc.vector.scalar_tensor_tensor(out=silu2[0:r, j % 2, :], in0=silu[0:r, j % 2, :], scalar=1.0,
                                                   in1=gate[0:r, j % 2, :], op0=ALU.add, op1=ALU.mult).then_inc(silu2_s, 1)
                    dve.wait_ge(silu2_s, START + c * FB + j + 1)
                    nc.vector.tensor_tensor(hT[0:r, j, :], silu2[0:r, j % 2, :], up[0:r, j % 2, :],
                                            ALU.mult).then_inc(h_ready, 1)

                def residual(c, ahead):
                    for i in range(CT):
                        t = c * CT + i
                        nc.vector.tensor_scalar(at(core.x, t), at(core.x, t), col(keep, t), col(shift, t),
                                                ALU.mult, ALU.add).then_inc(setup, 1)
                    for i in range(CT):
                        t = c * CT + i
                        dve.wait_ge(setup, START + t + 3)
                        dve.wait_ge(down_ready, START + t + 1)
                        nc.vector.scalar_tensor_tensor(out=at(core.x, t), in0=down[:, i % 2, 0:D], scalar=hgate[:, i:i + 1],
                                                       in1=at(core.x, t), op0=ALU.mult, op1=ALU.add).then_inc(x_done, 1)
                        if ahead:
                            normalise(c + 2, i)

                done = 0

                def link(c, instruction):
                    nonlocal done
                    done += 1
                    instruction.then_inc(route, 1)
                    dve.wait_ge(route, START + c * STEPS + done)

                def shift_logits(c):
                    dve.wait_ge(logit_s, START + c + 1)
                    nc.vector.tensor_copy(lg[:], logits).then_inc(lg_kept, 1)
                    dve.wait_ge(lg_kept, START + c + 1)
                    link(c, nc.vector.tensor_reduce(lmax[:], lg[:, :, 0:NE], AX.X, ALU.max))
                    nc.vector.tensor_tensor(prob[:], lg[:, :, 0:NE], spread(lmax[:], 2, NE), ALU.subtract).then_inc(shifted, 1)

                def choose(c):
                    dve.wait_ge(exp_s, START + 2 * c + 2)
                    link(c, nc.vector.tensor_reduce(psum_[:], prob[:], AX.X, ALU.add))
                    link(c, nc.vector.reciprocal(psum_[:], psum_[:]))
                    link(c, nc.vector.tensor_tensor(prob[:], prob[:], spread(psum_[:], 2, NE), ALU.mult))
                    nc.vector.tensor_scalar(hgate[:], hgate[:], 4.0, 4.0, ALU.mult, ALU.add).then_inc(gated, 1)
                    for i in range(CT):
                        last = nc.vector.max(top[:, i, :], prob[:, i, :])
                    link(c, last)
                    dve.wait_ge(gated, START + c + 1)
                    nc.vector.reciprocal(hgate[:], hgate[:])
                    for i in range(CT):
                        last = nc.vector.max_index(topi[:, i, :], top[:, i, :], prob[:, i, :])
                    link(c, last)

                def count_experts(c):
                    link(c, nc.vector.tensor_copy(topf[:], topi[:, :, 0:TOPK]))
                    expert = spread(spread(core.const("expert"), 1, TOPK), 1, CT)
                    link(c, nc.vector.tensor_tensor(hot[:], expert, spread(topf[:], 3, NE), ALU.is_equal))
                    link(c, nc.vector.tensor_reduce(count[:], hot[:].rearrange("p i k e -> p i e k"), AX.X, ALU.add))
                    nc.vector.tensor_copy(mask[:], count[:])
                    link(c, nc.vector.tensor_copy(before_[:, 0, :], before_[:, CT, :]))
                    for i in range(CT):
                        last = nc.vector.tensor_tensor(before_[:, i + 1, :], before_[:, i, :], mask[:, i, :], ALU.add)
                        if i < CT - 1:
                            link(c, last)
                    last.then_inc(masked, 1)

                def place(c):
                    dve.wait_ge(ranked, START + c + 1)
                    if not (isinstance(c, int) and c == 0):
                        dve.wait_ge(placed, c * 16 * CT * TOPK)
                    nc.vector.tensor_tensor(hotr[:], hot[:], spread(ranks, 2, TOPK), ALU.mult).then_inc(ranks_used, 1)
                    dve.wait_ge(ranks_used, START + c + 1)
                    link(c, nc.vector.tensor_reduce(pos[:], hotr[:], AX.X, ALU.add))
                    nc.vector.tensor_scalar(over[:], pos[:], float(CAP), float(2 * NE * CAP), ALU.is_ge, ALU.mult)
                    link(c, nc.vector.scalar_tensor_tensor(out=pos[:], in0=topf[:], scalar=float(CAP), in1=pos[:],
                                                           op0=ALU.mult, op1=ALU.add))
                    nc.vector.tensor_copy(entry[:, :, :, 0], spread(core.const("token")[:, bass.ds(c * CT, CT)], 2, TOPK))
                    nc.vector.tensor_copy(entry[:].bitcast(F32)[:, :, :, 1], top[:, :, 0:TOPK])
                    nc.vector.tensor_tensor(dest[:], pos[:], over[:], ALU.add).then_inc(dest_ready, 1)

                def chunk(c, ahead):
                    nonlocal done
                    done = 0
                    hidden(c, 0)
                    shift_logits(c)
                    hidden(c, 1)
                    choose(c)
                    hidden(c, 2)
                    count_experts(c)
                    hidden(c, 3)
                    hidden(c, 4)
                    place(c)
                    assert done == STEPS, done
                    hidden(c, 5)
                    residual(c, ahead > 1)

                for c in range(2):
                    for i in range(CT):
                        normalise(c, i)
                chunk(0, NCH - 1)
                with dve.Fori(1, NCH - 2) as c:
                    chunk(c, 2)
                chunk(NCH - 2, 1)
                chunk(NCH - 1, 0)


def experts_phase(core, tag, acc):
    nc, dram = core.nc, core.dram
    with ExitStack() as ctx:
        sb, ps, sem = scope(core, ctx)
        wn = sb(tag + "wn", [P, KC])
        table = sb(tag + "table", [P, NE, 2], I32)
        gidx = sb(tag + "gidx", [P, DEEP], I32)
        sidx = sb(tag + "sidx", [P, 2], I32)
        wgu = sb(tag + "wgu", [P, DEEP, KC, 2 * EF])
        wd = sb(tag + "wd", [EH, DEEP, 2, D])
        xg = sb(tag + "xg", [P, DEEP, D])
        xgT = sb(tag + "xgT", [P, 2, KC, P])
        silu = sb(tag + "silu", [P, 2, EF])
        silu2 = sb(tag + "silu2", [P, 2, EF])
        silu2_s = sem(tag + "silu2")
        h = sb(tag + "h", [P, 2, EF])
        hT = sb(tag + "hT", [EH, 2, 2, P])
        ys = sb(tag + "ys", [P, 2, D])
        tp = ps(tag + "tp", [P, 2, 512])
        gu = ps(tag + "gu", [P, 2, 512])
        ht = ps(tag + "ht", [P, 2, 512])
        dn = ps(tag + "dn", [P, 2, 512])
        names = "small_in gidx_s turned xgT_s gu_s silu_s h_s h_turned hT_s dn_s y_s added posted"
        (small_in, gidx_s, turned, xgT_s, gu_s, silu_s, h_s, h_turned, hT_s, dn_s, y_s,
         added, posted) = (sem(tag + n, 0 if n == "added" else START) for n in names.split())
        w_slot = [sem(f"{tag}w_slot{s}") for s in range(DEEP)]
        gathered = [sem(f"{tag}gathered{s}", 0) for s in range(DEEP)]
        ident = core.const("ident")

        def every(eng, body):
            for s in range(DEEP):
                body(0, s, s)
            with eng.Fori(1, NE // DEEP - 1) as it:
                for s in range(DEEP):
                    body(it, it * DEEP + s, s)
            for s in range(DEEP):
                body(NE // DEEP - 1, NE - DEEP + s, s)

        def within(e, n):
            return not isinstance(e, int) or e + n < NE

        nc.all_engine_barrier()
        with nc.Block() as block:
            @block.sync
            def _(sp):
                sp.dma_start(table[:], dram["table"].rearrange("(e s) w -> s e w", e=NE)).then_inc(small_in, 16)
                sp.dma_start(wn[:].rearrange("p (k a) -> p k a", a=1),
                             dram["L1_ffn_w_norm"].rearrange("(k p a) -> p k a", p=P, a=1)).then_inc(small_in, 16)

                def load(e, s):
                    for w, name in enumerate(("L1_ffn_w_gate", "L1_ffn_w_up")):
                        sp.dma_start(wgu[:, s, :, w * EF:(w + 1) * EF],
                                     dram[name][bass.ds(e, 1)].rearrange("a (k p) f -> p (a k) f", p=P)).then_inc(w_slot[s], 16)
                    sp.dma_start(wd[:, s], dram["L1_ffn_w_down"][bass.ds(e, 1)].rearrange("a (h f) d -> f (a h) d", h=2)).then_inc(w_slot[s], 16)

                for s in range(DEEP):
                    load(s, s)
                with sp.Fori(1, NE // DEEP) as it:
                    for s in range(DEEP):
                        sp.wait_ge(dn_s, START + (it - 1) * DEEP + s + 1)
                        load(it * DEEP + s, s)

            @block.gpsimd
            def _(pool):
                def gather(e, s):
                    pool.wait_ge(gidx_s, START + e + 1)
                    pool.sem_inc(posted, 1)
                    nc.gpsimd.indirect_dma_start(out=xg[:, s, :], out_offset=None, in_=dram["xn"],
                                                 in_offset=bass.IndirectOffsetOnAxis(ap=gidx[:, s:s + 1], axis=0),
                                                 bounds_check=NTOK + TRASH - 1, oob_is_err=True).then_inc(gathered[s], 16)

                def add(e, s):
                    pool.wait_ge(y_s, START + e + 1)
                    if not (isinstance(e, int) and e == 0):
                        pool.wait_ge(added, 16 * e)
                    pool.sem_inc(posted, 1)
                    nc.gpsimd.indirect_dma_start(out=acc, out_offset=bass.IndirectOffsetOnAxis(ap=sidx[:, s % 2:s % 2 + 1], axis=0),
                                                 in_=ys[:, s % 2, :], in_offset=None, compute_op=ALU.add,
                                                 bounds_check=NTOK + TRASH - 1, oob_is_err=True).then_inc(added, 16)

                for s in range(DEEP):
                    gather(s, s)

                def body(it, e, s):
                    add(e, s)
                    if within(e, DEEP):
                        gather(e + DEEP, s)

                every(pool, body)
                pool.wait_ge(added, 16 * NE)

            @block.tensor
            def _(pe):
                def turn(it, e, s):
                    pe.wait_ge(gathered[s], 16 * (it + 1))
                    for k in range(KC):
                        last = nc.tensor.transpose(tp[:, s % 2, k * P:(k + 1) * P], xg[:, s, k * P:(k + 1) * P], ident)
                    last.then_inc(turned, 1)

                def gate_up(it, e, s):
                    pe.wait_ge(xgT_s, START + e + 1)
                    pe.wait_ge(w_slot[s], START + 48 * (it + 1))
                    if not (isinstance(e, int) and e < 2):
                        pe.wait_ge(h_s, START + e - 1)
                    for k in range(KC):
                        last = nc.tensor.matmul(gu[:, s % 2, 0:2 * EF], xgT[:, s % 2, k, :], wgu[:, s, k, :],
                                                start=(k == 0), stop=(k == KC - 1))
                    last.then_inc(gu_s, 1)

                def turn_h(e, s):
                    pe.wait_ge(h_s, START + e + 1)
                    for half in range(2):
                        last = nc.tensor.transpose(ht[0:EH, s % 2, half * P:(half + 1) * P],
                                                   h[:, s % 2, half * EH:(half + 1) * EH], ident)
                    last.then_inc(h_turned, 1)

                def down(e, s):
                    pe.wait_ge(hT_s, START + e + 1)
                    if not (isinstance(e, int) and e < 2):
                        pe.wait_ge(y_s, START + e - 1)
                    for half in range(2):
                        last = nc.tensor.matmul(dn[:, s % 2, 0:D], hT[:, s % 2, half, :], wd[:, s, half, :],
                                                start=(half == 0), stop=(half == 1))
                    last.then_inc(dn_s, 1)

                def body(it, e, s):
                    if within(e, 1):
                        gate_up(it + (s + 1) // DEEP, e + 1, (s + 1) % DEEP)
                    turn_h(e, s)
                    if within(e, 2):
                        turn(it + (s + 2) // DEEP, e + 2, (s + 2) % DEEP)
                    down(e, s)

                turn(0, 0, 0)
                turn(0, 1, 1)
                gate_up(0, 0, 0)
                every(pe, body)

            @block.scalar
            def _(act):
                act.wait_ge(small_in, START + 32)

                def keep(e, s):
                    act.wait_ge(turned, START + e + 1)
                    for k in range(KC):
                        last = nc.scalar.activation(xgT[:, s % 2, k, :], tp[:, s % 2, k * P:(k + 1) * P], ACT.Copy, scale=wn[:, k:k + 1])
                    last.then_inc(xgT_s, 1)

                def tanh(e, s):
                    act.wait_ge(gu_s, START + e + 1)
                    nc.scalar.activation(silu[:, s % 2, :], gu[:, s % 2, 0:EF], ACT.Tanh, scale=0.5).then_inc(silu_s, 1)

                def keep_h(e, s):
                    act.wait_ge(h_turned, START + e + 1)
                    nc.scalar.activation(hT[:, s % 2], ht[0:EH, s % 2, 0:2 * P].rearrange("p (h c) -> p h c", h=2), ACT.Copy).then_inc(hT_s, 1)

                def body(it, e, s):
                    if within(e, 1):
                        tanh(e + 1, (s + 1) % DEEP)
                    keep_h(e, s)
                    if within(e, 2):
                        keep(e + 2, (s + 2) % DEEP)

                keep(0, 0)
                tanh(0, 0)
                keep(1, 1)
                every(act, body)

            @block.vector
            def _(dve):
                dve.wait_ge(small_in, START + 32)
                for e in range(DEEP):
                    nc.vector.tensor_copy(gidx[:, e:e + 1], table[:, e, 0:1]).then_inc(gidx_s, 1)

                def hidden(e, s):
                    dve.wait_ge(silu_s, START + e + 1)
                    nc.vector.scalar_tensor_tensor(out=silu2[:, s % 2, :], in0=silu[:, s % 2, :], scalar=1.0,
                                                   in1=gu[:, s % 2, 0:EF], op0=ALU.add, op1=ALU.mult).then_inc(silu2_s, 1)
                    dve.wait_ge(silu2_s, START + e + 1)
                    nc.vector.tensor_tensor(h[:, s % 2, :], silu2[:, s % 2, :], gu[:, s % 2, EF:2 * EF], ALU.mult).then_inc(h_s, 1)

                def weigh(e, s):
                    dve.wait_ge(dn_s, START + e + 1)
                    if not (isinstance(e, int) and e < 2):
                        dve.wait_ge(added, 16 * (e - 1))
                    nc.vector.tensor_copy(sidx[:, s % 2:s % 2 + 1], at(table, e)[:, 0:1])
                    nc.vector.tensor_scalar(ys[:, s % 2, :], dn[:, s % 2, 0:D], at(table[:].bitcast(F32), e)[:, 1:2], 0.25,
                                            ALU.mult, ALU.mult).then_inc(y_s, 1)

                def body(it, e, s):
                    if within(e, 1):
                        hidden(e + 1, (s + 1) % DEEP)
                    if within(e, DEEP):
                        dve.wait_ge(gathered[s], 16 * (it + 1))
                        nc.vector.tensor_copy(gidx[:, s:s + 1], at(table, e + DEEP)[:, 0:1]).then_inc(gidx_s, 1)
                    weigh(e, s)

                hidden(0, 0)
                every(dve, body)


def reload_phase(core, tag, acc):
    nc = core.nc
    with ExitStack() as ctx:
        sb, _, sem = scope(core, ctx)
        bn = sb(tag + "bn", [P, NT, 6])
        back, stats = [sem(f"{tag}back{b}") for b in range(B)], sem(tag + "stats")
        nc.all_engine_barrier()
        with nc.Block() as block:
            @block.sync
            def _(sp):
                for b in range(B):
                    sp.dma_start(core.x[:, b * TPB:(b + 1) * TPB, :],
                                 acc[b * T:(b + 1) * T, :].rearrange("(i p) d -> p i d", p=P)).then_inc(back[b], 16)

            @block.vector
            def _(dve):
                for t in range(NT):
                    if t % TPB == 0:
                        dve.wait_ge(back[t // TPB], START + 16)
                    last = nc.vector.bn_stats(bn[:, t, :], core.x[:, t, :])
                last.then_inc(stats, 1)
                dve.wait_ge(stats, START + 1)
                for t in range(NT):
                    nc.vector.bn_aggr(core.mv[:, t, :], bn[:, t, :])


def spread(ap, axis, n):
    u = ap.unsqueeze(axis)
    shape = list(u.shape)
    shape[axis] = n
    return u.to_broadcast(shape)


def attention_phase(core, tag, second):
    nc, dram = core.nc, core.dram
    W = 6 * HD + (6 if second else 0)
    WM = W + 3
    GH = 4
    NG = NH // GH
    HALF = 512
    QH = T // HALF
    KPH = HALF // P
    units = [(h, kt, max(0, kt - KPH * h) * P if second else 0)
             for h in range(QH) for kt in range(KPH * (h + 1) if second else TPB)]
    U = len(units)
    chunks = [(j, qt, kh, min(HALF, (qt + 1) * P - kh * HALF) if second else HALF)
              for j in range(GH) for qt in range(TPB) for kh in range(2)
              if not second or (qt + 1) * P > kh * HALF]
    C = len(chunks)
    AHEAD = 3 * C // U
    TURN_AT = C + 3

    def beside(g, u):
        at = (g + 1) * C + AHEAD + C * u // U if g < NG - 1 else NG * C
        return min(at, NG * C)

    m_unit = next(u for u in range(U) if beside(0, u) >= 2 * C)
    assert all(beside(g, m_unit) == (g + 2) * C for g in range(NG - 1))
    firsts = sorted(chunks, key=lambda c: max(c[1], (c[2] * HALF + c[3] - 1) // P))
    BESIDE_OPS = (0, 1, 2, 1, 3, 1)
    EARLY = sum(BESIDE_OPS)
    EARLIER = (TPB // 2 - 1) * EARLY + sum(BESIDE_OPS[:4])
    for i in range(TPB // 2, TPB):
        for placed, tiles in (((i - TPB // 2) * EARLY + sum(BESIDE_OPS[:4]), i), ((i - TPB // 2 + 1) * EARLY, i + 1)):
            assert i == TPB - 1 and tiles > i or all(max(c[1], (c[2] * HALF + c[3] - 1) // P) < tiles for c in firsts[:placed])
    NV = 2
    SB = 3
    y_unit = 2 + next(u for u in range(U) if units[u][0])

    Y_LATE = 2
    assert Y_LATE < y_unit != m_unit + 1

    with ExitStack() as ctx:
        sb, ps, sem = scope(core, ctx)
        xn = sb(tag + "xn", [P, TPB, D])
        y = xn
        xT = sb(tag + "xT", [P, KC, T])
        qk = sb(tag + "qk", [P, 2, 2 * NH, HD])
        rot = sb(tag + "rot", [P, 2, 2 * NH, ROPE])
        rest = sb(tag + "rest", [P, 2, NH, HD])
        A = sb(tag + "A", [P, 2, 2, NH, W], BF16)
        QT = sb(tag + "QT", [WM, NH, T], BF16)
        KT = sb(tag + "KT", [WM, NH, T], BF16)
        V = sb(tag + "V", [P, TPB, NH, HD])
        Vg = sb(tag + "Vg", [P, TPB, GH, VW])
        E = sb(tag + "E", [P, 2, GH, HALF])
        Ysb = sb(tag + "Ysb", [P, 2, HALF])
        rden = sb(tag + "rden", [P, KPH, GH])
        mx = sb(tag + "mx", [P, GH, TPB, 2])
        m = sb(tag + "m", [P, GH, TPB])
        mrest = sb(tag + "mrest", [P, GH, TPB])
        mparts = sb(tag + "mparts", [P, GH, 3, TPB], BF16)
        mT = sb(tag + "mT", [GH * 3 * TPB, P], BF16)
        yT = sb(tag + "yT", [P, 2, KC, P])
        bn8 = sb(tag + "bn8", [P, TPB, 6])
        carrier = sb(tag + "carrier", [P, 1])
        mv8 = sb(tag + "mv8", [P, TPB, 2])
        masks = sb(tag + "masks", [P, 2, P], BF16)
        bank = ps(tag + "bank", [P, 8, 512])
        ident, ident_b = core.const("ident"), core.ident_b
        names = ("w_in pool_ones ones consts_b root scales normed turned xT_kept qkv qk_kept v_kept roped part1 rested "
                 "part2 parts ops_turned ops_dve ops_act chunk_done reduced v_group m_step m_turned mT_kept m_rows "
                 "scored exps pv y_kept y_turned y_step y_normed out_turned yT_kept out_done x_done stats aggregated")
        S = {n: sem(tag + n) for n in names.split()}
        (w_in, pool_ones, ones, consts_b, root, scales, normed, turned, xT_kept, qkv, qk_kept, v_kept, roped, part1, rested,
         part2, parts, ops_turned, ops_dve, ops_act, chunk_done, reduced, v_group, m_step, m_turned, mT_kept, m_rows,
         scored, exps, pv, y_kept, y_turned, y_step, y_normed, out_turned, yT_kept, out_done, x_done,
         stats, aggregated) = (S[n] for n in names.split())

        def tile_bank(i):
            return bank[:, (i // 2) % 2, :].rearrange("p (k h c) -> p k h c", k=KC, h=2)

        def ops_bank(n):
            return bank[:, 5 + n % 2, :].bitcast(BF16).rearrange("p (h c) -> p h c", h=8)

        def slot(q):
            return bank[:, (0, 1, 7)[q % SB] if q < C else 5 + q % SB, :]

        def early(i, n):
            at = (i - TPB // 2) * EARLY + sum(BESIDE_OPS[:n])
            return (at, at + BESIDE_OPS[n]) if i >= TPB // 2 else (0, 0)

        def before(b, per_batch, n):
            return b * per_batch + max(n, 0)

        nc.all_engine_barrier()
        with nc.Block() as block:
            @block.sync
            def _(sp):
                if second:
                    sp.dma_start(core.wqkvT[:], dram["L1_attn_W_qkv"].rearrange("(k p) e -> p k e", p=P)).then_inc(w_in, 16)
                    sp.dma_start(core.woT[:], dram["L1_attn_W_o"].rearrange("(k p) e -> p k e", p=P)).then_inc(w_in, 16)

                def rows(b, g):
                    sp.wait_ge(mT_kept, START + b * NG + g + 1)
                    for j in range(GH):
                        h = g * GH + j
                        dst = QT[W:WM, h, :].rearrange("r (q c) -> r q c", c=P)
                        sp.dma_start(dst, mT[j * 3 * TPB:(j + 1) * 3 * TPB, :]).then_inc(m_rows, 16)

                with sp.Fori(0, B) as b:
                    for g in range(NG):
                        rows(b, g)

            @block.gpsimd
            def _(pool):
                def rope(b, i):
                    tab = core.const("rope").rearrange("p (i s r) -> p i s r", i=TPB, s=2)
                    z = qk[:, i % 2]
                    pool.wait_ge(qk_kept, START + b * TPB + i + 1)
                    pool.wait_ge(roped, START + b * 2 * TPB + 2 * i)
                    H2 = ROPE // 2
                    nc.gpsimd.tensor_tensor(rot[:, 1, :, 0:H2], z[:, :, H2:ROPE], spread(tab[:, i, 1, 0:H2], 1, 2 * NH), ALU.mult)
                    nc.gpsimd.tensor_tensor(rot[:, 1, :, H2:ROPE], z[:, :, 0:H2], spread(tab[:, i, 1, H2:ROPE], 1, 2 * NH), ALU.mult)
                    nc.gpsimd.tensor_tensor(rot[:, 0, :, :], z[:, :, 0:ROPE], spread(tab[:, i, 0, :], 1, 2 * NH),
                                            ALU.mult).then_inc(roped, 1)
                    pool.wait_ge(roped, START + b * 2 * TPB + 2 * i + 1)
                    nc.gpsimd.tensor_tensor(z[:, :, 0:ROPE], rot[:, 0], rot[:, 1], ALU.add).then_inc(roped, 1)

                def rests(b, i):
                    pool.wait_ge(part1, START + b * TPB + i + 1)
                    pool.wait_ge(parts, START + b * TPB + i)
                    for q, slot in ((0, 0), (1, 1)):
                        a = A[:, i % 2, q, :, 0:6 * HD].rearrange("p h (s d) -> p h s d", d=HD)
                        nc.gpsimd.tensor_tensor(rest[:, q], qk[:, i % 2, q * NH:(q + 1) * NH, :], a[:, :, slot, :],
                                                ALU.subtract).then_inc(rested, 1)

                def third_parts(b, i):
                    pool.wait_ge(part2, START + b * TPB + i + 1)
                    for q, low, slot in ((0, 3, 5), (1, 0, 2)):
                        a = A[:, i % 2, q, :, 0:6 * HD].rearrange("p h (s d) -> p h s d", d=HD)
                        last = nc.gpsimd.tensor_tensor(a[:, :, slot, :], rest[:, q], a[:, :, low, :], ALU.subtract)
                    last.then_inc(parts, 1)

                nc.gpsimd.memset(KT[96:WM, GH:NH, :], 1.0).then_inc(pool_ones, 1)
                pool.wait_ge(pool_ones, START + 1)
                nc.gpsimd.memset(Vg[:], 0.0).then_inc(pool_ones, 1)
                pool.wait_ge(pool_ones, START + 2)
                nc.gpsimd.memset(Vg[:, :, :, HD:HD + 1], 1.0).then_inc(pool_ones, 1)
                with pool.Fori(0, B) as b:
                    if not second:
                        rope(b, 0)
                    for i in range(TPB):
                        if not second and i + 1 < TPB:
                            rope(b, i + 1)
                        rests(b, i)
                        third_parts(b, i)
                    for g in range(NG):
                        pool.wait_ge(pool_ones, START + 3)
                        pool.wait_ge(v_kept, START + (b + 1) * TPB)
                        pool.wait_ge(pv, START + (b * NG + g) * U)
                        own = V[:, :, g * GH:(g + 1) * GH, :]
                        one = Vg[:, :, :, HD:HD + 1].to_broadcast([P, TPB, GH, HD])
                        nc.gpsimd.tensor_tensor(Vg[:, :, :, 0:HD], own, one, ALU.mult).then_inc(v_group, 1)

            @block.tensor
            def _(pe):
                def max_chunks(b, lo, hi, used=None):
                    for n in range(lo, hi):
                        head, (j, qt, kh, w) = n // C * GH, (chunks if n >= C else firsts)[n % C]
                        pe.wait_ge(reduced, START + b * NG * C + max(n - SB + 1, 0))
                        if n == lo and used is not None:
                            pe.wait_ge(used[0], START + used[1])
                        out = slot(n)[:, 0:w]
                        q = QT[0:W, head + j, qt * P:(qt + 1) * P]
                        k = KT[0:W, head + j, kh * HALF:kh * HALF + w]
                        diag = second and qt * P < kh * HALF + w <= (qt + 1) * P
                        last = nc.tensor.matmul(out, q, k, start=True, stop=not diag)
                        if diag:
                            last = nc.tensor.matmul(out[:, w - P:w], ident_b[:], masks[:, 0, :], start=False, stop=True)
                        last.then_inc(chunk_done, 1)

                def turn_max(b, G, n):
                    pe.wait_ge(m_step, START + (G + 1) * 4)
                    pe.wait_ge(reduced, START + b * NG * C + n - SB + 1)
                    out = slot(n)[0:GH * 3 * TPB].bitcast(BF16)[:, 0:P]
                    nc.tensor.transpose(out, mparts[:].rearrange("p j r q -> p (j r q)"), ident_b[:]).then_inc(m_turned, 1)

                def score_pair(G, g, u, pair):
                    (half, kt, c0), head = units[u], g * GH
                    pe.wait_ge(exps, START + G * 2 * U + (2 * u - 1 + pair if u or g else 0))
                    for j in (2 * pair, 2 * pair + 1):
                        out = bank[:, j, c0:HALF]
                        k = KT[:, head + j, kt * P:(kt + 1) * P]
                        q = QT[:, head + j, half * HALF + c0:(half + 1) * HALF]
                        diag = second and kt >= KPH * half
                        last = nc.tensor.matmul(out, k, q, start=True, stop=not diag)
                        if diag:
                            last = nc.tensor.matmul(out[:, 0:P], ident_b[:], masks[:, 1, :], start=False, stop=True)
                    last.then_inc(scored, 1)

                def pv_unit(G, u):
                    half, kt, c0 = units[u]
                    first, final = u == 0 or units[u - 1][0] != half, u == U - 1 or units[u + 1][0] != half
                    pe.wait_ge(exps, START + G * 2 * U + 2 * u + 2)
                    if first:
                        pe.wait_ge(y_kept, START + G * NV + half)
                    if u == 0:
                        pe.wait_ge(v_group, START + G + 1)
                    for j in range(GH):
                        last = nc.tensor.matmul(bank[VW * j:VW * (j + 1), 4, c0:HALF], Vg[:, kt, j, :], E[:, u % 2, j, c0:HALF],
                                                start=first, stop=final, tile_position=(0, VW * j))
                    last.then_inc(pv, 1)

                def turn_y(b, G, half, n):
                    pe.wait_ge(reduced, START + b * NG * C + n - SB + 1)
                    pe.wait_ge(y_kept, START + G * NV + half + 1)
                    pe.wait_ge(y_normed, START + G * NV + half)
                    for i in range(KPH):
                        last = nc.tensor.transpose(slot(n)[:, i * P:(i + 1) * P], Ysb[:, half, i * P:(i + 1) * P], ident)
                    last.then_inc(y_turned, 1)

                def group(b, g, more):
                    G = b * NG + g
                    pe.wait_ge(m_rows, START + (G + 1) * GH * 16)
                    for u in range(U):
                        lo, hi = beside(g, u), beside(g, u + 1)
                        used = None
                        if u == Y_LATE and g:
                            turn_y(b, G - 1, 1, lo)
                            used = (y_normed, G * NV)
                        if u == y_unit:
                            turn_y(b, G, 0, lo)
                            used = (y_normed, G * NV + 1)
                        if u == m_unit + 1 and more:
                            turn_max(b, G + 1, lo)
                            used = (mT_kept, G + 2)
                        a, z = min(lo + 1, hi), min(lo + 2, hi)
                        score_pair(G, g, u, 0)
                        max_chunks(b, lo, a, used)
                        score_pair(G, g, u, 1)
                        max_chunks(b, a, z)
                        if u:
                            pv_unit(G, u - 1)
                        elif g:
                            pv_unit(G - 1, U - 1)
                        max_chunks(b, z, hi)
                    if not more:
                        pv_unit(G, U - 1)
                        turn_y(b, G, 1, beside(g, U))

                def turn_tile(b, i):
                    pe.wait_ge(normed, START + b * TPB + i + 1)
                    if i >= 4:
                        pe.wait_ge(xT_kept, START + b * (TPB // 2) + i // 2 - 1)
                    for k in range(KC):
                        last = nc.tensor.transpose(tile_bank(i)[:, k, i % 2, :], xn[:, i, k * P:(k + 1) * P], ident)
                    last.then_inc(turned, 1)

                def project(b, i):
                    if i < TPB:
                        pe.wait_ge(xT_kept, START + b * (TPB // 2) + i // 2 + 1)
                        pe.wait_ge(qk_kept, START + before(b, TPB, i - 1))
                        for k in range(KC):
                            nc.tensor.matmul(bank[:, 2 + i % 2, :], xT[:, k, i * P:(i + 1) * P], core.wqkvT[:, k, 0:2 * D],
                                             start=(k == 0), stop=(k == KC - 1))
                    max_chunks(b, *early(i - 3, 4))
                    if i < TPB:
                        pe.wait_ge(v_kept, START + before(b, TPB, i))
                        for k in range(KC):
                            last = nc.tensor.matmul(bank[:, 4, 0:D], xT[:, k, i * P:(i + 1) * P], core.wqkvT[:, k, 2 * D:3 * D],
                                                    start=(k == 0), stop=(k == KC - 1))
                        last.then_inc(qkv, 1)
                    max_chunks(b, *early(i - 3, 5))

                def turn_ops(b, i):
                    pe.wait_ge(parts, START + b * TPB + i + 1)
                    for n in range(4):
                        pe.wait_ge(ops_dve, START + b * 3 * TPB + 3 * i + max(n - 1, 0))
                        if n == 1:
                            pe.wait_ge(ops_act, START + b * TPB + i)
                        for h in range(8):
                            last = nc.tensor.transpose(ops_bank(n)[0:W, h, :], A[:, i % 2, n // 2, (n % 2) * 8 + h, :], ident_b[:])
                        last.then_inc(ops_turned, 1)
                        max_chunks(b, *early(i, n))

                def turn_out(b, i):
                    pe.wait_ge(yT_kept, START + before(b, TPB, i - 1))
                    for k in range(KC):
                        last = nc.tensor.transpose(bank[:, i % 2, k * P:(k + 1) * P], y[:, i, k * P:(k + 1) * P], ident)
                    last.then_inc(out_turned, 1)

                def out_proj(b, i):
                    pe.wait_ge(yT_kept, START + b * TPB + i + 1)
                    pe.wait_ge(x_done, START + before(b, TPB, i - 1))
                    for k in range(KC):
                        last = nc.tensor.matmul(bank[:, 2 + i % 2, 0:D], yT[:, i % 2, k, :], core.woT[:, k, :],
                                                start=(k == 0), stop=(k == KC - 1))
                    last.then_inc(out_done, 1)

                if second:
                    pe.wait_ge(consts_b, START + 2)
                    pe.wait_ge(w_in, START + 32)
                with pe.Fori(0, B) as b:
                    for i in range(4):
                        turn_tile(b, i)
                    project(b, 0)
                    project(b, 1)
                    for i in range(4, TPB):
                        turn_tile(b, i)
                    for i in range(TPB):
                        project(b, i + 2)
                        turn_ops(b, i)
                    pe.wait_ge(ops_dve, START + (b + 1) * 3 * TPB)
                    pe.wait_ge(ops_act, START + (b + 1) * TPB)
                    pe.wait_ge(pool_ones, START + 1)
                    max_chunks(b, EARLIER, TURN_AT)
                    turn_max(b, b * NG, TURN_AT)
                    max_chunks(b, TURN_AT, C + AHEAD, (mT_kept, b * NG + 1))
                    for g in range(NG):
                        group(b, g, g + 1 < NG)
                    pe.wait_ge(y_normed, START + (b + 1) * NG * NV)
                    turn_out(b, 0)
                    for i in range(TPB):
                        if i + 1 < TPB:
                            turn_out(b, i + 1)
                        out_proj(b, i)

            @block.scalar
            def _(act):
                nc.scalar.activation(core.rstd[:], core.mv[:, :, 1], ACT.Sqrt, bias=core.eps[:, 0:1]).then_inc(root, 1)

                def take(b, i):
                    act.wait_ge(qkv, START + b * TPB + i + 1)
                    act.wait_ge(rested, START + before(b, 2 * TPB, 2 * (i - 1)))
                    nc.scalar.activation(V[:, i, :, :], bank[:, 4, 0:D].rearrange("p (h d) -> p h d", d=HD),
                                         ACT.Copy).then_inc(v_kept, 1)
                    pq = bank[:, 2 + i % 2, :].rearrange("p (h d) -> p h d", d=HD)
                    nc.scalar.activation(qk[:, i % 2, 0:NH, :], pq[:, 0:NH], ACT.Copy, scale=HD ** -0.5)
                    nc.scalar.activation(qk[:, i % 2, NH:2 * NH, :], pq[:, NH:2 * NH], ACT.Copy).then_inc(qk_kept, 1)

                def first_parts(b, i):
                    act.wait_ge(qk_kept if second else roped, START + b * TPB * (1 if second else 2) + (i + 1) * (1 if second else 2))
                    act.wait_ge(ops_turned, START + before(b, 4 * TPB, 4 * (i - 1)))
                    for q, slots in ((0, slice(0, 3)), (1, slice(1, 6, 2))):
                        dst = A[:, i % 2, q, :, 0:6 * HD].rearrange("p h (s d) -> p h s d", d=HD)[:, :, slots, :]
                        last = nc.scalar.activation(dst, spread(qk[:, i % 2, q * NH:(q + 1) * NH, :], 2, 3), ACT.Copy)
                    last.then_inc(part1, 1)

                def keep_ops(b, i):
                    if i == 0:
                        act.wait_ge(pool_ones, START + 1)
                    act.wait_ge(ops_turned, START + b * 4 * TPB + 4 * i + 4)
                    nc.scalar.activation(KT[0:W, 8:16, i * P:(i + 1) * P], ops_bank(3)[0:W], ACT.Copy).then_inc(ops_act, 1)

                def exp_unit(G, g, u):
                    half, kt, c0 = units[u]
                    act.wait_ge(pv, START + G * U + (u - 1 if u or g else 0))
                    for pair in range(2):
                        act.wait_ge(scored, START + G * 2 * U + 2 * u + pair + 1)
                        nc.scalar.activation(E[:, u % 2, 2 * pair:2 * pair + 2, c0:HALF], bank[:, 2 * pair:2 * pair + 2, c0:HALF],
                                             ACT.Exp).then_inc(exps, 1)

                def keep_y(G, half):
                    done = sum(1 for h, _, _ in units if h <= half)
                    act.wait_ge(pv, START + G * U + done)
                    act.wait_ge(y_turned, START + G * NV + half)
                    nc.scalar.activation(Ysb[:, half, :], bank[:, 4, :], ACT.Copy).then_inc(y_kept, 1)

                def group(b, g):
                    for u in range(U):
                        exp_unit(b * NG + g, g, u)
                        if u == 0 and g:
                            keep_y(b * NG + g - 1, 1)
                        if u and units[u][0] != units[u - 1][0]:
                            keep_y(b * NG + g, 0)
                    if g == NG - 1:
                        keep_y(b * NG + g, 1)

                with act.Fori(0, B) as b:
                    def keep_tiles(k):
                        act.wait_ge(turned, START + b * TPB + 2 * k + 2)
                        dst = xT[:, :, 2 * k * P:2 * (k + 1) * P].rearrange("p k (h c) -> p k h c", h=2)
                        nc.scalar.activation(dst, tile_bank(2 * k), ACT.Copy).then_inc(xT_kept, 1)

                    keep_tiles(0)
                    keep_tiles(1)
                    take(b, 0)
                    keep_tiles(2)
                    keep_tiles(3)
                    for i in range(TPB + 1):
                        if i + 1 < TPB:
                            take(b, i + 1)
                        if i < TPB:
                            first_parts(b, i)
                        if i:
                            keep_ops(b, i - 1)
                    for g in range(NG):
                        group(b, g)
                    for i in range(TPB):
                        act.wait_ge(out_turned, START + b * TPB + i + 1)
                        act.wait_ge(out_done, START + before(b, TPB, i - 1))
                        nc.scalar.activation(yT[:, i % 2], bank[:, i % 2, 0:D].rearrange("p (k c) -> p k c", k=KC),
                                             ACT.Copy).then_inc(yT_kept, 1)

            @block.vector
            def _(dve):
                nc.vector.memset(KT[96:WM, 0:GH, :], 1.0).then_inc(ones, 1)
                dve.wait_ge(root, START + 1)
                nc.vector.reciprocal(core.rstd[:], core.rstd[:]).then_inc(scales, 1)
                if second:
                    nc.vector.memset(mx[:], NEG)
                    nc.vector.tensor_copy(masks[:, 0, :], core.const("mask_qk"))
                    nc.vector.tensor_copy(masks[:, 1, :], core.const("mask_kq")).then_inc(consts_b, 1)
                    for s in range(2):
                        nc.vector.tensor_copy(A[:, s, 0, :, 6 * HD:W], core.const("slopes").rearrange("p (h s) -> p h s", h=NH))
                        last = nc.vector.tensor_copy(A[:, s, 1, :, 6 * HD + 3:W], spread(core.const("kpos"), 1, NH))
                    last.then_inc(consts_b, 1)
                dve.wait_ge(scales, START + 1)

                def second_parts(b, i):
                    if second:
                        nc.vector.tensor_copy(A[:, i % 2, 1, :, 6 * HD:6 * HD + 3],
                                              spread(core.const("kbase")[:, 3 * i:3 * i + 3], 1, NH))
                    for q, slots in ((0, slice(3, 5)), (1, slice(0, 5, 4))):
                        dve.wait_ge(rested, START + b * 2 * TPB + 2 * i + q + 1)
                        dst = A[:, i % 2, q, :, 0:6 * HD].rearrange("p h (s d) -> p h s d", d=HD)[:, :, slots, :]
                        last = nc.vector.tensor_copy(dst, spread(rest[:, q], 2, 2))
                    last.then_inc(part2, 1)

                def keep_ops(b, i):
                    for n in range(3):
                        if i == 0 and n == 2:
                            dve.wait_ge(pool_ones, START + 1)
                        dve.wait_ge(ops_turned, START + b * 4 * TPB + 4 * i + n + 1)
                        dst = (QT if n // 2 == 0 else KT)[0:W, (n % 2) * 8:(n % 2) * 8 + 8, i * P:(i + 1) * P]
                        nc.vector.tensor_copy(dst, ops_bank(n)[0:W]).then_inc(ops_dve, 1)
                        if n:
                            reduce_chunks(b, *early(i, n))
                    reduce_chunks(b, *early(i, 3))

                def reduce_chunks(b, lo, hi):
                    for n in range(lo, hi):
                        j, qt, kh, w = (chunks if n >= C else firsts)[n % C]
                        dve.wait_ge(chunk_done, START + b * NG * C + n + 1)
                        nc.vector.tensor_reduce(mx[:, j, qt, kh:kh + 1], slot(n)[:, 0:w], AX.X, ALU.max).then_inc(reduced, 1)

                def maxima(G):
                    dve.wait_ge(reduced, START + (G + 1) * C)
                    nc.vector.tensor_reduce(m[:], mx[:], AX.X, ALU.max).then_inc(m_step, 1)
                    dve.wait_ge(m_step, START + G * 4 + 1)
                    nc.vector.tensor_scalar(mparts[:, :, 0, :], m[:], -1.0, None, ALU.mult).then_inc(m_step, 1)
                    dve.wait_ge(m_step, START + G * 4 + 2)
                    nc.vector.scalar_tensor_tensor(out=mrest[:], in0=m[:], scalar=-1.0, in1=mparts[:, :, 0, :],
                                                   op0=ALU.mult, op1=ALU.subtract).then_inc(m_step, 1)
                    dve.wait_ge(m_step, START + G * 4 + 3)
                    nc.vector.tensor_copy(mparts[:, :, 1, :], mrest[:]).then_inc(ones, 1)
                    dve.wait_ge(ones, START + 1 + G + 1)
                    nc.vector.tensor_tensor(mparts[:, :, 2, :], mrest[:], mparts[:, :, 1, :], ALU.subtract).then_inc(m_step, 1)

                def keep_max(G, n):
                    dve.wait_ge(m_turned, START + G + 1)
                    dve.wait_ge(m_rows, START + G * GH * 16)
                    nc.vector.tensor_copy(mT[:], slot(n)[0:GH * 3 * TPB].bitcast(BF16)[:, 0:P]).then_inc(mT_kept, 1)

                def norm_y(G, g, half, n):
                    z = slot(n).rearrange("p (i j v) -> p i j v", i=KPH, j=GH)
                    dve.wait_ge(y_turned, START + G * NV + half + 1)
                    dve.wait_ge(y_normed, START + G * NV + half)
                    nc.vector.reciprocal(rden[:], z[:, :, :, HD]).then_inc(y_step, 1)
                    dve.wait_ge(y_step, START + G * NV + half + 1)
                    dst = y[:, half * KPH:(half + 1) * KPH, bass.ds(g * GH * HD, GH * HD)].rearrange("p i (j d) -> p i j d", d=HD)
                    nc.vector.tensor_tensor(dst, z[:, :, :, 0:HD], spread(rden[:], 3, HD), ALU.mult).then_inc(y_normed, 1)

                def group(b, g, more):
                    G = b * NG + g
                    for u in range(U):
                        if u == Y_LATE and g:
                            norm_y(G - 1, g - 1, 1, beside(g, u))
                        if u == y_unit:
                            norm_y(G, g, 0, beside(g, u))
                        if u == m_unit and more:
                            maxima(G + 1)
                        if u == m_unit + 1 and more:
                            keep_max(G + 1, beside(g, u))
                        reduce_chunks(b, beside(g, u), beside(g, u + 1))
                    if not more:
                        norm_y(G, g, 1, beside(g, U))

                with dve.Fori(0, B) as b:
                    for i in range(TPB):
                        t = b * TPB + i
                        dve.wait_ge(out_turned, START + b * TPB)
                        nc.vector.tensor_scalar(xn[:, i, :], at(core.x, t), at(core.mv, t)[:, 0:1], col(core.rstd, t),
                                                ALU.subtract, ALU.mult).then_inc(normed, 1)
                    for i in range(TPB + 1):
                        if i:
                            keep_ops(b, i - 1)
                        if i < TPB:
                            second_parts(b, i)
                            for n in (4, 5):
                                reduce_chunks(b, *early(i - 1, n))
                    reduce_chunks(b, EARLIER, C)
                    maxima(b * NG)
                    reduce_chunks(b, C, TURN_AT)
                    keep_max(b * NG, TURN_AT)
                    reduce_chunks(b, TURN_AT, C + AHEAD)
                    for g in range(NG):
                        group(b, g, g + 1 < NG)
                    for i in range(TPB):
                        t = b * TPB + i
                        dve.wait_ge(out_done, START + t + 1)
                        nc.vector.tensor_tensor(at(core.x, t), bank[:, 2 + i % 2, 0:D], at(core.x, t), ALU.add).then_inc(x_done, 1)
                        dve.wait_ge(scales, START + 1)
                        dve.wait_ge(x_done, START + t + 1)
                        nc.vector.bn_stats(bn8[:, i, :], at(core.x, t)).then_inc(stats, 1)
                    dve.wait_ge(stats, START + (b + 1) * TPB)
                    nc.vector.memset(carrier[:], 0.0)
                    for i in range(TPB):
                        last = nc.vector.bn_aggr(mv8[:, i, :], bn8[:, i, :])
                    last.then_inc(aggregated, 1)
                    dve.wait_ge(aggregated, START + b + 1)
                    nc.vector.tensor_copy(core.mv[:, bass.ds(b * TPB, TPB), :], mv8[:])


def at(tensor, t):
    return tensor[:, t] if isinstance(t, int) else tensor[:, bass.ds(t, 1)].rearrange("p a d -> p (a d)")


def col(tensor, t):
    return tensor[:, t:t + 1] if isinstance(t, int) else tensor[:, bass.ds(t, 1)]


OUT_SHAPE = (NTOK + TRASH, D)


def store_phase(core):
    nc = core.nc
    with ExitStack() as ctx:
        _, _, sem = scope(core, ctx)
        stored = sem("stored")
        nc.all_engine_barrier()
        with nc.Block() as block:
            @block.sync
            def _(sp):
                sp.dma_start(core.dram["out"][0:NTOK, :].rearrange("(t p) d -> p t d", p=P), core.x[:]).then_inc(stored, 16)
                sp.wait_ge(stored, START + 16)


PHASES = ("prep", "ffn0", "attn0", "ffn0", "moe1", "attn1", "moe2")


def program(nc, dram, phases=PHASES):
    nc.disable_value_cache = True
    with ExitStack() as ctx:
        ctx.enter_context(nc.allow_non_contiguous_dma(reason="per-channel scales, once"))
        core = Core(nc, ctx, dram)
        dram["xn"] = nc.dram_tensor("normalised", (NTOK + TRASH, D), F32, kind="Internal").ap()
        dram["table"] = nc.dram_tensor("table", (NE * CAP, 2), I32, kind="Internal").ap()
        dram["acc"] = nc.dram_tensor("acc", (NTOK + TRASH, D), F32, kind="Internal").ap()
        for n, name in enumerate(phases):
            if name == "prep":
                prepare_phase(core)
            elif name == "ffn0":
                ffn0_phase(core, f"f{n}_")
            elif name in ("attn0", "attn1"):
                attention_phase(core, f"a{n}_", name == "attn1")
            elif name == "moe1":
                mixture_dense_phase(core, f"d{n}_", dram["acc"], True)
                experts_phase(core, f"e{n}_", dram["acc"])
                reload_phase(core, f"r{n}_", dram["acc"])
                core.clear_semaphores()
            elif name == "moe2":
                mixture_dense_phase(core, f"d{n}_", dram["out"], False)
                experts_phase(core, f"e{n}_", dram["out"])
            elif name == "store":
                store_phase(core)


_INS = ['L0_attn_x', 'L0_attn_wq', 'L0_attn_wk', 'L0_attn_wv', 'L0_attn_wo', 'L0_ffn_wq_gate', 'L0_ffn_s_gate',
        'L0_ffn_wq_up', 'L0_ffn_s_up', 'L0_ffn_wq_down', 'L0_ffn_s_down', 'L1_attn_W_qkv', 'L1_attn_W_o',
        'L1_ffn_w_norm', 'L1_ffn_w_router', 'L1_ffn_w_gate', 'L1_ffn_w_up', 'L1_ffn_w_down', 'L1_ffn_sw_gate',
        'L1_ffn_sw_up', 'L1_ffn_sw_down', 'L1_ffn_w_shared_gate']


def kernel(**inputs):
    import concourse.bacc as _bacc
    from concourse.bass_utils import run_bass_kernel_spmd as _run

    nc = _bacc.Bacc("TRN2", target_bir_lowering=False, num_devices=1)
    arrays, dram = {}, {}
    for name in _INS:
        arrays[f"in_{name}"] = np.ascontiguousarray(inputs[name])
    arrays["in_consts"] = constants()
    for name, a in arrays.items():
        dram[name[3:]] = nc.dram_tensor(name, a.shape, mybir.dt.from_np(a.dtype), kind="ExternalInput").ap()
    dram["out"] = nc.dram_tensor("out_0", OUT_SHAPE, F32, kind="ExternalOutput").ap()
    program(nc, dram)
    r = _run(nc, [arrays], core_ids=[0])
    return r.results[0]["out_0"][:NTOK].reshape(B, T, D)
```
